# Optimizing a Trainium2 kernel written in Bass

```python
import numpy as np
import jax
import jax.numpy as jnp

def _softmax(x, axis=-1):
    return jax.nn.softmax(x, axis=axis)

def _gelu(x):
    return jax.nn.gelu(x, approximate=True)

def _silu(x):
    return jax.nn.silu(x)

def _sigmoid(x):
    return jax.nn.sigmoid(x)

def _layernorm(x, axis=-1, eps=1e-05):
    m = jnp.mean(x, axis=axis, keepdims=True)
    v = jnp.var(x, axis=axis, keepdims=True)
    return (x - m) / jnp.sqrt(v + eps)

def _scatter_add(tgt, idx, src, axis=0):
    return tgt.at[idx].add(src)

def _segment_sum(src, seg, n):
    return jax.ops.segment_sum(src, seg, n)
kernel_name = 'mk_hybrid_d2_jaxref_r8_260641'

def setup_inputs(seed: int=0):
    np.random.seed(seed)
    _w = jnp.asarray

    def _L0_attn_a_setup():
        import jax, jax.numpy as jnp
        import numpy as np
        B, T, D, H, K, V, F = (4, 512, 128, 8, 128, 128, 512)
        EPS = 1e-05

        def layernorm(x, w, b):
            m = jnp.mean(x, -1, keepdims=True)
            v = jnp.var(x, -1, keepdims=True)
            return (x - m) * jax.lax.rsqrt(v + EPS) * w + b

        def l2norm(x):
            return x * jax.lax.rsqrt(jnp.sum(x * x, -1, keepdims=True) + 1e-06)

        def gdn_recurrence(q, k, v, alpha, beta):
            qT = jnp.moveaxis(q, 1, 0)
            kT = jnp.moveaxis(k, 1, 0)
            vT = jnp.moveaxis(v, 1, 0)
            aT = jnp.moveaxis(alpha, 1, 0)
            bT = jnp.moveaxis(beta, 1, 0)

            def step(S, inp):
                q_t, k_t, v_t, a_t, b_t = inp
                kS = jnp.einsum('bhk,bhkv->bhv', k_t, S)
                bk = (b_t[..., None] * k_t)[..., :, None]
                S = a_t[..., None, None] * (S - bk * kS[..., None, :]) + bk * v_t[..., None, :]
                o = jnp.einsum('bhk,bhkv->bhv', q_t, S)
                return (S, o)
            S0 = jnp.zeros((q.shape[0], H, K, V), q.dtype)
            _, oT = jax.lax.scan(step, S0, (qT, kT, vT, aT, bT))
            return jnp.moveaxis(oT, 0, 1)
        key = jax.random.key(seed)
        ks = jax.random.split(key, 12)
        s = 0.02
        return {'x': jax.random.normal(ks[0], (B, T, D), jnp.float32), 'Wq': jax.random.normal(ks[1], (D, H * K), jnp.float32) * s, 'Wk': jax.random.normal(ks[2], (D, H * K), jnp.float32) * s, 'Wv': jax.random.normal(ks[3], (D, H * V), jnp.float32) * s, 'Wb': jax.random.normal(ks[4], (D, H), jnp.float32) * s, 'Wa': jax.random.normal(ks[5], (D, H), jnp.float32) * s, 'Wo': jax.random.normal(ks[6], (H * V, D), jnp.float32) * s, 'ln1_w': jnp.ones((D,), jnp.float32), 'ln1_b': jnp.zeros((D,), jnp.float32), 'ln2_w': jnp.ones((D,), jnp.float32), 'ln2_b': jnp.zeros((D,), jnp.float32), 'W1': jax.random.normal(ks[7], (D, F), jnp.float32) * s, 'b1': jnp.zeros((F,), jnp.float32), 'W2': jax.random.normal(ks[8], (F, D), jnp.float32) * s, 'b2': jnp.zeros((D,), jnp.float32)}
    _L0_attn_a_in = _L0_attn_a_setup()

    def _L0_attn_b_setup():
        import jax, jax.numpy as jnp
        import numpy as np
        B_SZ, T, D_MODEL, N_STATE = (4, 512, 128, 32)
        D_FF = (int(8 / 3 * D_MODEL) + 7) // 8 * 8
        EPS = 1e-06

        def _rmsnorm(x, w):
            rms = jnp.sqrt(jnp.mean(x * x, axis=-1, keepdims=True) + EPS)
            return x / rms * w
        key = jax.random.key(seed)
        ks = jax.random.split(key, 8)
        return {'x': jax.random.normal(ks[0], (B_SZ, T, D_MODEL), dtype=jnp.float32), 'log_lambda': jax.random.normal(ks[1], (N_STATE,), dtype=jnp.float32) * 0.5 + 3.0, 'B_w': jax.random.normal(ks[2], (N_STATE, D_MODEL), dtype=jnp.float32) / np.sqrt(D_MODEL), 'C_w': jax.random.normal(ks[3], (D_MODEL, N_STATE), dtype=jnp.float32) / np.sqrt(N_STATE), 'D_skip': jnp.zeros((D_MODEL,), dtype=jnp.float32), 'ssm_norm_w': jnp.ones((D_MODEL,), dtype=jnp.float32), 'ffn_norm_w': jnp.ones((D_MODEL,), dtype=jnp.float32), 'w1': jax.random.normal(ks[4], (D_FF, D_MODEL), dtype=jnp.float32) / np.sqrt(D_MODEL), 'w2': jax.random.normal(ks[5], (D_MODEL, D_FF), dtype=jnp.float32) / np.sqrt(D_FF), 'w3': jax.random.normal(ks[6], (D_FF, D_MODEL), dtype=jnp.float32) / np.sqrt(D_MODEL)}
    _L0_attn_b_in = _L0_attn_b_setup()

    def _L0_ffn_setup():
        import jax, jax.numpy as jnp
        import numpy as np
        E = 32
        K = 4
        H = 128
        I = 96
        ROUTED_SCALING_FACTOR = 1.0
        key = jax.random.key(seed)
        k0, k1, k2, k3, k4, k5 = jax.random.split(key, 6)
        return {'hidden_states': jax.random.normal(k0, (1, 256, H), jnp.float32), 'gate_w': jax.random.normal(k1, (E, H), jnp.float32) * 0.02, 'w1': jax.random.normal(k2, (E, H, I), jnp.float32) * 0.02, 'w3': jax.random.normal(k3, (E, H, I), jnp.float32) * 0.02, 'w2': jax.random.normal(k4, (E, I, H), jnp.float32) * 0.02, 'e_bias': jax.random.normal(k5, (E,), jnp.float32) * 0.02}
    _L0_ffn_in = _L0_ffn_setup()

    def _L1_attn_a_setup():
        import jax, jax.numpy as jnp
        import numpy as np
        B, S, D, H, L, F = (4, 256, 128, 16, 8, 512)
        DH = D // H

        def _ln(x, g, b):
            m = jnp.mean(x, axis=-1, keepdims=True)
            v = jnp.mean((x - m) ** 2, axis=-1, keepdims=True)
            return (x - m) * jax.lax.rsqrt(v + 1e-05) * g + b

        def _phi(t):
            return jax.nn.elu(t) + 1.0
        key = jax.random.key(seed)
        ks = jax.random.split(key, 12)
        s = 0.02
        n = jax.random.normal
        return {'x': n(ks[0], (B, S, D), jnp.float32), 'Wq': n(ks[1], (L, D, D), jnp.float32) * s, 'bq': jnp.zeros((L, D), jnp.float32), 'Wk': n(ks[2], (L, D, D), jnp.float32) * s, 'bk': jnp.zeros((L, D), jnp.float32), 'Wv': n(ks[3], (L, D, D), jnp.float32) * s, 'bv': jnp.zeros((L, D), jnp.float32), 'Wo': n(ks[4], (L, D, D), jnp.float32) * s, 'bo': jnp.zeros((L, D), jnp.float32), 'g1': jnp.ones((L, D), jnp.float32), 'be1': jnp.zeros((L, D), jnp.float32), 'g2': jnp.ones((L, D), jnp.float32), 'be2': jnp.zeros((L, D), jnp.float32), 'W1': n(ks[5], (L, D, F), jnp.float32) * s, 'c1': jnp.zeros((L, F), jnp.float32), 'W2': n(ks[6], (L, F, D), jnp.float32) * s, 'c2': jnp.zeros((L, D), jnp.float32), 'gf': jnp.ones((D,), jnp.float32), 'bef': jnp.zeros((D,), jnp.float32)}
    _L1_attn_a_in = _L1_attn_a_setup()

    def _L1_attn_b_setup():
        import math
        import jax, jax.numpy as jnp
        import numpy as np
        D_MODEL = 128
        N_HEADS = 16
        HEAD_DIM = D_MODEL // N_HEADS
        D_FF = 512
        LN_EPS = 1e-05

        def _layer_norm(x, g, b):
            mu = jnp.mean(x, axis=-1, keepdims=True)
            var = jnp.var(x, axis=-1, keepdims=True)
            return (x - mu) * jax.lax.rsqrt(var + LN_EPS) * g + b
        key = jax.random.key(seed)
        ks = jax.random.split(key, 8)
        s = 0.02
        d, dff = (D_MODEL, D_FF)
        return {'src': jax.random.normal(ks[0], (2, 256, d), dtype=jnp.float32), 'in_proj_w': jax.random.normal(ks[1], (3 * d, d), dtype=jnp.float32) * s, 'in_proj_b': jnp.zeros((3 * d,), dtype=jnp.float32), 'out_w': jax.random.normal(ks[2], (d, d), dtype=jnp.float32) * s, 'out_b': jnp.zeros((d,), dtype=jnp.float32), 'lin1_w': jax.random.normal(ks[3], (dff, d), dtype=jnp.float32) * s, 'lin1_b': jnp.zeros((dff,), dtype=jnp.float32), 'lin2_w': jax.random.normal(ks[4], (d, dff), dtype=jnp.float32) * s, 'lin2_b': jnp.zeros((d,), dtype=jnp.float32), 'ln1_g': jnp.ones((d,), dtype=jnp.float32), 'ln1_b': jnp.zeros((d,), dtype=jnp.float32), 'ln2_g': jnp.ones((d,), dtype=jnp.float32), 'ln2_b': jnp.zeros((d,), dtype=jnp.float32)}
    _L1_attn_b_in = _L1_attn_b_setup()

    def _L1_ffn_setup():
        import jax, jax.numpy as jnp
        import numpy as np
        BLOCK = 16
        _GRID = jnp.array([0.0, 0.5, 1.0, 1.5, 2.0, 3.0, 4.0, 6.0], dtype=jnp.float32)
        _MID = jnp.array([0.25, 0.75, 1.25, 1.75, 2.5, 3.5, 5.0], dtype=jnp.float32)

        def fp4_quant_dequant(x):
            shape = x.shape
            xb = x.reshape(shape[:-1] + (shape[-1] // BLOCK, BLOCK))
            scale = jnp.max(jnp.abs(xb), axis=-1, keepdims=True) / 6.0
            scale = jnp.maximum(scale, jnp.float32(1e-12))
            xn = xb / scale
            idx = jnp.searchsorted(_MID, jnp.abs(xn))
            q = _GRID[idx] * jnp.sign(xn) * scale
            return q.reshape(shape)

        def fp4_linear(x, w):
            xq = fp4_quant_dequant(x)
            wq = fp4_quant_dequant(w)
            return jnp.einsum('bsk,nk->bsn', xq, wq)
        key = jax.random.key(seed)
        k1, k2, k3, k4 = jax.random.split(key, 4)
        H, I = (128, 352)
        x = jax.random.normal(k1, (4, 512, H), dtype=jnp.float32)
        w_gate = jax.random.normal(k2, (I, H), dtype=jnp.float32) * 0.02
        w_up = jax.random.normal(k3, (I, H), dtype=jnp.float32) * 0.02
        w_down = jax.random.normal(k4, (H, I), dtype=jnp.float32) * 0.02
        return {'x': x, 'w_gate': w_gate, 'w_up': w_up, 'w_down': w_down}
    _L1_ffn_in = _L1_ffn_setup()
    _d = {'L0_attn_a_x': _L0_attn_a_in['x'], 'L0_attn_a_Wq': _L0_attn_a_in['Wq'], 'L0_attn_a_Wk': _L0_attn_a_in['Wk'], 'L0_attn_a_Wv': _L0_attn_a_in['Wv'], 'L0_attn_a_Wb': _L0_attn_a_in['Wb'], 'L0_attn_a_Wa': _L0_attn_a_in['Wa'], 'L0_attn_a_Wo': _L0_attn_a_in['Wo'], 'L0_attn_a_ln1_w': _L0_attn_a_in['ln1_w'], 'L0_attn_a_ln1_b': _L0_attn_a_in['ln1_b'], 'L0_attn_a_ln2_w': _L0_attn_a_in['ln2_w'], 'L0_attn_a_ln2_b': _L0_attn_a_in['ln2_b'], 'L0_attn_a_W1': _L0_attn_a_in['W1'], 'L0_attn_a_b1': _L0_attn_a_in['b1'], 'L0_attn_a_W2': _L0_attn_a_in['W2'], 'L0_attn_a_b2': _L0_attn_a_in['b2'], 'L0_attn_b_log_lambda': _L0_attn_b_in['log_lambda'], 'L0_attn_b_B_w': _L0_attn_b_in['B_w'], 'L0_attn_b_C_w': _L0_attn_b_in['C_w'], 'L0_attn_b_D_skip': _L0_attn_b_in['D_skip'], 'L0_attn_b_ssm_norm_w': _L0_attn_b_in['ssm_norm_w'], 'L0_attn_b_ffn_norm_w': _L0_attn_b_in['ffn_norm_w'], 'L0_attn_b_w1': _L0_attn_b_in['w1'], 'L0_attn_b_w2': _L0_attn_b_in['w2'], 'L0_attn_b_w3': _L0_attn_b_in['w3'], 'L0_ffn_gate_w': _L0_ffn_in['gate_w'], 'L0_ffn_w1': _L0_ffn_in['w1'], 'L0_ffn_w3': _L0_ffn_in['w3'], 'L0_ffn_w2': _L0_ffn_in['w2'], 'L0_ffn_e_bias': _L0_ffn_in['e_bias'], 'L1_attn_a_Wq': _L1_attn_a_in['Wq'], 'L1_attn_a_bq': _L1_attn_a_in['bq'], 'L1_attn_a_Wk': _L1_attn_a_in['Wk'], 'L1_attn_a_bk': _L1_attn_a_in['bk'], 'L1_attn_a_Wv': _L1_attn_a_in['Wv'], 'L1_attn_a_bv': _L1_attn_a_in['bv'], 'L1_attn_a_Wo': _L1_attn_a_in['Wo'], 'L1_attn_a_bo': _L1_attn_a_in['bo'], 'L1_attn_a_g1': _L1_attn_a_in['g1'], 'L1_attn_a_be1': _L1_attn_a_in['be1'], 'L1_attn_a_g2': _L1_attn_a_in['g2'], 'L1_attn_a_be2': _L1_attn_a_in['be2'], 'L1_attn_a_W1': _L1_attn_a_in['W1'], 'L1_attn_a_c1': _L1_attn_a_in['c1'], 'L1_attn_a_W2': _L1_attn_a_in['W2'], 'L1_attn_a_c2': _L1_attn_a_in['c2'], 'L1_attn_a_gf': _L1_attn_a_in['gf'], 'L1_attn_a_bef': _L1_attn_a_in['bef'], 'L1_attn_b_in_proj_w': _L1_attn_b_in['in_proj_w'], 'L1_attn_b_in_proj_b': _L1_attn_b_in['in_proj_b'], 'L1_attn_b_out_w': _L1_attn_b_in['out_w'], 'L1_attn_b_out_b': _L1_attn_b_in['out_b'], 'L1_attn_b_lin1_w': _L1_attn_b_in['lin1_w'], 'L1_attn_b_lin1_b': _L1_attn_b_in['lin1_b'], 'L1_attn_b_lin2_w': _L1_attn_b_in['lin2_w'], 'L1_attn_b_lin2_b': _L1_attn_b_in['lin2_b'], 'L1_attn_b_ln1_g': _L1_attn_b_in['ln1_g'], 'L1_attn_b_ln1_b': _L1_attn_b_in['ln1_b'], 'L1_attn_b_ln2_g': _L1_attn_b_in['ln2_g'], 'L1_attn_b_ln2_b': _L1_attn_b_in['ln2_b'], 'L1_ffn_w_gate': _L1_ffn_in['w_gate'], 'L1_ffn_w_up': _L1_ffn_in['w_up'], 'L1_ffn_w_down': _L1_ffn_in['w_down']}
    _x0 = _d['L0_attn_a_x']
    _d['L0_attn_a_x'] = jax.random.normal(jax.random.fold_in(jax.random.key(seed), 1), (2, 1024, 128), dtype=_x0.dtype)
    del _x0
    return _d

def reference(L0_attn_a_x, L0_attn_a_Wq, L0_attn_a_Wk, L0_attn_a_Wv, L0_attn_a_Wb, L0_attn_a_Wa, L0_attn_a_Wo, L0_attn_a_ln1_w, L0_attn_a_ln1_b, L0_attn_a_ln2_w, L0_attn_a_ln2_b, L0_attn_a_W1, L0_attn_a_b1, L0_attn_a_W2, L0_attn_a_b2, L0_attn_b_log_lambda, L0_attn_b_B_w, L0_attn_b_C_w, L0_attn_b_D_skip, L0_attn_b_ssm_norm_w, L0_attn_b_ffn_norm_w, L0_attn_b_w1, L0_attn_b_w2, L0_attn_b_w3, L0_ffn_gate_w, L0_ffn_w1, L0_ffn_w3, L0_ffn_w2, L0_ffn_e_bias, L1_attn_a_Wq, L1_attn_a_bq, L1_attn_a_Wk, L1_attn_a_bk, L1_attn_a_Wv, L1_attn_a_bv, L1_attn_a_Wo, L1_attn_a_bo, L1_attn_a_g1, L1_attn_a_be1, L1_attn_a_g2, L1_attn_a_be2, L1_attn_a_W1, L1_attn_a_c1, L1_attn_a_W2, L1_attn_a_c2, L1_attn_a_gf, L1_attn_a_bef, L1_attn_b_in_proj_w, L1_attn_b_in_proj_b, L1_attn_b_out_w, L1_attn_b_out_b, L1_attn_b_lin1_w, L1_attn_b_lin1_b, L1_attn_b_lin2_w, L1_attn_b_lin2_b, L1_attn_b_ln1_g, L1_attn_b_ln1_b, L1_attn_b_ln2_g, L1_attn_b_ln2_b, L1_ffn_w_gate, L1_ffn_w_up, L1_ffn_w_down):

    def _L0_attn_a_ref(x, Wq, Wk, Wv, Wb, Wa, Wo, ln1_w, ln1_b, ln2_w, ln2_b, W1, b1, W2, b2):
        import jax, jax.numpy as jnp
        import numpy as np
        B, T, D, H, K, V, F = (4, 512, 128, 8, 128, 128, 512)
        EPS = 1e-05

        def layernorm(x, w, b):
            m = jnp.mean(x, -1, keepdims=True)
            v = jnp.var(x, -1, keepdims=True)
            return (x - m) * jax.lax.rsqrt(v + EPS) * w + b

        def l2norm(x):
            return x * jax.lax.rsqrt(jnp.sum(x * x, -1, keepdims=True) + 1e-06)

        def gdn_recurrence(q, k, v, alpha, beta):
            qT = jnp.moveaxis(q, 1, 0)
            kT = jnp.moveaxis(k, 1, 0)
            vT = jnp.moveaxis(v, 1, 0)
            aT = jnp.moveaxis(alpha, 1, 0)
            bT = jnp.moveaxis(beta, 1, 0)

            def step(S, inp):
                q_t, k_t, v_t, a_t, b_t = inp
                kS = jnp.einsum('bhk,bhkv->bhv', k_t, S)
                bk = (b_t[..., None] * k_t)[..., :, None]
                S = a_t[..., None, None] * (S - bk * kS[..., None, :]) + bk * v_t[..., None, :]
                o = jnp.einsum('bhk,bhkv->bhv', q_t, S)
                return (S, o)
            S0 = jnp.zeros((q.shape[0], H, K, V), q.dtype)
            _, oT = jax.lax.scan(step, S0, (qT, kT, vT, aT, bT))
            return jnp.moveaxis(oT, 0, 1)
        b, t, _ = x.shape
        n = layernorm(x, ln1_w, ln1_b)
        q = l2norm(jax.nn.silu(n @ Wq).reshape(b, t, H, K))
        k = l2norm(jax.nn.silu(n @ Wk).reshape(b, t, H, K))
        v = jax.nn.silu(n @ Wv).reshape(b, t, H, V)
        beta = jax.nn.sigmoid(n @ Wb)
        alpha = jax.nn.sigmoid(n @ Wa)
        o = gdn_recurrence(q, k, v, alpha, beta).reshape(b, t, H * V) @ Wo
        x = x + o
        h = layernorm(x, ln2_w, ln2_b)
        x = x + (jax.nn.gelu(h @ W1 + b1, approximate=False) @ W2 + b2)
        return x

    def _L0_attn_b_ref(x, log_lambda, B_w, C_w, D_skip, ssm_norm_w, ffn_norm_w, w1, w2, w3):
        import jax, jax.numpy as jnp
        import numpy as np
        B_SZ, T, D_MODEL, N_STATE = (4, 512, 128, 32)
        D_FF = (int(8 / 3 * D_MODEL) + 7) // 8 * 8
        EPS = 1e-06

        def _rmsnorm(x, w):
            rms = jnp.sqrt(jnp.mean(x * x, axis=-1, keepdims=True) + EPS)
            return x / rms * w
        u = _rmsnorm(x, ssm_norm_w)
        lam = jax.nn.sigmoid(log_lambda)
        Bu = jnp.einsum('btd,nd->btn', u, B_w)

        def step(h, bu_t):
            h = lam * h + bu_t
            return (h, h)
        h0 = jnp.zeros((x.shape[0], log_lambda.shape[0]), dtype=x.dtype)
        _, hs = jax.lax.scan(step, h0, jnp.swapaxes(Bu, 0, 1))
        hs = jnp.swapaxes(hs, 0, 1)
        y = jnp.einsum('btn,dn->btd', hs, C_w) + D_skip * u
        x = x + y
        z = _rmsnorm(x, ffn_norm_w)
        gate = jax.nn.silu(jnp.einsum('btd,fd->btf', z, w1))
        val = jnp.einsum('btd,fd->btf', z, w3)
        ffn = jnp.einsum('btf,df->btd', gate * val, w2)
        return x + ffn

    def _L0_ffn_ref(hidden_states, gate_w, w1, w3, w2, e_bias):
        import jax, jax.numpy as jnp
        import numpy as np
        E = 32
        K = 4
        H = 128
        I = 96
        ROUTED_SCALING_FACTOR = 1.0
        orig_shape = hidden_states.shape
        x = hidden_states.reshape(-1, orig_shape[-1])
        T = x.shape[0]
        router_logits = x @ gate_w.T
        scores = jax.nn.sigmoid(router_logits.astype(jnp.float32))
        _, topk_ids = jax.lax.top_k(scores + e_bias[None, :], K)
        topk_w = jnp.take_along_axis(scores, topk_ids, axis=1)
        topk_w = topk_w / jnp.sum(topk_w, axis=1, keepdims=True)
        combine = jnp.zeros((T, E), jnp.float32).at[jnp.arange(T)[:, None], topk_ids].add(topk_w)
        g = jnp.einsum('th,ehi->tei', x, w1)
        u = jnp.einsum('th,ehi->tei', x, w3)
        a = jax.nn.silu(g) * u * combine[:, :, None].astype(x.dtype)
        out = jnp.einsum('tei,eih->th', a, w2)
        out = out * ROUTED_SCALING_FACTOR
        return out.reshape(orig_shape)

    def _L1_attn_a_ref(x, Wq, bq, Wk, bk, Wv, bv, Wo, bo, g1, be1, g2, be2, W1, c1, W2, c2, gf, bef):
        import jax, jax.numpy as jnp
        import numpy as np
        B, S, D, H, L, F = (4, 256, 128, 16, 8, 512)
        DH = D // H

        def _ln(x, g, b):
            m = jnp.mean(x, axis=-1, keepdims=True)
            v = jnp.mean((x - m) ** 2, axis=-1, keepdims=True)
            return (x - m) * jax.lax.rsqrt(v + 1e-05) * g + b

        def _phi(t):
            return jax.nn.elu(t) + 1.0
        b, s, d = x.shape

        def layer(h, p):
            wq, bq_, wk, bk_, wv, bv_, wo, bo_, g1_, be1_, g2_, be2_, w1, c1_, w2, c2_ = p
            q = _phi((h @ wq + bq_).reshape(b, s, H, DH))
            k = _phi((h @ wk + bk_).reshape(b, s, H, DH))
            v = (h @ wv + bv_).reshape(b, s, H, DH)
            kv = jnp.einsum('bshd,bshm->bhdm', k, v)
            z = 1.0 / (jnp.einsum('bshd,bhd->bsh', q, k.sum(axis=1)) + 1e-06)
            att = jnp.einsum('bshd,bhdm,bsh->bshm', q, kv, z).reshape(b, s, d)
            h = h + att @ wo + bo_
            h = _ln(h, g1_, be1_)
            y = jax.nn.gelu(h @ w1 + c1_, approximate=False) @ w2 + c2_
            return (_ln(h + y, g2_, be2_), None)
        params = (Wq, bq, Wk, bk, Wv, bv, Wo, bo, g1, be1, g2, be2, W1, c1, W2, c2)
        h, _ = jax.lax.scan(layer, x, params)
        return _ln(h, gf, bef)

    def _L1_attn_b_ref(src, in_proj_w, in_proj_b, out_w, out_b, lin1_w, lin1_b, lin2_w, lin2_b, ln1_g, ln1_b, ln2_g, ln2_b):
        import math
        import jax, jax.numpy as jnp
        import numpy as np
        D_MODEL = 128
        N_HEADS = 16
        HEAD_DIM = D_MODEL // N_HEADS
        D_FF = 512
        LN_EPS = 1e-05

        def _layer_norm(x, g, b):
            mu = jnp.mean(x, axis=-1, keepdims=True)
            var = jnp.var(x, axis=-1, keepdims=True)
            return (x - mu) * jax.lax.rsqrt(var + LN_EPS) * g + b
        B, S, d = src.shape
        q = src @ in_proj_w[:d].T + in_proj_b[:d]
        kv = src @ in_proj_w[d:].T + in_proj_b[d:]
        q = q.reshape(B, S, N_HEADS, HEAD_DIM)
        kv = kv.reshape(B, S, 2, N_HEADS, HEAD_DIM)
        k, v = (kv[:, :, 0], kv[:, :, 1])
        softmax_scale = 1.0 / math.sqrt(HEAD_DIM)
        scores = jnp.einsum('bthd,bshd->bhts', q, k) * softmax_scale
        attention = jax.nn.softmax(scores, axis=-2)
        post = jnp.einsum('bhts,bshd->bthd', attention, v)
        post = jax.nn.gelu(post, approximate=False)
        post = post / math.sqrt(S)
        attn_out = post.reshape(B, S, d) @ out_w.T + out_b
        x = _layer_norm(src + attn_out, ln1_g, ln1_b)
        ff = jax.nn.gelu(x @ lin1_w.T + lin1_b, approximate=False) @ lin2_w.T + lin2_b
        return _layer_norm(x + ff, ln2_g, ln2_b)

    def _L1_ffn_ref(x, w_gate, w_up, w_down):
        import jax, jax.numpy as jnp
        import numpy as np
        BLOCK = 16
        _GRID = jnp.array([0.0, 0.5, 1.0, 1.5, 2.0, 3.0, 4.0, 6.0], dtype=jnp.float32)
        _MID = jnp.array([0.25, 0.75, 1.25, 1.75, 2.5, 3.5, 5.0], dtype=jnp.float32)

        def fp4_quant_dequant(x):
            shape = x.shape
            xb = x.reshape(shape[:-1] + (shape[-1] // BLOCK, BLOCK))
            scale = jnp.max(jnp.abs(xb), axis=-1, keepdims=True) / 6.0
            scale = jnp.maximum(scale, jnp.float32(1e-12))
            xn = xb / scale
            idx = jnp.searchsorted(_MID, jnp.abs(xn))
            q = _GRID[idx] * jnp.sign(xn) * scale
            return q.reshape(shape)

        def fp4_linear(x, w):
            xq = fp4_quant_dequant(x)
            wq = fp4_quant_dequant(w)
            return jnp.einsum('bsk,nk->bsn', xq, wq)
        gate = fp4_linear(x, w_gate)
        y = fp4_linear(x, w_up)
        h = jax.nn.silu(gate) * y
        return fp4_linear(h, w_down)
    x = L0_attn_a_x
    x = x + _L0_attn_a_ref(_layernorm(x, axis=-1), L0_attn_a_Wq, L0_attn_a_Wk, L0_attn_a_Wv, L0_attn_a_Wb, L0_attn_a_Wa, L0_attn_a_Wo, L0_attn_a_ln1_w, L0_attn_a_ln1_b, L0_attn_a_ln2_w, L0_attn_a_ln2_b, L0_attn_a_W1, L0_attn_a_b1, L0_attn_a_W2, L0_attn_a_b2)
    x = x + _L0_ffn_ref(_layernorm(x, axis=-1), L0_ffn_gate_w, L0_ffn_w1, L0_ffn_w3, L0_ffn_w2, L0_ffn_e_bias)
    x = x + _L0_attn_b_ref(_layernorm(x, axis=-1), L0_attn_b_log_lambda, L0_attn_b_B_w, L0_attn_b_C_w, L0_attn_b_D_skip, L0_attn_b_ssm_norm_w, L0_attn_b_ffn_norm_w, L0_attn_b_w1, L0_attn_b_w2, L0_attn_b_w3)
    x = x + _L0_ffn_ref(_layernorm(x, axis=-1), L0_ffn_gate_w, L0_ffn_w1, L0_ffn_w3, L0_ffn_w2, L0_ffn_e_bias)
    x = x + _L1_attn_a_ref(_layernorm(x, axis=-1), L1_attn_a_Wq, L1_attn_a_bq, L1_attn_a_Wk, L1_attn_a_bk, L1_attn_a_Wv, L1_attn_a_bv, L1_attn_a_Wo, L1_attn_a_bo, L1_attn_a_g1, L1_attn_a_be1, L1_attn_a_g2, L1_attn_a_be2, L1_attn_a_W1, L1_attn_a_c1, L1_attn_a_W2, L1_attn_a_c2, L1_attn_a_gf, L1_attn_a_bef)
    x = x + _L1_ffn_ref(_layernorm(x, axis=-1), L1_ffn_w_gate, L1_ffn_w_up, L1_ffn_w_down)
    x = x + _L1_attn_b_ref(_layernorm(x, axis=-1), L1_attn_b_in_proj_w, L1_attn_b_in_proj_b, L1_attn_b_out_w, L1_attn_b_out_b, L1_attn_b_lin1_w, L1_attn_b_lin1_b, L1_attn_b_lin2_w, L1_attn_b_lin2_b, L1_attn_b_ln1_g, L1_attn_b_ln1_b, L1_attn_b_ln2_g, L1_attn_b_ln2_b)
    x = x + _L1_ffn_ref(_layernorm(x, axis=-1), L1_ffn_w_gate, L1_ffn_w_up, L1_ffn_w_down)
    return x

_drawn_inputs = setup_inputs


def setup_inputs(seed=0):
    import zlib

    import numpy as np

    out = dict(_drawn_inputs(seed))
    spreads = {'L0_attn_a_ln1_w': (1.0, 0.6),
     'L0_attn_a_ln1_b': (0.0, 0.8),
     'L0_attn_a_ln2_w': (1.0, 0.6),
     'L0_attn_a_ln2_b': (0.0, 0.504),
     'L0_attn_a_b1': (0.0, 0.1),
     'L0_attn_a_b2': (0.0, 0.1),
     'L0_attn_b_D_skip': (0.0, 0.315),
     'L0_attn_b_ssm_norm_w': (1.0, 0.2),
     'L0_attn_b_ffn_norm_w': (1.0, 0.2),
     'L1_attn_a_bq': (0.0, 2.0),
     'L1_attn_a_bk': (0.0, 2.0),
     'L1_attn_a_bv': (0.0, 0.583),
     'L1_attn_a_bo': (0.0, 0.1),
     'L1_attn_a_g1': (1.0, 0.2),
     'L1_attn_a_be1': (0.0, 0.1),
     'L1_attn_a_g2': (1.0, 0.2),
     'L1_attn_a_be2': (0.0, 0.1),
     'L1_attn_a_c1': (0.0, 0.667),
     'L1_attn_a_c2': (0.0, 0.1),
     'L1_attn_a_gf': (1.0, 0.2),
     'L1_attn_a_bef': (0.0, 0.39),
     'L1_attn_b_in_proj_b': (0.0, 0.8),
     'L1_attn_b_out_b': (0.0, 0.492),
     'L1_attn_b_lin1_b': (0.0, 0.8),
     'L1_attn_b_lin2_b': (0.0, 0.496),
     'L1_attn_b_ln1_g': (1.0, 0.2),
     'L1_attn_b_ln1_b': (0.0, 0.562),
     'L1_attn_b_ln2_g': (1.0, 0.2),
     'L1_attn_b_ln2_b': (0.0, 0.509)}
    factors = {'L0_attn_a_Wq': 8.0,
     'L0_attn_a_Wk': 8.0,
     'L0_attn_a_Wv': 8.0,
     'L0_attn_a_Wb': 8.0,
     'L0_attn_a_Wa': 8.0,
     'L0_attn_a_Wo': 8.0,
     'L0_ffn_gate_w': 8.0,
     'L0_ffn_w1': 8.0,
     'L0_ffn_w3': 8.0,
     'L0_ffn_w2': 8.0,
     'L0_ffn_e_bias': 8.0,
     'L1_attn_a_Wq': 8.0,
     'L1_attn_a_Wk': 8.0,
     'L1_attn_a_Wv': 5.056,
     'L1_attn_a_Wo': 3.698,
     'L1_attn_b_in_proj_w': 8.0,
     'L1_attn_b_out_w': 8.0,
     'L1_attn_b_lin1_w': 6.269,
     'L1_attn_b_lin2_w': 5.734,
     'L1_ffn_w_gate': 8.0,
     'L1_ffn_w_up': 8.0,
     'L1_ffn_w_down': 8.0}
    for name, (base, spread) in spreads.items():
        noise = np.random.default_rng([zlib.crc32(name.encode()), seed]).standard_normal(out[name].shape)
        drawn = base * np.exp(spread * noise) if base else spread * noise
        out[name] = jnp.asarray(drawn.astype(out[name].dtype))
    for name, factor in factors.items():
        out[name] = (out[name] * factor).astype(out[name].dtype)
    return out
```

```python
from contextlib import ExitStack

import numpy as np

import concourse.bass as bass
from concourse import mybir

F32 = mybir.dt.float32
BF16 = mybir.dt.bfloat16
ALU = mybir.AluOpType
ACT = mybir.ActivationFunctionType
AX = mybir.AxisListType.X

P = 128
B, T, D = 2, 1024, 128
NT = B * T // P
TPB = T // P
GT = 4
NG = NT // GT
H = 8
HG = 4
LEVELS = [2, 4, 8, 16, 32, 64]

C_ID, C_UTRI, C_GT, C_ONES, C_BLK, C_M0, C_LV = 0, 128, 256, 384, 512, 640, 768
C_RST = C_LV + 64 * len(LEVELS)
C_SEL = C_RST + 512
C_END = C_SEL + 32


def constants():
    i = np.arange(P)
    row, col = i[:, None], i[None, :]
    c = np.zeros((P, C_END), np.float32)
    c[:, C_ID:C_ID + P] = row == col
    c[:, C_UTRI:C_UTRI + P] = row <= col
    c[:, C_GT:C_GT + P] = row > col
    c[:, C_ONES:C_ONES + P] = 1.0
    c[:, C_BLK:C_BLK + P] = row // 8 == col // 8
    c[:, C_M0:C_M0 + P] = -1.0 * ((row % 2 == 0) & (col == row + 1))
    for n, s in enumerate(LEVELS):
        even = i[(i // s) % 2 == 0]
        c[:, C_LV + 64 * n:C_LV + 64 * n + 64] = row // s == even[None, :] // s + 1
    c[:, C_RST:C_RST + 512] = np.arange(512) % 32 != 0
    c[:, C_SEL:C_SEL + 32] = row % 32 == np.arange(32)[None, :]
    return c


class Core:

    def __init__(self, nc, ctx, dram):
        self.nc, self.ctx, self.dram = nc, ctx, dram
        self.n = 0
        self.held = []

    def sem(self, name):
        self.n += 1
        self.held.append(self.nc.alloc_semaphore(name=f"{name}_{self.n}"))
        return self.held[-1]

    def end_phase(self):
        self.nc.clear_and_free_semaphores(self.held)
        self.nc.all_engine_barrier()
        self.held = []


def layernorm_steps(c, st, name, src, dst, eps=1e-5, rms=False):
    k = dict(
        src=src, dst=dst, eps=eps, rms=rms,
        stats=st.enter_context(c.nc.sbuf_tensor(f"{name}_stats", [P, NT, 6], F32)),
        mv=st.enter_context(c.nc.sbuf_tensor(f"{name}_mv", [P, NT, 2], F32)),
        ve=st.enter_context(c.nc.sbuf_tensor(f"{name}_ve", [P, NT], F32)),
        m2=st.enter_context(c.nc.sbuf_tensor(f"{name}_m2", [P, NT], F32)),
        rstd=st.enter_context(c.nc.sbuf_tensor(f"{name}_rstd", [P, NT], F32)),
        stat=c.sem(name + "_stat"), mean=c.sem(name + "_mean"), sq=c.sem(name + "_sq"),
        var=c.sem(name + "_var"), rs=c.sem(name + "_rs"), out=c.sem(name + "_out"),
    )
    return k


def ln_stats(c, e, k, g, base=0):
    a, b = GT * g, GT * g + GT
    for t in range(a, b):
        e.bn_stats(k["stats"][:, t, :], k["src"][:, t, :]).then_inc(k["stat"], 1)
    e.wait_ge(k["stat"], base * NT + b)
    if not isinstance(base, int):
        e.nop(nofuse=True)
    for t in range(a, b):
        e.bn_aggr(k["mv"][:, t, :], k["stats"][:, t, :]).then_inc(k["mean"], 1)
    e.wait_ge(k["mean"], base * NT + b)
    mean, var, ve = k["mv"][:, a:b, 0], k["mv"][:, a:b, 1], k["ve"][:, a:b]
    if k["rms"]:
        m2 = k["m2"][:, a:b]
        e.tensor_tensor(m2, mean, mean, ALU.mult).then_inc(k["sq"], 1)
        e.wait_ge(k["sq"], base * NG + g + 1)
        e.scalar_tensor_tensor(ve, var, k["eps"], m2, ALU.add, ALU.add).then_inc(k["var"], 1)
    else:
        e.tensor_scalar(ve, var, k["eps"], None, ALU.add).then_inc(k["var"], 1)


def ln_rstd(c, e, k, g, base=0):
    e.wait_ge(k["var"], base * NG + g + 1)
    e.tensor_tensor(k["rstd"][:, GT * g:GT * g + GT], k["ve"][:, GT * g:GT * g + GT],
                    c.neg_half[:, 0:GT], ALU.pow).then_inc(k["rs"], 1)


def ln_apply(c, e, k, g, base=0, waits=()):
    e.wait_ge(k["rs"], base * NG + g + 1)
    for s, v in waits:
        e.wait_ge(s, v)
    for t in range(GT * g, GT * g + GT):
        r = k["rstd"][:, t:t + 1]
        if k["rms"]:
            e.tensor_scalar(k["dst"][:, t, :], k["src"][:, t, :], r, None, ALU.mult).then_inc(k["out"], 1)
        else:
            e.tensor_scalar(k["dst"][:, t, :], k["src"][:, t, :], k["mv"][:, t, 0:1], r,
                            ALU.subtract, ALU.mult).then_inc(k["out"], 1)


def transpose_group(c, e, src, bank, g):
    for t in range(GT):
        ins = e.transpose(c.ps[:, bank, t * P:(t + 1) * P], src[:, GT * g + t, :], c.ident)
    return ins


def load_phase(c):
    loaded = c.sem("loaded")
    with c.nc.Block() as block:
        @block.sync
        def _(e):
            e.dma_start(c.const[:, :], c.dram["consts"]).then_inc(loaded, 16)
            e.dma_start(c.x[:, :, :], c.dram["x"].rearrange("b (t p) d -> p (b t) d", p=P)).then_inc(loaded, 16)
            e.wait_ge(loaded, 32)

        @block.gpsimd
        def _(e):
            e.memset(c.neg_half[:, :], -0.5)
            e.memset(c.neg_one[:, :], -1.0)


def gdn_norm_phase(c, st, x1, nT, cols):
    zn = st.enter_context(c.nc.sbuf_tensor("gdn_zn", [P, NT, D], F32))
    ln0 = layernorm_steps(c, st, "ln0", c.x, x1)
    ln1 = layernorm_steps(c, st, "ln1", x1, zn)
    turned, taken = c.sem("turned"), c.sem("taken")
    with c.nc.Block() as block:
        @block.vector
        def _(e):
            for g in range(NG):
                ln_stats(c, e, ln0, g)
            for g in range(NG):
                ln_apply(c, e, ln0, g)
            for g in range(NG):
                e.wait_ge(ln0["out"], GT * g + GT)
                ln_stats(c, e, ln1, g)
            for g in range(NG):
                ln_apply(c, e, ln1, g)

        @block.gpsimd
        def _(e):
            for k in (ln0, ln1):
                for g in range(NG):
                    ln_rstd(c, e, k, g)

        @block.tensor
        def _(e):
            for g in range(NG):
                e.wait_ge(ln1["out"], GT * g + GT)
                transpose_group(c, e, zn, g, g).then_inc(turned, 1)

        @block.scalar
        def _(e):
            for g in range(NG):
                e.wait_ge(turned, g + 1)
                e.activation(nT[:, g * 512:(g + 1) * 512], c.ps[:, g, :], ACT.Identity,
                             bias=cols["ln1_b"], scale=cols["ln1_w"]).then_inc(taken, 1)


def gdn_phase(c, st, x1, nT, w):
    nc = c.nc

    def sb(name, shape):
        return st.enter_context(nc.sbuf_tensor("gdn_" + name, shape, F32))

    nTs = sb("nTs", [P, 2, P])
    raw = {n: sb("raw" + n, [P, H, P]) for n in "qkv"}
    sq = sb("sq", [P, 2, H, P])
    ss = sb("ss", [P, 2, H]); sse = sb("sse", [P, 2, H]); rn = sb("rn", [P, 2, H])
    Q = sb("Q", [P, 2, H, P]); K = sb("K", [P, 2, H, P]); Kb = sb("Kb", [P, 2, H, P])
    Kd = sb("Kd", [P, 2, H, P]); Bv = sb("Bv", [P, 2, H, P])
    z = sb("z", [P, 16]); zneg = sb("zneg", [P, 16]); ez = sb("ez", [P, 16]); lz = sb("lz", [P, 8])
    zmin = sb("zmin", [P, 8]); eb = sb("eb", [P, 8]); beta = sb("beta", [P, 2, 8]); la = sb("la", [P, 2, 8])
    laU = sb("laU", [P, 2, HG, P])
    G = sb("G", [P, 2, 3, 8])
    bG = sb("bG", [P, 2, 8])
    kT = sb("kT", [P, 2, HG, P]); kbT = sb("kbT", [P, 2, HG, P]); qT = sb("qT", [P, 2, HG, P])
    E = sb("E", [P, 2, HG, P]); Em = sb("Em", [P, 2, HG, P])
    AT = sb("AT", [P, 2, HG, P]); PT = sb("PT", [P, 2, HG, P]); A0 = sb("A0", [P, 2, HG, P])
    X = sb("X", [P, 2, HG, P]); XT = sb("XT", [P, 2, HG, P]); Pm = sb("Pm", [P, 2, HG, 64])
    R = sb("R", [P, 2, HG, P]); U = sb("U", [P, 2, HG, P]); oS = sb("oS", [P, 2, HG, P])
    O = sb("O", [P, 2, HG, P]); oT = sb("oT", [P, 2, HG, P])
    S = sb("S", [P, 2, H, P])

    s = {n: c.sem("gdn_" + n) for n in (
        "nts", "ba", "z", "ez_in", "ez", "lz", "zb", "beta", "la", "laU", "proj_q", "proj_k", "proj_v",
        "raw_q", "raw_k", "raw_v", "sq_q", "sq_k", "ss", "sse", "rn", "K", "Q", "Kb", "Kd", "Bv",
        "lst", "G", "bG", "tk", "tb", "tq", "kT", "kbT", "qT", "d", "E", "Em", "kk", "AT", "kq", "PT",
        "ks", "R", "qs", "oS", "A0", "XT0", "t0", "X0", "m1", "Pm", "m2", "X", "t", "XT",
        "u", "U", "pu", "O", "ku", "S", "to", "oT", "wo", "y")}
    ps = c.ps
    bT, bM, bL = (lambda p: p), (lambda p: 2 + p), (lambda p: 4 + p)
    NL = len(LEVELS)

    def hs(p):
        return slice(HG * p, HG * p + HG)

    def bank(k):
        return ps[:, k, :].rearrange("p (h n) -> p h n", h=HG)

    def even(t, p, l):
        return t[:, p].rearrange("p h (k two s) -> p (h k) two s", two=2, s=LEVELS[l])[:, :, 0, :]

    def even_h(t, p, h, l):
        return t[:, p, h].rearrange("p (k two s) -> p k two s", two=2, s=LEVELS[l])[:, :, 0, :]

    def lv(n2, l, p):
        return n2 * (2 * NL) + 2 * l + p + 1

    def pe_proj(e, kind, nx, bx, half):
        bk = {"k": 6, "q": 7, "v": 6}[kind] if half == 0 else {"k": 7, "q": 6, "v": 7}[kind]
        e.matmul(ps[:, bk, :], nTs[:, bx, :], w[kind][:, half * 512:(half + 1) * 512],
                 start=True, stop=True).then_inc(s["proj_" + kind], 1)

    def pe_gates(e, nx, bx):
        e.wait_ge(s["nts"], nx + 1)
        e.matmul(ps[:, 6, 0:16], nTs[:, bx, :], w["ba"][:, :], start=True, stop=True).then_inc(s["ba"], 1)

    def pe_lstat(e, nx, bx):
        e.wait_ge(s["la"], nx + 1)
        for j, m in enumerate((c.utri, c.gt, c.ones)):
            ins = e.matmul(ps[:, 7, 8 * j:8 * j + 8], m, la[:, bx, :], start=True, stop=True)
        ins.then_inc(s["lst"], 1)

    def pe_next(e, step, n2, bx, first=False):
        nx = n2 + 1 if not first else 0
        g = 2 * nx
        if step == 0:
            if not first:
                e.wait_ge(s["y"], n2 + 1)
            pe_gates(e, nx, bx)
        elif step == 1:
            e.wait_ge(s["z"], nx + 1)
            pe_proj(e, "k", nx, bx, 0)
            if not first:
                e.wait_ge(s["G"], nx)
            pe_proj(e, "k", nx, bx, 1)
        elif step == 2:
            e.wait_ge(s["raw_k"], g + 2)
            pe_proj(e, "q", nx, bx, 0)
            pe_proj(e, "q", nx, bx, 1)
        elif step == 3:
            e.wait_ge(s["raw_q"], g + 2)
            pe_proj(e, "v", nx, bx, 0)
            pe_proj(e, "v", nx, bx, 1)
        elif step == 4:
            e.wait_ge(s["raw_v"], g + 2)
            pe_lstat(e, nx, bx)

    def pe_pair(e, n2, b):
        gs = [(p, 2 * n2 + p) for p in range(2)]
        for p, g in gs:
            e.wait_ge(s["K"], g + 1)
            e.wait_ge(s["S"], g + 3)
            for h in range(HG):
                ins = e.transpose(ps[:, bT(p), h * P:(h + 1) * P], K[:, b, HG * p + h, :], c.ident)
            ins.then_inc(s["tk"], 1)
        for p, g in gs:
            e.wait_ge(s["Kb"], g + 1)
            e.wait_ge(s["oT"], g + 1)
            for h in range(HG):
                ins = e.transpose(ps[:, bM(p), h * P:(h + 1) * P], Kb[:, b, HG * p + h, :], c.ident)
            ins.then_inc(s["tb"], 1)
        for p, g in gs:
            e.wait_ge(s["Q"], g + 1)
            e.wait_ge(s["O"], g + 1)
            for h in range(HG):
                ins = e.transpose(ps[:, bL(p), h * P:(h + 1) * P], Q[:, b, HG * p + h, :], c.ident)
            ins.then_inc(s["tq"], 1)
        for p, g in gs:
            e.wait_ge(s["laU"], g + 1)
            e.wait_ge(s["kT"], g + 1)
            e.matmul(ps[:, bT(p), :], c.gt, laU[:, p].rearrange("p h n -> p (h n)"),
                     start=True, stop=True).then_inc(s["d"], 1)
        for p, g in gs:
            e.wait_ge(s["kbT"], g + 1)
            for h in range(HG):
                ins = e.matmul(ps[:, bM(p), h * P:(h + 1) * P], kT[:, p, h, :], kbT[:, p, h, :],
                               start=True, stop=True)
            ins.then_inc(s["kk"], 1)
        for p, g in gs:
            e.wait_ge(s["qT"], g + 1)
            for h in range(HG):
                ins = e.matmul(ps[:, bL(p), h * P:(h + 1) * P], kT[:, p, h, :], qT[:, p, h, :],
                               start=True, stop=True)
            ins.then_inc(s["kq"], 1)
        for p, g in gs:
            e.wait_ge(s["E"], g + 1)
            for h in range(HG):
                ins = e.matmul(ps[:, bT(p), h * P:(h + 1) * P], kT[:, p, h, :], S[:, b, HG * p + h, :],
                               start=True, stop=True)
            ins.then_inc(s["ks"], 1)
        for p, g in gs:
            e.wait_ge(s["AT"], g + 1)
            for h in range(HG):
                ins = e.matmul(ps[:, bM(p), h * P:(h + 1) * P], qT[:, p, h, :], S[:, b, HG * p + h, :],
                               start=True, stop=True)
            ins.then_inc(s["qs"], 1)
        for p, g in gs:
            e.wait_ge(s["XT0"], g + 1)
            e.wait_ge(s["R"], g + 1)
            for h in range(HG):
                ins = e.transpose(ps[:, bT(p), h * P:(h + 1) * P], XT[:, p, h, :], c.ident)
            ins.then_inc(s["t0"], 1)
        for l in range(NL):
            for p, g in gs:
                if l == 0:
                    e.wait_ge(s["X0"], g + 1)
                    e.wait_ge(s["PT"], g + 1)
                else:
                    e.wait_ge(s["X"], lv(n2, l - 1, p))
                for h in range(HG):
                    ins = e.matmul(ps[:, bL(p), h * 64:(h + 1) * 64], AT[:, p, h, :], even_h(X, p, h, l),
                                   start=True, stop=True)
                ins.then_inc(s["m1"], 1)
            for p, g in gs:
                e.wait_ge(s["Pm"], lv(n2, l, p))
                if l:
                    e.wait_ge(s["XT"], lv(n2, l - 1, p))
                for h in range(HG):
                    ins = e.matmul(ps[:, bL(p), 256 + h * 64:256 + (h + 1) * 64], XT[:, p, h, :],
                                   Pm[:, p, h, :], start=True, stop=True)
                ins.then_inc(s["m2"], 1)
            for p, g in gs:
                e.wait_ge(s["X"], lv(n2, l, p))
                for h in range(HG):
                    ins = e.transpose(ps[:, bT(p), h * P:(h + 1) * P], X[:, p, h, :], c.ident)
                ins.then_inc(s["t"], 1)
            pe_next(e, l, n2, 1 - b)
        for p, g in gs:
            e.wait_ge(s["XT"], lv(n2, NL - 1, p))
            e.wait_ge(s["oS"], g + 1)
            for h in range(HG):
                ins = e.matmul(ps[:, bM(p), h * P:(h + 1) * P], XT[:, p, h, :], R[:, p, h, :],
                               start=True, stop=True)
            ins.then_inc(s["u"], 1)
        for p, g in gs:
            e.wait_ge(s["U"], g + 1)
            for h in range(HG):
                ins = e.matmul(ps[:, bL(p), h * P:(h + 1) * P], PT[:, p, h, :], U[:, p, h, :],
                               start=True, stop=True)
            ins.then_inc(s["pu"], 1)
        for p, g in gs:
            for h in range(HG):
                ins = e.matmul(ps[:, bT(p), h * P:(h + 1) * P], Kd[:, b, HG * p + h, :], U[:, p, h, :],
                               start=True, stop=True)
            ins.then_inc(s["ku"], 1)
        for p, g in gs:
            e.wait_ge(s["O"], g + 3)
            for h in range(HG):
                ins = e.transpose(ps[:, bM(p), h * P:(h + 1) * P], O[:, p, h, :], c.ident)
            ins.then_inc(s["to"], 1)
        for p, g in gs:
            e.wait_ge(s["oT"], g + 3)
            for h in range(HG):
                ins = e.matmul(ps[:, 6, 0:P], oT[:, p, h, :], w["o"][:, HG * p + h, :],
                               start=(p == 0 and h == 0), stop=(p == 1 and h == HG - 1))
        ins.then_inc(s["wo"], 1)

    def act_next(e, step, nx, bx):
        g = 2 * nx
        if step == 0:
            e.wait_ge(s["ba"], nx + 1)
            e.wait_ge(s["zb"], nx)
            e.activation(z[:, :], ps[:, 6, 0:16], ACT.Copy).then_inc(s["z"], 1)
        elif step == 1:
            e.wait_ge(s["ez_in"], nx + 1)
            e.activation(ez[:, :], zneg[:, :], ACT.Exp).then_inc(s["ez"], 1)
            e.wait_ge(s["ez"], nx + 1)
            e.wait_ge(s["la"], nx)
            e.activation(lz[:, :], ez[:, 8:16], ACT.Ln, bias=1.0).then_inc(s["lz"], 1)
            silu(e, "k", g)
        elif step == 2:
            silu(e, "q", g)
        elif step == 3:
            silu(e, "v", g)
        elif step == 4:
            e.wait_ge(s["lst"], nx + 1)
            e.activation(G[:, bx].rearrange("p a h -> p (a h)"), ps[:, 7, 0:24], ACT.Exp).then_inc(s["G"], 1)

    def silu(e, kind, g):
        for half in range(2):
            bk = {"k": 6, "q": 7, "v": 6}[kind] if half == 0 else {"k": 7, "q": 6, "v": 7}[kind]
            e.wait_ge(s["proj_" + kind], g + half + 1)
            e.wait_ge(s[{"q": "Q", "k": "Kd", "v": "Bv"}[kind]], g)
            e.activation(raw[kind][:, hs(half), :], bank(bk), ACT.Silu).then_inc(s["raw_" + kind], 1)

    def act_pair(e, n2, b):
        gs = [(p, 2 * n2 + p) for p in range(2)]
        for dst, src, bk, done in ((kT, "tk", bT, "kT"), (kbT, "tb", bM, "kbT"), (qT, "tq", bL, "qT")):
            for p, g in gs:
                e.wait_ge(s[src], g + 1)
                e.activation(dst[:, p], bank(bk(p)), ACT.Copy).then_inc(s[done], 1)
        for p, g in gs:
            e.wait_ge(s["d"], g + 1)
            e.activation(E[:, p], bank(bT(p)), ACT.Exp).then_inc(s["E"], 1)
        for p, g in gs:
            e.wait_ge(s["qs"], g + 1)
            for h in range(HG):
                ins = e.activation(oS[:, p, h, :], ps[:, bM(p), h * P:(h + 1) * P], ACT.Copy,
                                   scale=G[:, b, 0, HG * p + h:HG * p + h + 1])
            ins.then_inc(s["oS"], 1)
        for p, g in gs:
            e.wait_ge(s["t0"], g + 1)
            e.activation(X[:, p], bank(bT(p)), ACT.Copy).then_inc(s["X0"], 1)
        for l in range(NL):
            for p, g in gs:
                e.wait_ge(s["t"], lv(n2, l, p))
                e.activation(XT[:, p], bank(bT(p)), ACT.Copy).then_inc(s["XT"], 1)
            act_next(e, l, n2 + 1, 1 - b)
        for p, g in gs:
            e.wait_ge(s["u"], g + 1)
            e.activation(U[:, p], bank(bM(p)), ACT.Copy).then_inc(s["U"], 1)
        for p, g in gs:
            e.wait_ge(s["to"], g + 1)
            e.activation(oT[:, p], bank(bM(p)), ACT.Copy).then_inc(s["oT"], 1)

    def dve_next(e, step, nx, bx):
        g = 2 * nx
        if step == 0:
            e.wait_ge(s["z"], nx + 1)
            e.tensor_scalar(zneg[:, 0:8], z[:, 0:8], -1.0, None, ALU.mult)
            e.tensor_scalar(zmin[:, :], z[:, 8:16], 0.0, None, ALU.min)
            e.scalar_tensor_tensor(zneg[:, 8:16], z[:, 8:16], -1.0, z[:, 8:16], ALU.mult, ALU.min)\
                .then_inc(s["ez_in"], 1)
        elif step == 1:
            e.wait_ge(s["ez"], nx + 1)
            e.tensor_scalar(eb[:, :], ez[:, 0:8], 1.0, None, ALU.add).then_inc(s["zb"], 1)
            e.wait_ge(s["zb"], nx + 1)
            e.reciprocal(beta[:, bx, :], eb[:, :]).then_inc(s["beta"], 1)
            e.wait_ge(s["lz"], nx + 1)
            e.tensor_tensor(la[:, bx, :], zmin[:, :], lz[:, :], ALU.subtract).then_inc(s["la"], 1)
        elif step == 3:
            for j, kind in enumerate("kq"):
                e.wait_ge(s["sq_" + kind], g + 2)
                e.tensor_reduce(ss[:, j, :], sq[:, j], AX, ALU.add).then_inc(s["ss"], 1)
            e.wait_ge(s["ss"], 2 * nx + 2)
            e.tensor_scalar(sse[:, :, :], ss[:, :, :], 1e-6, None, ALU.add).then_inc(s["sse"], 1)
        elif step == 4:
            e.wait_ge(s["rn"], nx + 1)
            e.wait_ge(s["beta"], nx + 1)
            for half in range(2):
                for h in range(HG * half, HG * half + HG):
                    ins = e.tensor_scalar(K[:, bx, h, :], raw["k"][:, h, :], rn[:, 0, h:h + 1], None, ALU.mult)
                ins.then_inc(s["K"], 1)
            for half in range(2):
                for h in range(HG * half, HG * half + HG):
                    ins = e.tensor_scalar(Kb[:, bx, h, :], raw["k"][:, h, :], rn[:, 0, h:h + 1],
                                          beta[:, bx, h:h + 1], ALU.mult, ALU.mult)
                ins.then_inc(s["Kb"], 1)
            for half in range(2):
                for h in range(HG * half, HG * half + HG):
                    ins = e.tensor_scalar(Q[:, bx, h, :], raw["q"][:, h, :], rn[:, 1, h:h + 1], None, ALU.mult)
                ins.then_inc(s["Q"], 1)
        elif step == 5:
            e.wait_ge(s["raw_v"], g + 2)
            for half in range(2):
                for h in range(HG * half, HG * half + HG):
                    ins = e.tensor_scalar(Bv[:, bx, h, :], raw["v"][:, h, :], beta[:, bx, h:h + 1], None, ALU.mult)
                ins.then_inc(s["Bv"], 1)
            e.wait_ge(s["G"], nx + 1)
            e.scalar_tensor_tensor(bG[:, bx, :], G[:, bx, 0, :], -1.0, beta[:, bx, :], ALU.mult, ALU.mult)\
                .then_inc(s["bG"], 1)
            for half in range(2):
                for h in range(HG * half, HG * half + HG):
                    ins = e.tensor_scalar(Kd[:, bx, h, :], raw["k"][:, h, :], rn[:, 0, h:h + 1],
                                          G[:, bx, 1, h:h + 1], ALU.mult, ALU.mult)
                ins.then_inc(s["Kd"], 1)

    def dve_pair(e, n2, b, tile):
        gs = [(p, 2 * n2 + p) for p in range(2)]
        for p, g in gs:
            e.wait_ge(s["kk"], g + 1)
            e.wait_ge(s["E"], g + 1)
            e.tensor_tensor(AT[:, p], bank(bM(p)), E[:, p], ALU.mult).then_inc(s["AT"], 1)
        for p, g in gs:
            e.wait_ge(s["AT"], g + 1)
            e.tensor_tensor(A0[:, p], AT[:, p], c.m0.unsqueeze(1).broadcast_to([P, HG, P]), ALU.mult)\
                .then_inc(s["A0"], 1)
        for p, g in gs:
            e.wait_ge(s["A0"], g + 1)
            e.tensor_tensor(XT[:, p], A0[:, p], c.ident.unsqueeze(1).broadcast_to([P, HG, P]), ALU.add)\
                .then_inc(s["XT0"], 1)
        for p, g in gs:
            e.wait_ge(s["ks"], g + 1)
            e.wait_ge(s["bG"], n2 + 1)
            e.wait_ge(s["Bv"], g + 1)
            for h in range(HG):
                hh = HG * p + h
                ins = e.scalar_tensor_tensor(R[:, p, h, :], ps[:, bT(p), h * P:(h + 1) * P], bG[:, b, hh:hh + 1],
                                             Bv[:, b, hh, :], ALU.mult, ALU.add)
            ins.then_inc(s["R"], 1)
        for p, g in gs:
            e.wait_ge(s["kq"], g + 1)
            e.wait_ge(s["Em"], g + 1)
            e.tensor_tensor(PT[:, p], bank(bL(p)), Em[:, p], ALU.mult).then_inc(s["PT"], 1)
        for l in range(NL):
            mask = c.lv[:, l, :].unsqueeze(1).broadcast_to([P, HG, 64])
            for p, g in gs:
                e.wait_ge(s["m1"], lv(n2, l, p))
                e.tensor_tensor(Pm[:, p], ps[:, bL(p), 0:256].rearrange("p (h n) -> p h n", h=HG), mask,
                                ALU.mult).then_inc(s["Pm"], 1)
            for p, g in gs:
                e.wait_ge(s["m2"], lv(n2, l, p))
                xe = even(X, p, l)
                e.tensor_tensor(xe, xe, ps[:, bL(p), 256:512].rearrange("p (k s) -> p k s", s=LEVELS[l]),
                                ALU.subtract).then_inc(s["X"], 1)
            dve_next(e, l, n2 + 1, 1 - b)
        for p, g in gs:
            e.wait_ge(s["pu"], g + 1)
            e.wait_ge(s["oS"], g + 1)
            e.tensor_tensor(O[:, p], oS[:, p], bank(bL(p)), ALU.add).then_inc(s["O"], 1)
        for p, g in gs:
            e.wait_ge(s["ku"], g + 1)
            for h in range(HG):
                hh = HG * p + h
                ins = e.scalar_tensor_tensor(S[:, b, hh, :], S[:, b, hh, :], G[:, b, 2, hh:hh + 1],
                                             ps[:, bT(p), h * P:(h + 1) * P], ALU.mult, ALU.add)
            ins.then_inc(s["S"], 1)
        e.wait_ge(s["wo"], n2 + 1)
        xt = x1[:, tile, :]
        e.tensor_tensor(xt, xt, ps[:, 6, 0:P], ALU.add).then_inc(s["y"], 1)

    def pool_next(e, step, nx, bx, tile=None, first=False):
        g = 2 * nx
        if step == 0:
            if not first:
                e.wait_ge(s["y"], nx)
            e.tensor_copy(nTs[:, bx, :], nT[:, bass.ts(tile, P)]).then_inc(s["nts"], 1)
        elif step == 1:
            e.wait_ge(s["la"], nx + 1)
            for half in range(2):
                if not first:
                    e.wait_ge(s["d"], g - 1 + half)
                e.tensor_tensor(laU[:, half], la[:, bx, hs(half)].unsqueeze(2).broadcast_to([P, HG, P]),
                                c.utri.unsqueeze(1).broadcast_to([P, HG, P]), ALU.mult).then_inc(s["laU"], 1)
            for j, kind in enumerate("kq"):
                for half in range(2):
                    e.wait_ge(s["raw_" + kind], g + half + 1)
                    r = raw[kind][:, hs(half), :]
                    e.tensor_tensor(sq[:, j, hs(half)], r, r, ALU.mult).then_inc(s["sq_" + kind], 1)
            e.wait_ge(s["sse"], nx + 1)
            e.tensor_tensor(rn[:, :, :], sse[:, :, :], c.neg_half[:, :].rearrange("p (a b) -> p a b", a=2), ALU.pow)\
                .then_inc(s["rn"], 1)

    def pool_pair(e, n2, b, next_tile):
        pool_next(e, 0, n2 + 1, 1 - b, next_tile)
        for p in range(2):
            g = 2 * n2 + p
            e.wait_ge(s["E"], g + 1)
            e.tensor_tensor(Em[:, p], E[:, p], c.utri.unsqueeze(1).broadcast_to([P, HG, P]), ALU.mult)\
                .then_inc(s["Em"], 1)
        pool_next(e, 1, n2 + 1, 1 - b)

    with nc.Block() as block:
        @block.tensor
        def _(e):
            for step in range(5):
                pe_next(e, step, 0, 0, first=True)
            with e.Fori(0, TPB) as i:
                for b in range(B):
                    pe_pair(e, i * 2 + b, b)

        @block.scalar
        def _(e):
            e.sem_inc(s["oT"], 2)
            for step in range(5):
                act_next(e, step, 0, 0)
            with e.Fori(0, TPB) as i:
                for b in range(B):
                    act_pair(e, i * 2 + b, b)

        @block.vector
        def _(e):
            e.sem_inc(s["O"], 2)
            e.sem_inc(s["y"], 1)
            e.memset(S[:, :, :, :], 0.0).then_inc(s["S"], 4)
            for step in range(6):
                dve_next(e, step, 0, 0)
            e.wait_ge(s["S"], 4)
            with e.Fori(0, TPB) as i:
                for b in range(B):
                    dve_pair(e, i * 2 + b, b, i + b * TPB)

        @block.gpsimd
        def _(e):
            pool_next(e, 0, 0, 0, 0, first=True)
            pool_next(e, 1, 0, 0, first=True)
            with e.Fori(0, TPB) as i:
                for b in range(B):
                    pool_pair(e, i * 2 + b, b, i + TPB if b == 0 else i + 1)


def mlp_buffers(c, st, name, w1, b1, w2, src):
    return dict(
        w1=w1, b1=b1, w2=w2, src=src,
        hid=st.enter_context(c.nc.sbuf_tensor(name + "_hid", [P, 2, 4, 512], F32)),
        up=c.sem(name + "_up"), act=c.sem(name + "_act"), down=c.sem(name + "_down"), out=c.sem(name + "_out"))


def mlp_credits(e, k):
    e.sem_inc(k["act"], 4)


def mlp_up(c, e, k, g, n):
    for f in range(4):
        e.wait_ge(k["act"], n * 4 + f + 1)
        e.matmul(c.ps[:, f, :], k["w1"][:, f * P:(f + 1) * P], k["src"][:, g * 512:(g + 1) * 512],
                 start=True, stop=True).then_inc(k["up"], 1)


def mlp_act(c, e, k, g, n):
    for f in range(4):
        e.wait_ge(k["up"], n * 4 + f + 1)
        e.activation(k["hid"][:, g % 2, f, :], c.ps[:, f, :], ACT.Gelu, bias=k["b1"][:, f:f + 1])\
            .then_inc(k["act"], 1)


def mlp_down(c, e, k, g, n):
    e.wait_ge(k["act"], n * 4 + 8)
    e.wait_ge(k["out"], n + 1)
    for t in range(GT):
        for f in range(4):
            ins = e.matmul(c.ps[:, 4 + g % 2, t * P:(t + 1) * P], k["hid"][:, g % 2, f, t * P:(t + 1) * P],
                           k["w2"][:, f, :], start=(f == 0), stop=(f == 3))
    ins.then_inc(k["down"], 1)


def grp(t, g):
    return t[:, GT * g:GT * g + GT, :]


def bank4(c, k):
    return c.ps[:, k, :].rearrange("p (t d) -> p t d", d=D)


def rows4(r):
    return r.unsqueeze(1).broadcast_to([P, GT, D])


def gdn_mlp_phase(c, st, x1):
    nc = c.nc
    W1 = st.enter_context(nc.sbuf_tensor("m0_w1", [P, 512], F32))
    W2 = st.enter_context(nc.sbuf_tensor("m0_w2", [P, 4, D], F32))
    cols = st.enter_context(nc.sbuf_tensor("m0_cols", [P, 6], F32))
    b2 = st.enter_context(nc.sbuf_tensor("m0_b2", [P, D], F32))
    zn = st.enter_context(nc.sbuf_tensor("m0_z", [P, NT, D], F32))
    zT = st.enter_context(nc.sbuf_tensor("m0_zT", [P, NT * P], F32))
    base = st.enter_context(nc.sbuf_tensor("m0_base", [P, NT, D], F32))
    ln = layernorm_steps(c, st, "m0", x1, zn)
    mlp = mlp_buffers(c, st, "m0", W1, cols[:, 2:6], W2, zT)
    loaded, turned, taken, based, biased = (c.sem(n) for n in ("loaded", "turned", "taken", "based", "biased"))
    with nc.Block() as block:
        @block.sync
        def _(e):
            e.dma_start(W1[:, :], c.dram["L0a_W1"]).then_inc(loaded, 16)
            e.dma_start(W2[:, :, :], c.dram["L0a_W2"].rearrange("(f p) d -> p f d", p=P)).then_inc(loaded, 16)
            e.dma_start(cols[:, :], c.dram["L0a_cols"]).then_inc(loaded, 16)
            e.dma_start(b2[:, :], c.dram["L0a_b2"].partition_broadcast(P)).then_inc(loaded, 16)

        @block.gpsimd
        def _(e):
            e.wait_ge(loaded, 64)
            for g in range(NG):
                ln_rstd(c, e, ln, g)
                e.tensor_tensor(grp(base, g), grp(c.x, g), grp(x1, g), ALU.add).then_inc(based, 1)
                e.wait_ge(based, g + 1)
                e.tensor_tensor(grp(base, g), grp(base, g), rows4(b2[:, :]), ALU.add).then_inc(biased, 1)

        @block.vector
        def _(e):
            e.sem_inc(mlp["out"], 2)
            for g in range(NG):
                ln_stats(c, e, ln, g)
                if g:
                    ln_apply(c, e, ln, g - 1)
            ln_apply(c, e, ln, NG - 1)
            for g in range(NG):
                e.wait_ge(biased, g + 1)
                e.wait_ge(mlp["down"], g + 1)
                e.tensor_tensor(grp(c.x, g), grp(base, g), bank4(c, 4 + g % 2), ALU.add).then_inc(mlp["out"], 1)

        @block.tensor
        def _(e):
            e.wait_ge(loaded, 64)
            for g in range(NG):
                e.wait_ge(ln["out"], GT * g + GT)
                if g >= 2:
                    e.wait_ge(taken, g - 1)
                transpose_group(c, e, zn, 6 + g % 2, g).then_inc(turned, 1)
                if g:
                    mlp_down(c, e, mlp, g - 1, g - 1)
                e.wait_ge(taken, g + 1)
                mlp_up(c, e, mlp, g, g)
            mlp_down(c, e, mlp, NG - 1, NG - 1)

        @block.scalar
        def _(e):
            mlp_credits(e, mlp)
            e.wait_ge(loaded, 64)
            for g in range(NG):
                e.wait_ge(turned, g + 1)
                e.activation(zT[:, g * 512:(g + 1) * 512], c.ps[:, 6 + g % 2, :], ACT.Identity,
                             bias=cols[:, 1:2], scale=cols[:, 0:1]).then_inc(taken, 1)
                mlp_act(c, e, mlp, g, g)


NE, TOPK, FE = 32, 4, 96


def moe_phase(c, st, tag):
    nc = c.nc

    def sb(name, shape, dt=F32):
        return st.enter_context(nc.sbuf_tensor(f"{tag}_{name}", shape, dt))

    zn, zT = sb("z", [P, NT, D]), sb("zT", [P, NT * P])
    gate, ebias = sb("gate", [P, NE]), sb("ebias", [P, NE])
    sc, sbi = sb("scores", [P, NT, NE]), sb("biased", [P, NT, NE])
    m8, ngt = sb("max8", [P, NT, 8]), sb("ngt", [P, NT])
    gt, eq, pre, le = (sb(n, [P, NT, NE]) for n in ("gt", "eq", "pre", "le"))
    tot, rec = sb("tot", [P, NT]), sb("rec", [P, NT])
    comb, rest = sb("comb", [P, NT, NE]), sb("rest", [P, NT, NE])
    c3 = sb("c3", [P, NT, 3 * NE], BF16)
    idb, selb = sb("idb", [P, P], BF16), sb("selb", [P, NE], BF16)
    cT = sb("cT", [3 * NE, NT * P], BF16)
    w13, w2 = sb("w13", [P, 2, 2 * FE]), sb("w2", [FE, 2, D])
    sg, au, a = sb("sg", [FE, 2, 512]), sb("au", [FE, 2, 512]), sb("a", [FE, 2, 512])
    yT = sb("yT", [P, NT * P])
    ln = layernorm_steps(c, st, tag, c.x, zn)
    s = {n: c.sem(f"{tag}_{n}") for n in (
        "loaded", "turned", "taken", "logits", "scores", "step", "m8", "c3", "cturn", "cT", "cast", "zero",
        "w0", "w1", "g", "u", "cb", "silu", "a1", "a", "down", "accT", "yturn", "y")}
    ps = c.ps

    def bc(t):
        return t.unsqueeze(2).broadcast_to([P, NT, NE])

    with nc.Block() as block:
        @block.sync
        def _(e):
            e.dma_start(gate[:, :], c.dram["moe_gateT"]).then_inc(s["loaded"], 16)
            e.dma_start(ebias[:, :], c.dram["moe_ebias"].partition_broadcast(P)).then_inc(s["loaded"], 16)

            def load(ex, slot):
                e.dma_start(w13[:, slot, :], c.dram["moe_w13"][ex]).then_inc(s[f"w{slot}"], 16)
                e.dma_start(w2[:, slot, :], c.dram["moe_w2"][ex]).then_inc(s[f"w{slot}"], 16)

            load(0, 0)
            with e.Fori(0, NE // 2 - 1) as i:
                e.wait_ge(s["down"], i * 8 + 1)
                load(i * 2 + 1, 1)
                e.wait_ge(s["down"], i * 8 + 5)
                load(i * 2 + 2, 0)
            e.wait_ge(s["down"], 4 * NE - 7)
            load(NE - 1, 1)

        @block.gpsimd
        def _(e):
            e.memset(a[:, 1, :], 0.0).then_inc(s["zero"], 1)
            e.memset(w2[:, 1, :], 0.0).then_inc(s["zero"], 1)
            for g in range(NG):
                ln_rstd(c, e, ln, g)

        @block.vector
        def _(e):
            e.tensor_copy(idb[:, :], c.ident).then_inc(s["cast"], 1)
            e.tensor_copy(selb[:, :], c.sel).then_inc(s["cast"], 1)
            for g in range(NG):
                ln_stats(c, e, ln, g)
                if g:
                    ln_apply(c, e, ln, g - 1)
            ln_apply(c, e, ln, NG - 1)
            n = [0]

            def step(ins):
                n[0] += 1
                ins.then_inc(s["step"], 1)
                e.wait_ge(s["step"], n[0])

            e.wait_ge(s["loaded"], 32)
            e.wait_ge(s["scores"], 1)
            step(e.tensor_tensor(sbi[:, :, :], sc[:, :, :], ebias[:, :].unsqueeze(1).broadcast_to([P, NT, NE]), ALU.add))
            for t in range(NT):
                e.max(m8[:, t, :], sbi[:, t, :]).then_inc(s["m8"], 1)
            e.wait_ge(s["m8"], NT)
            thr = bc(m8[:, :, TOPK - 1])
            step(e.tensor_tensor(gt[:, :, :], sbi[:, :, :], thr, ALU.is_gt))
            step(e.tensor_tensor(eq[:, :, :], sbi[:, :, :], thr, ALU.is_equal))
            step(e.tensor_reduce(ngt[:, :], gt[:, :, :], AX, ALU.add))
            step(e.tensor_tensor_scan(pre[:, :, :].rearrange("p t n -> p (t n)"), c.rst[:, :],
                                      eq[:, :, :].rearrange("p t n -> p (t n)"), 0.0, ALU.mult, ALU.add))
            step(e.tensor_tensor(pre[:, :, :], pre[:, :, :], bc(ngt[:, :]), ALU.add))
            step(e.scalar_tensor_tensor(le[:, :, :], pre[:, :, :], float(TOPK), eq[:, :, :], ALU.is_le, ALU.mult))
            step(e.tensor_tensor(gt[:, :, :], gt[:, :, :], le[:, :, :], ALU.add))
            step(e.tensor_tensor(gt[:, :, :], gt[:, :, :], sc[:, :, :], ALU.mult))
            step(e.tensor_reduce(tot[:, :], gt[:, :, :], AX, ALU.add))
            step(e.reciprocal(rec[:, :], tot[:, :]))
            step(e.tensor_tensor(comb[:, :, :], gt[:, :, :], bc(rec[:, :]), ALU.mult))
            step(e.tensor_copy(c3[:, :, 0:NE], comb[:, :, :]))
            step(e.tensor_tensor(rest[:, :, :], comb[:, :, :], c3[:, :, 0:NE], ALU.subtract))
            step(e.tensor_copy(c3[:, :, NE:2 * NE], rest[:, :, :]))
            e.tensor_tensor(c3[:, :, 2 * NE:3 * NE], rest[:, :, :], c3[:, :, NE:2 * NE], ALU.subtract).then_inc(s["c3"], 1)
            e.sem_inc(s["a"], 2)
            e.sem_inc(s["a1"], 1)
            with e.Fori(0, NE) as ex:
                for g in range(NG):
                    m = ex * NG + g
                    e.wait_ge(s["silu"], m + 2)
                    e.wait_ge(s["u"], m + 1)
                    e.tensor_tensor(au[:, g % 2, :], sg[:, g % 2, :], ps[0:FE, (3 * g + 1) % 4, :], ALU.mult)\
                        .then_inc(s["a1"], 1)
                    e.wait_ge(s["cb"], m + 1)
                    e.wait_ge(s["a1"], m + 2)
                    e.tensor_tensor(a[:, g % 2, :], au[:, g % 2, :], ps[0:FE, (3 * g + 2) % 4, :], ALU.mult)\
                        .then_inc(s["a"], 1)
            for g in range(NG):
                e.wait_ge(s["yturn"], g + 1)
                e.tensor_tensor(grp(c.x, g), grp(c.x, g), bank4(c, g), ALU.add).then_inc(s["y"], 1)

        @block.tensor
        def _(e):
            for g in range(NG):
                e.wait_ge(ln["out"], GT * g + GT)
                transpose_group(c, e, zn, g, g).then_inc(s["turned"], 1)
            e.wait_ge(s["loaded"], 32)
            for t in range(NT):
                if t % GT == 0:
                    e.wait_ge(s["taken"], t // GT + 1)
                ins = e.matmul(ps[:, 4, t * NE:(t + 1) * NE], zT[:, t * P:(t + 1) * P], gate[:, :],
                               start=True, stop=True)
            ins.then_inc(s["logits"], 1)
            e.wait_ge(s["c3"], 1)
            e.wait_ge(s["cast"], 2)
            for t in range(NT):
                out = ps[0:3 * NE, t // 8, :].bitcast(BF16)[:, (t % 8) * P:(t % 8 + 1) * P]
                ins = e.transpose(out, c3[:, t, :], idb[:, :])
                if t % 8 == 7:
                    ins.then_inc(s["cturn"], 1)
            e.wait_ge(s["zero"], 2)
            e.wait_ge(s["scores"], 1)
            for g in range(NG):
                e.matmul(ps[:, 4 + g, :], w2[:, 1, :], a[:, 1, :], start=True, stop=False, skip_group_check=True)
            e.wait_ge(s["cT"], 2)

            def down(g, slot, m):
                e.wait_ge(s["a"], m + 2)
                e.matmul(ps[:, 4 + g, :], w2[:, slot, :], a[:, g % 2, :], start=False, stop=False,
                         skip_group_check=True).then_inc(s["down"], 1)

            with e.Fori(0, NE // 2) as i:
                for slot in range(2):
                    ex = i * 2 + slot
                    e.wait_ge(s[f"w{slot}"], i * 32 + 32)
                    for g in range(NG):
                        m = ex * NG + g
                        z = zT[:, g * 512:(g + 1) * 512]
                        e.wait_ge(s["a"], m + 1)
                        e.matmul(ps[0:FE, 3 * g % 4, :], w13[:, slot, 0:FE], z, start=True, stop=True).then_inc(s["g"], 1)
                        e.wait_ge(s["silu"], m + 1)
                        e.matmul(ps[0:FE, (3 * g + 1) % 4, :], w13[:, slot, FE:2 * FE], z, start=True, stop=True)\
                            .then_inc(s["u"], 1)
                        e.wait_ge(s["a1"], m + 1)
                        e.matmul(ps[0:FE, (3 * g + 2) % 4, :], selb[0:3 * NE, bass.ds(ex, 1)].broadcast_to([3 * NE, FE]),
                                 cT[:, g * 512:(g + 1) * 512], start=True, stop=True).then_inc(s["cb"], 1)
                        down((g - 1) % NG, slot if g else 1 - slot, m)
            down(NG - 1, 1, 4 * NE)
            for g in range(NG):
                e.wait_ge(s["accT"], g + 1)
                transpose_cols(c, e, yT, g, g).then_inc(s["yturn"], 1)

        @block.scalar
        def _(e):
            for g in range(NG):
                e.wait_ge(s["turned"], g + 1)
                e.activation(zT[:, g * 512:(g + 1) * 512], ps[:, g, :], ACT.Copy).then_inc(s["taken"], 1)
            e.wait_ge(s["logits"], 1)
            e.activation(sc[:, :, :].rearrange("p t n -> p (t n)"), ps[:, 4, :], ACT.Sigmoid).then_inc(s["scores"], 1)
            for k in range(2):
                e.wait_ge(s["cturn"], k + 1)
                e.activation(cT[:, k * 1024:(k + 1) * 1024], ps[0:3 * NE, k, :].bitcast(BF16), ACT.Copy)\
                    .then_inc(s["cT"], 1)
            e.sem_inc(s["silu"], 1)
            with e.Fori(0, NE) as ex:
                for g in range(NG):
                    e.wait_ge(s["g"], ex * NG + g + 1)
                    e.activation(sg[:, g % 2, :], ps[0:FE, 3 * g % 4, :], ACT.Silu).then_inc(s["silu"], 1)
            e.wait_ge(s["down"], 4 * NE + 1)
            for g in range(NG):
                e.activation(yT[:, g * 512:(g + 1) * 512], ps[:, 4 + g, :], ACT.Copy).then_inc(s["accT"], 1)


def transpose_cols(c, e, src, bank, g):
    for t in range(GT):
        ins = e.transpose(c.ps[:, bank, t * P:(t + 1) * P], src[:, (GT * g + t) * P:(GT * g + t + 1) * P], c.ident)
    return ins


FS = 344
FSC = [(0, 128), (128, 128), (256, 88)]


def ssm_phase(c, st):
    nc = c.nc

    def sb(name, shape):
        return st.enter_context(nc.sbuf_tensor("ssm_" + name, shape, F32))

    a, un, uT = sb("a", [P, NT, D]), sb("un", [P, NT, D]), sb("uT", [P, NT * P])
    hs, lam = sb("hs", [32, NT * P]), sb("lam", [32, 1])
    Bw, Cw, loglam = sb("Bw", [P, 32]), sb("Cw", [32, D]), sb("loglam", [32, 1])
    cols, diag = sb("cols", [P, 3]), sb("diag", [P, P])
    zT, base = sb("zT", [P, NT * P]), sb("base", [P, NT, D])
    W1, W3, W2 = sb("W1", [P, FS]), sb("W3", [P, FS]), sb("W2", [P, 3, D])
    sg, hid = sb("sg", [P, 2, 512]), sb("hid", [P, 2, 3, 512])
    ln = layernorm_steps(c, st, "ssm0", c.x, a)
    r1 = layernorm_steps(c, st, "ssm1", a, un, eps=1e-6, rms=True)
    r2 = layernorm_steps(c, st, "ssm2", a, un, eps=1e-6, rms=True)
    s = {n: c.sem("ssm_" + n) for n in (
        "loaded", "lam", "diag", "turned", "uT", "bu", "hs", "mix", "x1", "turned2", "zT", "based",
        "gate", "val", "silu", "hid", "down", "out")}
    ps = c.ps
    NF = len(FSC)
    def residual(e, g):
        e.wait_ge(s["down"], g + 1)
        e.wait_ge(s["based"], g + 1)
        e.tensor_tensor(grp(c.x, g), grp(base, g), bank4(c, 4 + g % 2), ALU.add).then_inc(s["out"], 1)

    def down(e, g):
        e.wait_ge(s["hid"], NF * g + NF)
        if g >= 2:
            e.wait_ge(s["out"], g - 1)
        for t in range(GT):
            for f, (f0, fn) in enumerate(FSC):
                ins = e.matmul(ps[:, 4 + g % 2, t * P:(t + 1) * P], hid[0:fn, g % 2, f, t * P:(t + 1) * P],
                               W2[0:fn, f, :], start=(f == 0), stop=(f == NF - 1))
        ins.then_inc(s["down"], 1)

    with nc.Block() as block:
        @block.sync
        def _(e):
            e.dma_start(Bw[:, :], c.dram["ssm_BT"]).then_inc(s["loaded"], 16)
            e.dma_start(Cw[:, :], c.dram["ssm_CT"]).then_inc(s["loaded"], 16)
            e.dma_start(loglam[:, :], c.dram["ssm_loglam"]).then_inc(s["loaded"], 16)
            e.dma_start(cols[:, :], c.dram["ssm_cols"]).then_inc(s["loaded"], 16)
            e.dma_start(W1[:, :], c.dram["ssm_W1T"]).then_inc(s["loaded"], 16)
            e.dma_start(W3[:, :], c.dram["ssm_W3T"]).then_inc(s["loaded"], 16)
            for f, (f0, fn) in enumerate(FSC):
                e.dma_start(W2[0:fn, f, :], c.dram["ssm_W2T"][f0:f0 + fn, :]).then_inc(s["loaded"], 16)

        @block.gpsimd
        def _(e):
            for k in (ln, r1):
                for g in range(NG):
                    ln_rstd(c, e, k, g)
            for g in range(NG):
                ln_rstd(c, e, r2, g)
                e.wait_ge(s["x1"], g + 1)
                e.tensor_tensor(grp(base, g), grp(c.x, g), grp(a, g), ALU.add).then_inc(s["based"], 1)

        @block.vector
        def _(e):
            for g in range(NG):
                ln_stats(c, e, ln, g)
            for g in range(NG):
                ln_apply(c, e, ln, g)
            for g in range(NG):
                e.wait_ge(ln["out"], GT * g + GT)
                ln_stats(c, e, r1, g)
            for g in range(NG):
                ln_apply(c, e, r1, g)
            e.wait_ge(s["loaded"], 144)
            e.tensor_scalar(diag[:, :], c.ident, cols[:, 1:2], None, ALU.mult).then_inc(s["diag"], 1)
            e.wait_ge(s["lam"], 1)
            for g in range(NG):
                e.wait_ge(s["bu"], g + 1)
                first = g % (NG // B) == 0
                if not first:
                    e.wait_ge(s["hs"], g)
                e.tensor_tensor_scan(hs[:, g * 512:(g + 1) * 512], lam[:, 0:1].broadcast_to([32, 512]), ps[0:32, g % 2, :],
                                     0.0 if first else hs[:, g * 512 - 1:g * 512], ALU.mult, ALU.add)\
                    .then_inc(s["hs"], 1)
            for g in range(NG):
                e.wait_ge(s["mix"], g + 1)
                e.tensor_tensor(grp(a, g), grp(a, g), bank4(c, 2 + g % 2), ALU.add).then_inc(s["x1"], 1)
            for g in range(NG):
                e.wait_ge(s["x1"], g + 1)
                ln_stats(c, e, r2, g)
                if g:
                    ln_apply(c, e, r2, g - 1)
            ln_apply(c, e, r2, NG - 1)
            for g in range(NG):
                for f, (f0, fn) in enumerate(FSC):
                    m = NF * g + f
                    e.wait_ge(s["silu"], m + 1)
                    e.wait_ge(s["val"], m + 1)
                    e.tensor_tensor(hid[0:fn, g % 2, f, :], sg[0:fn, m % 2, :], ps[0:fn, 2 + m % 2, :], ALU.mult)\
                        .then_inc(s["hid"], 1)
                if g:
                    residual(e, g - 1)
            residual(e, NG - 1)

        @block.tensor
        def _(e):
            for g in range(NG):
                e.wait_ge(r1["out"], GT * g + GT)
                if g >= 2:
                    e.wait_ge(s["uT"], g - 1)
                transpose_group(c, e, un, 6 + g % 2, g).then_inc(s["turned"], 1)
            e.wait_ge(s["loaded"], 144)
            for g in range(NG):
                e.wait_ge(s["uT"], g + 1)
                if g >= 2:
                    e.wait_ge(s["hs"], g - 1)
                e.matmul(ps[0:32, g % 2, :], Bw[:, :], uT[:, g * 512:(g + 1) * 512], start=True, stop=True)\
                    .then_inc(s["bu"], 1)
            e.wait_ge(s["diag"], 1)
            for g in range(NG):
                e.wait_ge(s["hs"], g + 1)
                if g >= 2:
                    e.wait_ge(s["x1"], g - 1)
                for t in range(GT):
                    tok = slice((GT * g + t) * P, (GT * g + t + 1) * P)
                    e.matmul(ps[:, 2 + g % 2, t * P:(t + 1) * P], hs[:, tok], Cw[:, :], start=True, stop=False)
                    ins = e.matmul(ps[:, 2 + g % 2, t * P:(t + 1) * P], uT[:, tok], diag[:, :], start=False, stop=True)
                ins.then_inc(s["mix"], 1)
            for g in range(NG):
                e.wait_ge(r2["out"], GT * g + GT)
                if g >= 2:
                    e.wait_ge(s["zT"], g - 1)
                transpose_group(c, e, un, 6 + g % 2, g).then_inc(s["turned2"], 1)
            for g in range(NG):
                e.wait_ge(s["zT"], g + 1)
                for f, (f0, fn) in enumerate(FSC):
                    m = NF * g + f
                    if m >= 2:
                        e.wait_ge(s["silu"], m - 1)
                    if m < 2:
                        e.wait_ge(s["hs"], NG)
                    e.matmul(ps[0:fn, m % 2, :], W1[:, f0:f0 + fn], zT[:, g * 512:(g + 1) * 512],
                             start=True, stop=True).then_inc(s["gate"], 1)
                    if m >= 2:
                        e.wait_ge(s["hid"], m - 1)
                    else:
                        e.wait_ge(s["x1"], NG)
                    e.matmul(ps[0:fn, 2 + m % 2, :], W3[:, f0:f0 + fn], zT[:, g * 512:(g + 1) * 512],
                             start=True, stop=True).then_inc(s["val"], 1)
                if g:
                    down(e, g - 1)
            down(e, NG - 1)

        @block.scalar
        def _(e):
            e.wait_ge(s["loaded"], 144)
            e.activation(lam[:, :], loglam[:, :], ACT.Sigmoid).then_inc(s["lam"], 1)
            for g in range(NG):
                e.wait_ge(s["turned"], g + 1)
                e.activation(uT[:, g * 512:(g + 1) * 512], ps[:, 6 + g % 2, :], ACT.Copy, scale=cols[:, 0:1])\
                    .then_inc(s["uT"], 1)
            for g in range(NG):
                e.wait_ge(s["turned2"], g + 1)
                e.activation(zT[:, g * 512:(g + 1) * 512], ps[:, 6 + g % 2, :], ACT.Copy, scale=cols[:, 2:3])\
                    .then_inc(s["zT"], 1)
            for g in range(NG):
                for f, (f0, fn) in enumerate(FSC):
                    m = NF * g + f
                    e.wait_ge(s["gate"], m + 1)
                    if m >= 2:
                        e.wait_ge(s["hid"], m - 1)
                    e.activation(sg[0:fn, m % 2, :], ps[0:fn, m % 2, :], ACT.Silu).then_inc(s["silu"], 1)


FQ = 352
FQC = [(0, 128), (128, 128), (256, 96)]
BLOCK = 16


class Fp4:

    def __init__(self, c, st, name, nb):
        def sb(n, shape):
            return st.enter_context(c.nc.sbuf_tensor(f"{name}_{n}", shape, F32))
        self.amax, self.scale, self.inv = (sb(n, [P, nb]) for n in ("amax", "scale", "inv"))
        self.ax, self.r05, self.r1, self.r2 = (sb(n, [P, nb, BLOCK]) for n in ("ax", "r05", "r1", "r2"))
        self.sem, self.n = c.sem(name + "_fp4"), 0

    def quantise(self, e, q, x, np_, nb, done):
        def step(ins):
            self.n += 1
            ins.then_inc(self.sem, 1)
            return self.n
        amax, scale, inv = self.amax[0:np_, 0:nb], self.scale[0:np_, 0:nb], self.inv[0:np_, 0:nb]
        ax, r05, r1, r2 = (t[0:np_, 0:nb, :] for t in (self.ax, self.r05, self.r1, self.r2))
        wide = [np_, nb, BLOCK]
        n = step(e.tensor_reduce(amax, x, AX, ALU.max, apply_absolute_value=True))
        e.wait_ge(self.sem, n)
        n = step(e.tensor_scalar(scale, amax, 1.0 / 6.0, 1e-12, ALU.mult, ALU.max))
        e.wait_ge(self.sem, n)
        n = step(e.reciprocal(inv, scale))
        e.wait_ge(self.sem, n)
        n = step(e.tensor_scalar(inv, inv, 1.0 - 2.0 ** -22, None, ALU.mult))
        e.wait_ge(self.sem, n)
        u = mybir.dt.uint32
        n = step(e.tensor_tensor(r1, x, inv.unsqueeze(2).broadcast_to(wide), ALU.mult))
        e.wait_ge(self.sem, n)
        n = step(e.tensor_scalar(ax.bitcast(u), r1.bitcast(u), 0x7FFFFFFF, None, ALU.bitwise_and))
        e.wait_ge(self.sem, n)
        for r, m in ((r1, 1.5 * 2 ** 23), (r05, 1.5 * 2 ** 22), (r2, 1.5 * 2 ** 24)):
            n = step(e.tensor_scalar(r, ax, m, m, ALU.add, ALU.subtract))
        e.wait_ge(self.sem, n - 2)
        n = step(e.tensor_scalar(r1, r1, 2.0, 4.0, ALU.max, ALU.min))
        e.wait_ge(self.sem, n)
        n = step(e.scalar_tensor_tensor(r1, r05, 2.0, r1, ALU.min, ALU.add))
        e.wait_ge(self.sem, n)
        n = step(e.scalar_tensor_tensor(r1, r2, 4.0, r1, ALU.max, ALU.add))
        e.wait_ge(self.sem, n)
        n = step(e.scalar_tensor_tensor(r1, r1, -6.0, scale.unsqueeze(2).broadcast_to(wide), ALU.add, ALU.mult))
        e.wait_ge(self.sem, n)
        e.scalar_tensor_tensor(q.bitcast(u), x.bitcast(u), 0x80000000, r1.bitcast(u),
                               ALU.bitwise_and, ALU.bitwise_or).then_inc(done, 1)


def blocks(t):
    return t.rearrange("p (b k) -> p b k", k=BLOCK)


def fp4_weight_phase(c, st, wgu, wd):
    nc = c.nc
    rows = st.enter_context(nc.sbuf_tensor("fw_rows", [P, 6, P], F32))
    down = st.enter_context(nc.sbuf_tensor("fw_down", [P, FQ], F32))
    rq = st.enter_context(nc.sbuf_tensor("fw_rq", [P, 6, P], F32))
    dq = st.enter_context(nc.sbuf_tensor("fw_dq", [P, FQ], F32))
    fp4 = Fp4(c, st, "fw", 48)
    loaded, quant, turned, taken = (c.sem("fw_" + n) for n in ("loaded", "quant", "turned", "taken"))
    with nc.Block() as block:
        @block.sync
        def _(e):
            for m, name in enumerate(("fp4_gate", "fp4_up")):
                for f, (f0, fn) in enumerate(FQC):
                    e.dma_start(rows[0:fn, 3 * m + f, :], c.dram[name][f0:f0 + fn, :]).then_inc(loaded, 16)
            e.dma_start(down[:, :], c.dram["fp4_down"]).then_inc(loaded, 16)

        @block.vector
        def _(e):
            e.wait_ge(loaded, 112)
            for m in range(2):
                for f, (f0, fn) in enumerate(FQC):
                    fp4.quantise(e, blocks(rq[0:fn, 3 * m + f, :]), blocks(rows[0:fn, 3 * m + f, :]), fn, P // BLOCK, quant)
            fp4.quantise(e, blocks(dq[:, :]), blocks(down[:, :]), P, FQ // BLOCK, quant)

        @block.tensor
        def _(e):
            e.wait_ge(quant, 7)
            for m in range(2):
                for f, (f0, fn) in enumerate(FQC):
                    ins = e.transpose(c.ps[:, m, f0:f0 + fn], rq[0:fn, 3 * m + f, :], c.ident[0:fn, 0:fn])
            for f, (f0, fn) in enumerate(FQC):
                ins = e.transpose(c.ps[0:fn, 2, f * P:(f + 1) * P], dq[:, f0:f0 + fn], c.ident)
            ins.then_inc(turned, 1)

        @block.scalar
        def _(e):
            e.wait_ge(turned, 1)
            for m in range(2):
                e.activation(wgu[:, m * FQ:(m + 1) * FQ], c.ps[:, m, 0:FQ], ACT.Copy).then_inc(taken, 1)
            for f, (f0, fn) in enumerate(FQC):
                e.activation(wd[0:fn, f, :], c.ps[0:fn, 2, f * P:(f + 1) * P], ACT.Copy).then_inc(taken, 1)


def fp4_phase(c, st, tag, wgu, wd):
    nc = c.nc

    def sb(name, shape):
        return st.enter_context(nc.sbuf_tensor(f"{tag}_{name}", shape, F32))

    zn, zq, zT = sb("z", [P, NT, D]), sb("zq", [P, NT, D]), sb("zT", [P, NT * P])
    sg, h, hq, hT = sb("sg", [P, 2, FQ]), sb("h", [P, 2, FQ]), sb("hq", [P, 2, FQ]), sb("hT", [P, 2, 3, P])
    ln = layernorm_steps(c, st, tag, c.x, zn)
    fx, fh = Fp4(c, st, tag + "x", GT * D // BLOCK), Fp4(c, st, tag + "h", FQ // BLOCK)
    s = {n: c.sem(f"{tag}_{n}") for n in (
        "zq", "turned", "zT", "gate", "up", "silu", "h", "hq", "hturn", "hT", "down", "out")}
    ps = c.ps
    def residual(e, t):
        e.wait_ge(s["down"], t + 1)
        e.tensor_tensor(c.x[:, t, :], c.x[:, t, :], ps[:, 6 + t % 2, 0:P], ALU.add).then_inc(s["out"], 1)

    def down(e, t):
        e.wait_ge(s["hq"], t + 1)
        if t >= 2:
            e.wait_ge(s["hT"], 3 * (t - 1))
        for f, (f0, fn) in enumerate(FQC):
            ins = e.transpose(ps[0:fn, 4 + t % 2, f * P:(f + 1) * P], hq[:, t % 2, f0:f0 + fn], c.ident)
        ins.then_inc(s["hturn"], 1)
        e.wait_ge(s["hT"], 3 * t + 3)
        if t >= 2:
            e.wait_ge(s["out"], t - 1)
        for f, (f0, fn) in enumerate(FQC):
            ins = e.matmul(ps[:, 6 + t % 2, 0:P], hT[0:fn, t % 2, f, :], wd[0:fn, f, :],
                           start=(f == 0), stop=(f == 2))
        ins.then_inc(s["down"], 1)

    def turn(e, t):
        e.wait_ge(s["hturn"], t + 1)
        for f, (f0, fn) in enumerate(FQC):
            e.activation(hT[0:fn, t % 2, f, :], ps[0:fn, 4 + t % 2, f * P:(f + 1) * P], ACT.Copy).then_inc(s["hT"], 1)

    with nc.Block() as block:
        @block.gpsimd
        def _(e):
            for g in range(NG):
                ln_rstd(c, e, ln, g)

        @block.vector
        def _(e):
            for g in range(NG):
                ln_stats(c, e, ln, g)
                if g:
                    ln_apply(c, e, ln, g - 1)
            ln_apply(c, e, ln, NG - 1)
            for g in range(NG):
                e.wait_ge(ln["out"], GT * g + GT)
                fx.quantise(e, blocks(grp(zq, g).rearrange("p t d -> p (t d)")),
                            blocks(grp(zn, g).rearrange("p t d -> p (t d)")), P, GT * D // BLOCK, s["zq"])
                for t in range(GT * g, GT * g + GT):
                    e.wait_ge(s["silu"], t + 1)
                    e.wait_ge(s["up"], t + 1)
                    e.tensor_tensor(h[:, t % 2, :], sg[:, t % 2, :], ps[:, 2 + t % 2, 0:FQ], ALU.mult).then_inc(s["h"], 1)
                    e.wait_ge(s["h"], t + 1)
                    fh.quantise(e, blocks(hq[:, t % 2, :]), blocks(h[:, t % 2, :]), P, FQ // BLOCK, s["hq"])
                    if t:
                        residual(e, t - 1)
            residual(e, NT - 1)

        @block.tensor
        def _(e):
            for g in range(NG):
                e.wait_ge(s["zq"], g + 1)
                if g:
                    e.wait_ge(s["out"], GT * g - 1)
                transpose_group(c, e, zq, 6, g).then_inc(s["turned"], 1)
                e.wait_ge(s["zT"], g + 1)
                for t in range(GT * g, GT * g + GT):
                    tok = zT[:, t * P:(t + 1) * P]
                    if t >= 2:
                        e.wait_ge(s["silu"], t - 1)
                    e.matmul(ps[:, t % 2, 0:FQ], tok, wgu[:, 0:FQ], start=True, stop=True).then_inc(s["gate"], 1)
                    if t >= 2:
                        e.wait_ge(s["h"], t - 1)
                    e.matmul(ps[:, 2 + t % 2, 0:FQ], tok, wgu[:, FQ:2 * FQ], start=True, stop=True).then_inc(s["up"], 1)
                    if t % GT:
                        down(e, t - 1)
                down(e, GT * g + GT - 1)

        @block.scalar
        def _(e):
            for g in range(NG):
                e.wait_ge(s["turned"], g + 1)
                e.activation(zT[:, g * 512:(g + 1) * 512], ps[:, 6, :], ACT.Copy).then_inc(s["zT"], 1)
                for t in range(GT * g, GT * g + GT):
                    e.wait_ge(s["gate"], t + 1)
                    if t >= 2:
                        e.wait_ge(s["h"], t - 1)
                    e.activation(sg[:, t % 2, :], ps[:, t % 2, 0:FQ], ACT.Silu).then_inc(s["silu"], 1)
                    if t % GT:
                        turn(e, t - 1)
                turn(e, GT * g + GT - 1)

NL1 = 8


def linear_attention_phase(c, st):
    nc = c.nc

    def sb(name, shape):
        return st.enter_context(nc.sbuf_tensor("la_" + name, shape, F32))

    Wq, Wkv, Wo = sb("Wq", [P, P]), sb("Wkv", [P, 2 * P]), sb("Wo", [P, P])
    W1, W2 = sb("W1", [P, 512]), sb("W2", [P, 4, D])
    colA, colB = sb("colA", [P, 3]), sb("colB", [P, 6])
    rowA, rowB = sb("rowA", [P, 5, P]), sb("rowB", [P, 3, P])
    rowF = sb("rowF", [P, 4, P])
    bq1, bk1 = sb("bq1", [P, 1]), sb("bk1", [P, 2, P])
    sumA, sumB = sb("sumA", [P, P]), sb("sumB", [P, P])
    z, base = sb("z", [P, NT, D]), sb("base", [P, NT, D])
    hT, qf = sb("hT", [P, NT * P]), sb("qf", [P, NT * P])
    kv = sb("kv", [P, NT, 2 * P + 1])
    q1, qe, ke = sb("q1", [P, 2, 512]), sb("qe", [P, 2, 512]), sb("ke", [P, 2, GT, P])
    KV, KS = sb("KV", [P, B, P]), sb("KS", [P, B, P])
    den, rec = sb("den", [P, 2, 512]), sb("rec", [P, 2, 512])
    attT, h1T = sb("attT", [P, NT * P]), sb("h1T", [P, NT * P])
    ln0 = layernorm_steps(c, st, "la0", c.x, z)
    lna = layernorm_steps(c, st, "laa", base, z)
    lnb = layernorm_steps(c, st, "lab", base, z)
    lnf = layernorm_steps(c, st, "laf", base, z)
    mlp = mlp_buffers(c, st, "la", W1, colB[:, 2:6], W2, h1T)
    s = {n: c.sem("la_" + n) for n in (
        "wA", "wB", "wF", "ones", "prepA", "prepB", "tr", "hT", "g0", "base1", "q", "q1", "qe", "qf",
        "kvp", "kv1", "ke", "kf", "s", "KV", "num", "dn", "den", "rec", "att", "wo", "y1",
        "tr2", "h1T", "g1", "base2", "f0", "f1", "f2", "f3", "f4")}
    ps = c.ps
    NA, NB = 8, 5

    def token(t):
        return slice(t * P, (t + 1) * P)

    def kslice(g):
        return kv[:, GT * g:GT * g + GT, 0:P]

    def add1(e, l, g):
        e.wait_ge(s["wo"], l * NG + g + 1)
        e.wait_ge(s["base1"], l * NG + g + 1)
        e.tensor_tensor(grp(base, g), grp(base, g), bank4(c, 4 + g % 2), ALU.add).then_inc(s["y1"], 1)
        e.wait_ge(s["y1"], l * NG + g + 1)

    with nc.Block() as block:
        @block.sync
        def _(e):
            def load_a(l):
                d = c.dram
                e.dma_start(Wq[:, :], d["la_Wq"][l]).then_inc(s["wA"], 16)
                e.dma_start(Wkv[:, :], d["la_Wkv"][l]).then_inc(s["wA"], 16)
                e.dma_start(Wo[:, :], d["la_Wo"][l]).then_inc(s["wA"], 16)
                e.dma_start(colA[:, :], d["la_colA"][l]).then_inc(s["wA"], 16)
                e.dma_start(rowA[:, :, :], d["la_rowA"][l].partition_broadcast(P)).then_inc(s["wA"], 16)

            def load_b(l):
                d = c.dram
                e.dma_start(W1[:, :], d["la_W1"][l]).then_inc(s["wB"], 16)
                e.dma_start(W2[:, :, :], d["la_W2"][l].rearrange("(f p) d -> p f d", p=P)).then_inc(s["wB"], 16)
                e.dma_start(colB[:, :], d["la_colB"][l]).then_inc(s["wB"], 16)
                e.dma_start(rowB[:, :, :], d["la_rowB"][l].partition_broadcast(P)).then_inc(s["wB"], 16)

            load_a(0)
            load_b(0)
            e.dma_start(rowF[:, :, :], c.dram["la_rowF"].partition_broadcast(P)).then_inc(s["wF"], 16)
            with e.Fori(0, NL1 - 1) as l:
                e.wait_ge(s["y1"], l * NG + NG)
                load_a(l + 1)
                e.wait_ge(mlp["out"], l * NG + NG + 2)
                load_b(l + 1)

        @block.gpsimd
        def _(e):
            e.memset(kv[:, :, 2 * P:2 * P + 1], 1.0).then_inc(s["ones"], 1)
            for g in range(NG):
                ln_rstd(c, e, ln0, g)
            with e.Fori(0, NL1) as l:
                e.wait_ge(s["wA"], l * 80 + 80)
                e.tensor_tensor(sumA[:, :], rowA[:, 1, :], rowA[:, 2, :], ALU.add).then_inc(s["prepA"], 1)
                for g in range(NG):
                    e.wait_ge(s["hT"], l * NG + g + 1)
                    e.tensor_tensor(grp(base, g), grp(z, g), rows4(rowA[:, 0, :]), ALU.mult).then_inc(s["g0"], 1)
                    e.wait_ge(s["g0"], l * NG + g + 1)
                    e.wait_ge(s["prepA"], l * 3 + 1)
                    e.tensor_tensor(grp(base, g), grp(base, g), rows4(sumA[:, :]), ALU.add).then_inc(s["base1"], 1)
                e.wait_ge(s["wB"], l * 64 + 64)
                e.tensor_tensor(sumB[:, :], rowB[:, 1, :], rowB[:, 2, :], ALU.add).then_inc(s["prepB"], 1)
                for g in range(NG):
                    ln_rstd(c, e, lna, g, l)
                for g in range(NG):
                    e.wait_ge(s["h1T"], l * NG + g + 5)
                    e.tensor_tensor(grp(base, g), grp(z, g), rows4(rowB[:, 0, :]), ALU.mult).then_inc(s["g1"], 1)
                    e.wait_ge(s["g1"], l * NG + g + 1)
                    e.wait_ge(s["prepB"], l + 1)
                    e.tensor_tensor(grp(base, g), grp(base, g), rows4(sumB[:, :]), ALU.add).then_inc(s["base2"], 1)
                for g in range(NG):
                    ln_rstd(c, e, lnb, g, l)
            for g in range(NG):
                ln_rstd(c, e, lnf, g)

        @block.vector
        def _(e):
            e.sem_inc(mlp["out"], 2)
            for g in range(NG):
                ln_stats(c, e, ln0, g)
                if g:
                    ln_apply(c, e, ln0, g - 1)
            ln_apply(c, e, ln0, NG - 1)
            e.wait_ge(ln0["out"], NT)
            e.sem_inc(lnb["out"], NT)

            def phi_q(l, g):
                e.wait_ge(s["qe"], l * NG + g + 1)
                e.scalar_tensor_tensor(qf[:, g * 512:(g + 1) * 512], qe[:, g % 2, :], 1.0, q1[:, g % 2, :],
                                       ALU.min, ALU.max).then_inc(s["qf"], 1)

            def phi_k(l, g):
                e.wait_ge(s["ke"], l * NG + g + 1)
                e.scalar_tensor_tensor(kslice(g), ke[:, g % 2], 1.0, kslice(g), ALU.min, ALU.max).then_inc(s["kf"], 1)

            with e.Fori(0, NL1) as l:
                e.wait_ge(s["wA"], l * 80 + 80)
                e.tensor_scalar(bq1[:, :], colA[:, 2:3], 1.0, None, ALU.add).then_inc(s["prepA"], 1)
                e.tensor_scalar(rowA[:, 3, :], rowA[:, 3, :], 1.0, None, ALU.add).then_inc(s["prepA"], 1)
                e.wait_ge(s["prepA"], l * 3 + 3)
                bkv = rowA[:, 3:5, :].rearrange("p a n -> p (a n)").unsqueeze(1).broadcast_to([P, 2, 2 * P])
                for g in range(NG):
                    e.wait_ge(s["q"], l * NG + g + 1)
                    if g >= 2:
                        e.wait_ge(s["qf"], l * NG + g - 1)
                    e.tensor_scalar(q1[:, g % 2, :], ps[:, g % 2, :], bq1[:, 0:1], None, ALU.add).then_inc(s["q1"], 1)
                    for k in range(2):
                        e.wait_ge(s["kvp"], l * 8 + 2 * g + k + 1)
                        e.tensor_tensor(kv[:, GT * g + 2 * k:GT * g + 2 * k + 2, 0:2 * P],
                                        ps[:, 2 + k, :].rearrange("p (t n) -> p t n", t=2), bkv, ALU.add)\
                            .then_inc(s["kv1"], 1)
                    if g:
                        phi_q(l, g - 1)
                        phi_k(l, g - 1)
                phi_q(l, NG - 1)
                phi_k(l, NG - 1)
                for b in range(B):
                    e.wait_ge(s["s"], l * B + b + 1)
                    e.tensor_tensor(KV[:, b, :], ps[:, 4 + b, 0:P], c.blk, ALU.mult)
                    e.tensor_scalar(KS[:, b, :], c.blk, ps[:, 4 + b, P:P + 1], None, ALU.mult).then_inc(s["KV"], 1)
                for g in range(NG):
                    e.wait_ge(s["dn"], l * NG + g + 1)
                    e.tensor_scalar(den[:, g % 2, :], ps[:, 2 + g % 2, :], 1e-6, None, ALU.add).then_inc(s["den"], 1)
                    e.wait_ge(s["den"], l * NG + g + 1)
                    e.reciprocal(rec[:, g % 2, :], den[:, g % 2, :]).then_inc(s["rec"], 1)
                    e.wait_ge(s["rec"], l * NG + g + 1)
                    e.tensor_tensor(attT[:, g * 512:(g + 1) * 512], ps[:, g % 2, :], rec[:, g % 2, :], ALU.mult)\
                        .then_inc(s["att"], 1)
                    if g:
                        add1(e, l, g - 1)
                        ln_stats(c, e, lna, g - 1, l)
                    if g >= 2:
                        ln_apply(c, e, lna, g - 2, l)
                add1(e, l, NG - 1)
                ln_stats(c, e, lna, NG - 1, l)
                ln_apply(c, e, lna, NG - 2, l)
                ln_apply(c, e, lna, NG - 1, l)
                for g in range(NG):
                    e.wait_ge(mlp["down"], l * NG + g + 1)
                    e.wait_ge(s["base2"], l * NG + g + 1)
                    e.tensor_tensor(grp(base, g), grp(base, g), bank4(c, 4 + g % 2), ALU.add).then_inc(mlp["out"], 1)
                    e.wait_ge(mlp["out"], l * NG + g + 3)
                    ln_stats(c, e, lnb, g, l)
                    if g:
                        ln_apply(c, e, lnb, g - 1, l)
                ln_apply(c, e, lnb, NG - 1, l)
            e.wait_ge(s["wF"], 16)
            e.wait_ge(lnb["out"], NT * NL1 + NT)
            for g in range(NG):
                e.tensor_tensor(grp(base, g), grp(z, g), rows4(rowF[:, 0, :]), ALU.mult).then_inc(s["f0"], 1)
                e.wait_ge(s["f0"], g + 1)
                e.tensor_tensor(grp(base, g), grp(base, g), rows4(rowF[:, 1, :]), ALU.add).then_inc(s["f1"], 1)
                e.wait_ge(s["f1"], g + 1)
                ln_stats(c, e, lnf, g)
                if g:
                    ln_apply(c, e, lnf, g - 1)
            ln_apply(c, e, lnf, NG - 1)
            for g in range(NG):
                e.wait_ge(lnf["out"], GT * g + GT)
                e.tensor_tensor(grp(z, g), grp(z, g), rows4(rowF[:, 2, :]), ALU.mult).then_inc(s["f2"], 1)
                e.wait_ge(s["f2"], g + 1)
                e.tensor_tensor(grp(z, g), grp(z, g), rows4(rowF[:, 3, :]), ALU.add).then_inc(s["f3"], 1)
                e.wait_ge(s["f3"], g + 1)
                e.tensor_tensor(grp(c.x, g), grp(c.x, g), grp(z, g), ALU.add).then_inc(s["f4"], 1)

        @block.tensor
        def _(e):
            e.wait_ge(s["ones"], 1)
            with e.Fori(0, NL1) as l:
                n = l * NG

                def turn(g):
                    e.wait_ge(lnb["out"], l * NT + GT * g + GT)
                    if g == 0:
                        e.wait_ge(s["h1T"], n + 4)
                    if g >= 2:
                        e.wait_ge(s["hT"], n + g - 1)
                    transpose_group(c, e, z, 6 + g % 2, g).then_inc(s["tr"], 1)

                def qkv(g):
                    e.wait_ge(s["hT"], n + g + 1)
                    if g >= 2:
                        e.wait_ge(s["q1"], n + g - 1)
                    e.matmul(ps[:, g % 2, :], Wq[:, :], hT[:, g * 512:(g + 1) * 512], start=True, stop=True)\
                        .then_inc(s["q"], 1)
                    for k in range(2):
                        if g:
                            e.wait_ge(s["kv1"], l * 8 + 2 * g + k - 1)
                        for t in range(2):
                            ins = e.matmul(ps[:, 2 + k, t * 256:(t + 1) * 256], hT[:, token(GT * g + 2 * k + t)],
                                           Wkv[:, :], start=True, stop=True)
                        ins.then_inc(s["kvp"], 1)

                def state(b):
                    e.wait_ge(s["kf"], n + 2 * b + 2)
                    for t in range(TPB):
                        ins = e.matmul(ps[:, 4 + b, 0:P + 1], kv[:, b * TPB + t, 0:P], kv[:, b * TPB + t, P:2 * P + 1],
                                       start=(t == 0), stop=(t == TPB - 1))
                    ins.then_inc(s["s"], 1)

                def attend(g):
                    b = g // (NG // B)
                    e.wait_ge(s["KV"], l * B + b + 1)
                    e.wait_ge(s["qf"], n + g + 1)
                    if g < 2:
                        e.wait_ge(s["q1"], n + 4)
                        e.wait_ge(s["kv1"], l * 8 + 8)
                    else:
                        e.wait_ge(s["att"], n + g - 1)
                    e.matmul(ps[:, g % 2, :], KV[:, b, :], qf[:, g * 512:(g + 1) * 512], start=True, stop=True)
                    e.matmul(ps[:, 2 + g % 2, :], KS[:, b, :], qf[:, g * 512:(g + 1) * 512], start=True, stop=True)\
                        .then_inc(s["dn"], 1)

                def project(g):
                    e.wait_ge(s["att"], n + g + 1)
                    if g >= 2:
                        e.wait_ge(s["y1"], n + g - 1)
                    else:
                        e.wait_ge(s["KV"], l * B + 2)
                    for t in range(GT):
                        ins = e.matmul(ps[:, 4 + g % 2, t * P:(t + 1) * P], attT[:, token(GT * g + t)], Wo[:, :],
                                       start=True, stop=True)
                    ins.then_inc(s["wo"], 1)

                def turn2(g):
                    e.wait_ge(lna["out"], l * NT + GT * g + GT)
                    if g >= 2:
                        e.wait_ge(s["h1T"], n + g + 3)
                    transpose_group(c, e, z, 6 + g % 2, g).then_inc(s["tr2"], 1)

                def up(g):
                    e.wait_ge(s["h1T"], n + g + 5)
                    mlp_up(c, e, mlp, g, n + g)

                def down(g):
                    if g < 2:
                        e.wait_ge(s["y1"], n + 4)
                    mlp_down(c, e, mlp, g, n + g)

                e.wait_ge(s["wA"], l * 80 + 80)
                turn(0)
                turn(1)
                qkv(0)
                qkv(1)
                turn(2)
                turn(3)
                qkv(2)
                state(0)
                qkv(3)
                state(1)
                attend(0)
                attend(1)
                project(0)
                attend(2)
                project(1)
                attend(3)
                project(2)
                project(3)
                e.wait_ge(s["wB"], l * 64 + 64)
                turn2(0)
                turn2(1)
                up(0)
                turn2(2)
                up(1)
                down(0)
                turn2(3)
                up(2)
                down(1)
                up(3)
                down(2)
                down(3)

        @block.scalar
        def _(e):
            mlp_credits(e, mlp)
            e.sem_inc(s["h1T"], 4)
            with e.Fori(0, NL1) as l:
                n = l * NG

                def take(g):
                    e.wait_ge(s["tr"], n + g + 1)
                    e.activation(hT[:, g * 512:(g + 1) * 512], ps[:, 6 + g % 2, :], ACT.Identity,
                                 bias=colA[:, 1:2], scale=colA[:, 0:1]).then_inc(s["hT"], 1)

                def exps(g):
                    e.wait_ge(s["q1"], n + g + 1)
                    e.activation(qe[:, g % 2, :], q1[:, g % 2, :], ACT.Exp, bias=c.neg_one[:, 0:1]).then_inc(s["qe"], 1)
                    e.wait_ge(s["kv1"], l * 8 + 2 * g + 2)
                    e.activation(ke[:, g % 2], kslice(g), ACT.Exp, bias=c.neg_one[:, 0:1]).then_inc(s["ke"], 1)

                e.wait_ge(s["wA"], l * 80 + 80)
                take(0)
                take(1)
                exps(0)
                exps(1)
                take(2)
                take(3)
                exps(2)
                exps(3)
                e.wait_ge(s["wB"], l * 64 + 64)
                for g in range(NG):
                    e.wait_ge(s["tr2"], n + g + 1)
                    e.activation(h1T[:, g * 512:(g + 1) * 512], ps[:, 6 + g % 2, :], ACT.Identity,
                                 bias=colB[:, 1:2], scale=colB[:, 0:1]).then_inc(s["h1T"], 1)
                    if g:
                        mlp_act(c, e, mlp, g - 1, n + g - 1)
                mlp_act(c, e, mlp, NG - 1, n + NG - 1)


HB, DH = 16, 8
HQ = 4
PQ = [0, 0, 1, 1, 0, 2, 1, 2]
PK = [0, 1, 0, 1, 2, 0, 2, 1]


def spread_matrices():
    m = np.zeros((P, 2, 3, HB // 2, P), np.float32)
    for j in range(HB // 2):
        for hp in range(2):
            for k in range(8):
                for d in range(DH):
                    f, r = (2 * j + hp) * DH + d, hp * 64 + k * DH + d
                    m[f, 0, PQ[k], j, r] = 1.0
                    m[f, 1, PK[k], j, r] = 1.0
    return m.reshape(P, -1)


def query_attention_project(c, st, a, parts, v):
    nc = c.nc

    def sb(name, shape, dt=F32):
        return st.enter_context(nc.sbuf_tensor("qp_" + name, shape, dt))

    aT, W, cols, vrow = sb("aT", [P, NT * P]), sb("W", [P, 3, P]), sb("cols", [P, 2]), sb("vrow", [P, P])
    xf, r1 = sb("xf", [P, 2, 512]), sb("r1", [P, 2, 512])
    ln = layernorm_steps(c, st, "qp", c.x, a)
    s = {n: c.sem("qp_" + n) for n in ("loaded", "turned", "aT", "qk", "xf", "p0", "r1", "p1", "p2", "vp", "v")}
    ps = c.ps
    with nc.Block() as block:
        @block.sync
        def _(e):
            e.dma_start(W[:, :, :], c.dram["qa_WT"].rearrange("p (a n) -> p a n", a=3)).then_inc(s["loaded"], 16)
            e.dma_start(cols[:, :], c.dram["qa_cols"]).then_inc(s["loaded"], 16)
            e.dma_start(vrow[:, :], c.dram["qa_vrow"].partition_broadcast(P)).then_inc(s["loaded"], 16)

        @block.gpsimd
        def _(e):
            for g in range(NG):
                ln_rstd(c, e, ln, g)

        @block.vector
        def _(e):
            for g in range(NG):
                ln_stats(c, e, ln, g)
                if g:
                    ln_apply(c, e, ln, g - 1)
            ln_apply(c, e, ln, NG - 1)
            e.wait_ge(s["loaded"], 48)
            for g in range(NG):
                for k in range(2):
                    m = 2 * g + k
                    e.wait_ge(s["qk"], m + 1)
                    if m >= 2:
                        e.wait_ge(s["p0"], m - 1)
                    e.tensor_scalar(xf[:, k, :], ps[:, k, :], cols[:, k:k + 1], DH ** -0.5 if k == 0 else 1.0,
                                    ALU.add, ALU.mult).then_inc(s["xf"], 1)
                for k in range(2):
                    m = 2 * g + k
                    e.wait_ge(s["p0"], m + 1)
                    e.tensor_tensor(r1[:, k, :], xf[:, k, :], parts[:, k, 0, g * 512:(g + 1) * 512], ALU.subtract)\
                        .then_inc(s["r1"], 1)
                for k in range(2):
                    m = 2 * g + k
                    e.wait_ge(s["p1"], m + 1)
                    e.tensor_tensor(parts[:, k, 2, g * 512:(g + 1) * 512], r1[:, k, :],
                                    parts[:, k, 1, g * 512:(g + 1) * 512], ALU.subtract).then_inc(s["p2"], 1)
                e.wait_ge(s["vp"], g + 1)
                e.tensor_tensor(grp(v, g), bank4(c, 2 + g % 2), rows4(vrow[:, :]), ALU.add).then_inc(s["v"], 1)

        @block.tensor
        def _(e):
            for g in range(NG):
                e.wait_ge(ln["out"], GT * g + GT)
                if g >= 2:
                    e.wait_ge(s["aT"], g - 1)
                transpose_group(c, e, a, 6 + g % 2, g).then_inc(s["turned"], 1)
            e.wait_ge(s["loaded"], 48)
            for g in range(NG):
                e.wait_ge(s["aT"], g + 1)
                for k in range(2):
                    if g:
                        e.wait_ge(s["xf"], 2 * g + k - 1)
                    e.matmul(ps[:, k, :], W[:, k, :], aT[:, g * 512:(g + 1) * 512], start=True, stop=True)\
                        .then_inc(s["qk"], 1)
                if g >= 2:
                    e.wait_ge(s["v"], g - 1)
                for t in range(GT):
                    ins = e.matmul(ps[:, 2 + g % 2, t * P:(t + 1) * P], aT[:, (GT * g + t) * P:(GT * g + t + 1) * P],
                                   W[:, 2, :], start=True, stop=True)
                ins.then_inc(s["vp"], 1)

        @block.scalar
        def _(e):
            for g in range(NG):
                e.wait_ge(s["turned"], g + 1)
                e.activation(aT[:, g * 512:(g + 1) * 512], ps[:, 6 + g % 2, :], ACT.Copy).then_inc(s["aT"], 1)
            for g in range(NG):
                for k in range(2):
                    e.wait_ge(s["xf"], 2 * g + k + 1)
                    e.activation(parts[:, k, 0, g * 512:(g + 1) * 512], xf[:, k, :], ACT.Copy).then_inc(s["p0"], 1)
                for k in range(2):
                    e.wait_ge(s["r1"], 2 * g + k + 1)
                    e.activation(parts[:, k, 1, g * 512:(g + 1) * 512], r1[:, k, :], ACT.Copy).then_inc(s["p1"], 1)


def query_attention_core(c, st, parts, v, post):
    nc = c.nc

    def sb(name, shape, dt=F32):
        return st.enter_context(nc.sbuf_tensor("qc_" + name, shape, dt))

    NR = 2 * 3 * (HB // 2) * P
    spread = sb("spread", [P, NR], BF16)
    stage = sb("stage", [P, NR // 4])
    qs, ks = sb("qs", [P, 2, T], BF16), sb("ks", [P, 2, T], BF16)
    E = sb("E", [P, 2, HQ, T])
    vz = sb("vz", [P, 2, HQ, 32])
    mx, zs, rz = sb("mx", [P, 8]), sb("zs", [P, 8]), sb("rz", [P, 8])
    s = {n: c.sem("qc_" + n) for n in (
        "loaded", "cast", "vz0", "sp", "stack", "sc", "mx", "E", "rz", "vz", "pv", "post")}
    ps = c.ps
    NIT, NU = B * HB // HQ, TPB * HQ

    with nc.Block() as block:
        @block.sync
        def _(e):
            for k in range(4):
                if k:
                    e.wait_ge(s["cast"], k)
                e.dma_start(stage[:, :], c.dram["spread"][:, k * NR // 4:(k + 1) * NR // 4]).then_inc(s["loaded"], 16)

        @block.gpsimd
        def _(e):
            e.memset(vz[:, :, :, :], 0.0).then_inc(s["vz0"], 1)

        @block.scalar
        def _(e):
            e.sem_inc(s["post"], 1)
            e.sem_inc(s["E"], 2)
            with e.Fori(0, NIT) as it:
                for k in range(8):
                    dst = (qs, ks)[k // 4]
                    e.wait_ge(s["sp"], it * 8 + k + 1)
                    e.activation(dst[:, k // 2 % 2, (k % 2) * 512:(k % 2) * 512 + 512], ps[:, 6 + k % 2, :], ACT.Copy)\
                        .then_inc(s["stack"], 1)
                for u in range(NU):
                    e.wait_ge(s["mx"], it * NU + u + 1)
                    if u >= 2 * HQ and u % HQ == 0:
                        e.wait_ge(s["pv"], it * TPB + u // HQ - 1)
                    e.activation(E[:, u // HQ % 2, u % HQ, :], ps[:, 2 * (u % 2):2 * (u % 2) + 2, :].rearrange("p a n -> p (a n)"),
                                 ACT.Exp, bias=mx[:, u % 8:u % 8 + 1], accum_out=zs[:, u % 8:u % 8 + 1]).then_inc(s["E"], 1)
                e.wait_ge(s["pv"], it * TPB + TPB)
                hq, b = it // 2, it % 2
                e.activation(post[:, bass.ds(hq * 2 + b, 1), :].rearrange("p a t -> p (a t)"),
                             ps[:, 4:6, :].rearrange("p a n -> p (a n)"), ACT.Copy).then_inc(s["post"], 1)

        @block.vector
        def _(e):
            for k in range(4):
                e.wait_ge(s["loaded"], 16 * k + 16)
                e.tensor_copy(spread[:, k * NR // 4:(k + 1) * NR // 4], stage[:, :]).then_inc(s["cast"], 1)
            e.wait_ge(s["vz0"], 1)
            with e.Fori(0, NIT) as it:
                hq, b = it // 2, it % 2

                def weight(u):
                    n = it * NU + u
                    e.wait_ge(s["E"], n + 3)
                    e.reciprocal(rz[:, u % 8:u % 8 + 1], zs[:, u % 8:u % 8 + 1]).then_inc(s["rz"], 1)
                    e.wait_ge(s["rz"], n + 1)
                    if u >= 2 * HQ and u % HQ == 0:
                        e.wait_ge(s["pv"], it * TPB + u // HQ - 1)
                    t, h = u // HQ, u % HQ
                    e.tensor_scalar(vz[:, t % 2, h, 0:DH],
                                    v[:, bass.ds(b * TPB + t, 1), bass.ds(hq * (HQ * DH) + h * DH, DH)].rearrange("p a d -> p (a d)"),
                                    rz[:, u % 8:u % 8 + 1], None, ALU.mult).then_inc(s["vz"], 1)

                for u in range(NU):
                    e.wait_ge(s["sc"], it * NU + u + 1)
                    e.tensor_reduce(mx[:, u % 8:u % 8 + 1], ps[:, 2 * (u % 2):2 * (u % 2) + 2, :].rearrange("p a n -> p (a n)"),
                                    AX, ALU.max, negate=True).then_inc(s["mx"], 1)
                    if u:
                        weight(u - 1)
                weight(NU - 1)

        @block.tensor
        def _(e):
            e.wait_ge(s["cast"], 4)
            with e.Fori(0, NIT) as it:
                hq, b = it // 2, it % 2
                for k in range(8):
                    if k >= 2:
                        e.wait_ge(s["stack"], it * 8 + k - 1)
                    for p in range(3):
                        row = ((k // 4) * 3 + p) * (HB // 2) * P + (k // 2 % 2) * P
                        ins = e.matmul(ps[:, 6 + k % 2, :], spread[:, bass.ds(hq * (2 * P) + row, P)],
                                       parts[:, k // 4, p, bass.ds(b * T + (k % 2) * 512, 512)],
                                       start=(p == 0), stop=(p == 2))
                    ins.then_inc(s["sp"], 1)
                e.wait_ge(s["stack"], it * 8 + 8)

                def scores(u):
                    t, h = u // HQ, u % HQ
                    e.wait_ge(s["E"], it * NU + u + 1)
                    r = slice(64 * (h % 2), 64 * (h % 2) + 64)
                    for half in range(2):
                        ins = e.matmul(ps[:, 2 * (u % 2) + half, :], ks[r, h // 2, t * P:(t + 1) * P],
                                       qs[r, h // 2, half * 512:(half + 1) * 512], start=True, stop=True)
                    ins.then_inc(s["sc"], 1)

                def weigh(t):
                    e.wait_ge(s["vz"], it * NU + HQ * t + HQ)
                    if t == 0:
                        e.wait_ge(s["post"], it + 1)
                    for half in range(2):
                        for h in range(HQ):
                            ins = e.matmul(ps[32 * h:32 * h + 32, 4 + half, :], vz[:, t % 2, h, :],
                                           E[:, t % 2, h, half * 512:(half + 1) * 512],
                                           start=(t == 0), stop=(t == TPB - 1))
                    ins.then_inc(s["pv"], 1)

                for u in range(NU):
                    scores(u)
                    if u >= HQ + 2 and (u - 2) % HQ == 0:
                        weigh((u - 2) // HQ - 1)
                weigh(TPB - 1)


def query_attention_finish(c, st, a, post):
    nc = c.nc

    def sb(name, shape):
        return st.enter_context(nc.sbuf_tensor("qf_" + name, shape, F32))

    Wo, W1, W2 = sb("Wo", [P, HB // HQ, D]), sb("W1", [P, 512]), sb("W2", [P, 4, D])
    cols, rows, sumr = sb("cols", [P, 6]), sb("rows", [P, 6, P]), sb("sum", [P, P])
    z, h1T = sb("z", [P, NT, D]), sb("h1T", [P, NT * P])
    lna = layernorm_steps(c, st, "qfa", a, z)
    lnb = layernorm_steps(c, st, "qfb", a, z)
    mlp = mlp_buffers(c, st, "qf", W1, cols[:, 2:6], W2, h1T)
    s = {n: c.sem("qf_" + n) for n in (
        "loaded", "wo", "sum", "gelu", "o", "based", "y1", "tr", "h1T", "g1", "base2", "o1", "o2", "o3")}
    ps = c.ps
    NH = HB // HQ

    def add1(e, g):
        e.wait_ge(s["o"], g + 1)
        e.wait_ge(s["based"], g + 1)
        e.tensor_tensor(grp(a, g), grp(a, g), bank4(c, 4 + g % 2), ALU.add).then_inc(s["y1"], 1)
        e.wait_ge(s["y1"], g + 1)

    with nc.Block() as block:
        @block.sync
        def _(e):
            d = c.dram
            e.dma_start(Wo[:, :, :], d["qa_WoT"]).then_inc(s["loaded"], 16)
            e.dma_start(W1[:, :], d["qa_W1T"]).then_inc(s["loaded"], 16)
            e.dma_start(W2[:, :, :], d["qa_W2T"].rearrange("(f p) d -> p f d", p=P)).then_inc(s["loaded"], 16)
            e.dma_start(cols[:, :], d["qa_mcols"]).then_inc(s["loaded"], 16)
            e.dma_start(rows[:, :, :], d["qa_rows"].partition_broadcast(P)).then_inc(s["loaded"], 16)

        @block.gpsimd
        def _(e):
            e.wait_ge(s["loaded"], 80)
            e.tensor_tensor(sumr[:, :], rows[:, 2, :], rows[:, 3, :], ALU.add).then_inc(s["sum"], 1)
            for g in range(NG):
                e.tensor_tensor(grp(a, g), grp(a, g), rows4(rows[:, 0, :]), ALU.add).then_inc(s["based"], 1)
            for g in range(NG):
                ln_rstd(c, e, lna, g)
            e.wait_ge(s["sum"], 1)
            for g in range(NG):
                e.wait_ge(lna["out"], GT * g + GT)
                e.tensor_tensor(grp(a, g), grp(z, g), rows4(rows[:, 1, :]), ALU.mult).then_inc(s["g1"], 1)
                e.wait_ge(s["g1"], g + 1)
                e.tensor_tensor(grp(a, g), grp(a, g), rows4(sumr[:, :]), ALU.add).then_inc(s["base2"], 1)
            for g in range(NG):
                ln_rstd(c, e, lnb, g)

        @block.vector
        def _(e):
            e.sem_inc(mlp["out"], 2)
            e.wait_ge(s["loaded"], 80)
            e.tensor_scalar(Wo[:, :, :], Wo[:, :, :], T ** -0.5, None, ALU.mult).then_inc(s["wo"], 1)
            for g in range(NG):
                add1(e, g)
                ln_stats(c, e, lna, g)
                if g:
                    ln_apply(c, e, lna, g - 1)
            ln_apply(c, e, lna, NG - 1)
            for g in range(NG):
                e.wait_ge(mlp["down"], g + 1)
                e.wait_ge(s["base2"], g + 1)
                e.tensor_tensor(grp(a, g), grp(a, g), bank4(c, 4 + g % 2), ALU.add).then_inc(mlp["out"], 1)
                e.wait_ge(mlp["out"], g + 3)
                ln_stats(c, e, lnb, g)
                if g:
                    ln_apply(c, e, lnb, g - 1)
            ln_apply(c, e, lnb, NG - 1)
            for g in range(NG):
                e.wait_ge(lnb["out"], GT * g + GT)
                e.tensor_tensor(grp(z, g), grp(z, g), rows4(rows[:, 4, :]), ALU.mult).then_inc(s["o1"], 1)
                e.wait_ge(s["o1"], g + 1)
                e.tensor_tensor(grp(z, g), grp(z, g), rows4(rows[:, 5, :]), ALU.add).then_inc(s["o2"], 1)
                e.wait_ge(s["o2"], g + 1)
                e.tensor_tensor(grp(c.x, g), grp(c.x, g), grp(z, g), ALU.add).then_inc(s["o3"], 1)

        @block.tensor
        def _(e):
            e.wait_ge(s["wo"], 1)
            for g in range(NG):
                if g >= 2:
                    e.wait_ge(s["y1"], g - 1)
                b = g // (NG // B)
                e.wait_ge(s["gelu"], NH * (b + 1))
                for t in range(GT):
                    tok = ((g % (NG // B)) * GT + t) * P
                    for h in range(NH):
                        ins = e.matmul(ps[:, 4 + g % 2, t * P:(t + 1) * P], post[:, 2 * h + b, tok:tok + P], Wo[:, h, :],
                                       start=(h == 0), stop=(h == NH - 1))
                ins.then_inc(s["o"], 1)
            e.wait_ge(s["y1"], NG)
            for g in range(NG):
                e.wait_ge(lna["out"], GT * g + GT)
                if g >= 2:
                    e.wait_ge(s["h1T"], g - 1)
                transpose_group(c, e, z, 6 + g % 2, g).then_inc(s["tr"], 1)
                e.wait_ge(s["h1T"], g + 1)
                mlp_up(c, e, mlp, g, g)
                if g:
                    mlp_down(c, e, mlp, g - 1, g - 1)
            mlp_down(c, e, mlp, NG - 1, NG - 1)

        @block.scalar
        def _(e):
            mlp_credits(e, mlp)
            for b in range(B):
                for h in range(NH):
                    e.activation(post[:, 2 * h + b, :], post[:, 2 * h + b, :], ACT.Gelu).then_inc(s["gelu"], 1)
            e.wait_ge(s["loaded"], 80)
            for g in range(NG):
                e.wait_ge(s["tr"], g + 1)
                e.activation(h1T[:, g * 512:(g + 1) * 512], ps[:, 6 + g % 2, :], ACT.Identity,
                             bias=cols[:, 1:2], scale=cols[:, 0:1]).then_inc(s["h1T"], 1)
                mlp_act(c, e, mlp, g, g)


def program(nc, dram, out, start=0, upto=99):
    with ExitStack() as ctx:
        c = Core(nc, ctx, dram)
        c.x = ctx.enter_context(nc.sbuf_tensor("x_res", [P, NT, D], F32))
        c.const = ctx.enter_context(nc.sbuf_tensor("const", [P, C_END], F32))
        c.neg_half = ctx.enter_context(nc.sbuf_tensor("neg_half", [P, 16], F32))
        c.neg_one = ctx.enter_context(nc.sbuf_tensor("neg_one", [P, 1], F32))
        c.ps = ctx.enter_context(nc.psum_tensor("ps", [P, 8, 512], F32))
        c.ident = c.const[:, C_ID:C_ID + P]
        c.utri = c.const[:, C_UTRI:C_UTRI + P]
        c.gt = c.const[:, C_GT:C_GT + P]
        c.ones = c.const[:, C_ONES:C_ONES + P]
        c.blk = c.const[:, C_BLK:C_BLK + P]
        c.m0 = c.const[:, C_M0:C_M0 + P]
        c.lv = c.const[:, C_LV:C_LV + 64 * len(LEVELS)].rearrange("p (l n) -> p l n", n=64)
        c.rst = c.const[:, C_RST:C_RST + 512]
        c.sel = c.const[:, C_SEL:C_SEL + 32]
        load_phase(c)
        c.end_phase()
        with ExitStack() as st:
          if start <= 1:
            x1 = st.enter_context(nc.sbuf_tensor("x1", [P, NT, D], F32))
            with ExitStack() as s1:
                nT = s1.enter_context(nc.sbuf_tensor("nT", [P, NT * P], F32))
                w, cols = gdn_weights(c, s1)
                with ExitStack() as s2:
                    gdn_norm_phase(c, s2, x1, nT, cols)
                    c.end_phase()
                with ExitStack() as s2:
                    gdn_phase(c, s2, x1, nT, w)
                    c.end_phase()
            if upto == 1:
                dump(c, x1)
            else:
                with ExitStack() as s1:
                    gdn_mlp_phase(c, s1, x1)
                    c.end_phase()
        if start <= 2 and upto >= 3:
            with ExitStack() as st:
                moe_phase(c, st, "moe0")
                c.end_phase()
        if start <= 3 and upto >= 4:
            with ExitStack() as st:
                ssm_phase(c, st)
                c.end_phase()
        if start <= 4 and upto >= 5:
            with ExitStack() as st:
                moe_phase(c, st, "moe1")
                c.end_phase()
        if start <= 5 and upto >= 6:
            with ExitStack() as st:
                linear_attention_phase(c, st)
                c.end_phase()
        wgu = ctx.enter_context(nc.sbuf_tensor("wgu", [P, 2 * FQ], F32))
        wd = ctx.enter_context(nc.sbuf_tensor("wd", [P, 3, D], F32))
        if upto >= 7:
            with ExitStack() as st:
                fp4_weight_phase(c, st, wgu, wd)
                c.end_phase()
        if start <= 6 and upto >= 7:
            with ExitStack() as st:
                fp4_phase(c, st, "fp0", wgu, wd)
                c.end_phase()
        if start <= 7 and upto >= 8:
            with ExitStack() as st:
                a = st.enter_context(nc.sbuf_tensor("qa_a", [P, NT, D], F32))
                with ExitStack() as s1:
                    post = st.enter_context(nc.sbuf_tensor("qa_post", [P, 2 * HB // HQ, T], F32))
                    parts = s1.enter_context(nc.sbuf_tensor("qa_parts", [P, 2, 3, NT * P], BF16))
                    v = s1.enter_context(nc.sbuf_tensor("qa_v", [P, NT, D], F32))
                    with ExitStack() as s2:
                        query_attention_project(c, s2, a, parts, v)
                        c.end_phase()
                    with ExitStack() as s2:
                        query_attention_core(c, s2, parts, v, post)
                        c.end_phase()
                with ExitStack() as s1:
                    query_attention_finish(c, s1, a, post)
                    c.end_phase()
        if start <= 8 and upto >= 9:
            with ExitStack() as st:
                fp4_phase(c, st, "fp1", wgu, wd)
                c.end_phase()
        store_phase(c, out)


def dump(c, t):
    d = c.sem("dump")
    with c.nc.Block() as block:
        @block.vector
        def _(e):
            e.tensor_copy(c.x[:, :, :], t[:, :, :]).then_inc(d, 1)


def gdn_weights(c, st):
    nc = c.nc
    w = {n: st.enter_context(nc.sbuf_tensor("gdn_w" + n, [P, H * P], F32)) for n in "qkv"}
    w["ba"] = st.enter_context(nc.sbuf_tensor("gdn_wba", [P, 16], F32))
    w["o"] = st.enter_context(nc.sbuf_tensor("gdn_wo", [P, H, P], F32))
    vec = st.enter_context(nc.sbuf_tensor("gdn_vec", [P, 2], F32))
    loaded = c.sem("gdn_w")
    with nc.Block() as block:
        @block.sync
        def _(e):
            for n in "qkv":
                e.dma_start(w[n][:, :], c.dram["L0a_W" + n]).then_inc(loaded, 16)
            e.dma_start(w["ba"][:, :], c.dram["L0a_Wba"]).then_inc(loaded, 16)
            e.dma_start(w["o"][:, :, :], c.dram["L0a_Wo"].rearrange("(h v) d -> v h d", v=P)).then_inc(loaded, 16)
            e.dma_start(vec[:, :], c.dram["L0a_ln1"]).then_inc(loaded, 16)
            e.wait_ge(loaded, 96)
    return w, dict(ln1_w=vec[:, 0:1], ln1_b=vec[:, 1:2])


def store_phase(c, out):
    stored = c.sem("stored")
    with c.nc.Block() as block:
        @block.sync
        def _(e):
            e.dma_start(out.rearrange("b (t p) d -> p (b t) d", p=P), c.x[:, :, :]).then_inc(stored, 16)
            e.wait_ge(stored, 16)


def layout(inputs):
    i = {k: np.asarray(v) for k, v in inputs.items()}
    f = lambda n: i[n]
    gin = np.concatenate([np.ones((1, D), np.float32), f("L1_attn_a_g2")[:-1]])
    bein = np.concatenate([np.zeros((1, D), np.float32), f("L1_attn_a_be2")[:-1]])
    qw, qb = f("L1_attn_b_in_proj_w"), f("L1_attn_b_in_proj_b")
    wo = np.zeros((HQ, 32, HB // HQ, D), np.float32)
    wo[:, 0:DH] = f("L1_attn_b_out_w").T.reshape(HB // HQ, HQ, DH, D).transpose(1, 2, 0, 3)
    wo = wo.reshape(P, HB // HQ, D)
    return {
        "consts": constants(),
        "x": f("L0_attn_a_x"),
        "L0a_Wq": f("L0_attn_a_Wq"), "L0a_Wk": f("L0_attn_a_Wk"), "L0a_Wv": f("L0_attn_a_Wv"),
        "L0a_Wba": np.concatenate([f("L0_attn_a_Wb"), f("L0_attn_a_Wa")], axis=1),
        "L0a_Wo": f("L0_attn_a_Wo"),
        "L0a_W1": f("L0_attn_a_W1"), "L0a_W2": f("L0_attn_a_W2"), "L0a_b2": f("L0_attn_a_b2"),
        "L0a_cols": np.concatenate([f("L0_attn_a_ln2_w")[:, None], f("L0_attn_a_ln2_b")[:, None],
                                    f("L0_attn_a_b1").reshape(4, P).T], axis=1),
        "moe_gateT": f("L0_ffn_gate_w").T, "moe_ebias": f("L0_ffn_e_bias"),
        "moe_w13": np.concatenate([f("L0_ffn_w1"), f("L0_ffn_w3")], axis=2), "moe_w2": f("L0_ffn_w2"),
        "ssm_BT": f("L0_attn_b_B_w").T, "ssm_CT": f("L0_attn_b_C_w").T,
        "ssm_loglam": f("L0_attn_b_log_lambda")[:, None],
        "ssm_cols": np.stack([f("L0_attn_b_ssm_norm_w"), f("L0_attn_b_D_skip"), f("L0_attn_b_ffn_norm_w")], axis=1),
        "ssm_W1T": f("L0_attn_b_w1").T, "ssm_W3T": f("L0_attn_b_w3").T, "ssm_W2T": f("L0_attn_b_w2").T,
        "fp4_gate": f("L1_ffn_w_gate"), "fp4_up": f("L1_ffn_w_up"), "fp4_down": f("L1_ffn_w_down"),
        "la_Wq": f("L1_attn_a_Wq"), "la_Wkv": np.concatenate([f("L1_attn_a_Wk"), f("L1_attn_a_Wv")], axis=2),
        "la_Wo": f("L1_attn_a_Wo"), "la_W1": f("L1_attn_a_W1"), "la_W2": f("L1_attn_a_W2"),
        "la_colA": np.stack([gin, bein, f("L1_attn_a_bq")], axis=2),
        "la_rowA": np.stack([gin, bein, f("L1_attn_a_bo"), f("L1_attn_a_bk"), f("L1_attn_a_bv")], axis=1),
        "la_colB": np.concatenate([f("L1_attn_a_g1")[:, :, None], f("L1_attn_a_be1")[:, :, None],
                                   f("L1_attn_a_c1").reshape(NL1, 4, P).transpose(0, 2, 1)], axis=2),
        "la_rowB": np.stack([f("L1_attn_a_g1"), f("L1_attn_a_be1"), f("L1_attn_a_c2")], axis=1),
        "la_rowF": np.stack([f("L1_attn_a_g2")[-1], f("L1_attn_a_be2")[-1], f("L1_attn_a_gf"), f("L1_attn_a_bef")]),
        "qa_WT": np.concatenate([qw[k * P:(k + 1) * P].T for k in range(3)], axis=1),
        "qa_cols": np.stack([qb[0:P], qb[P:2 * P]], axis=1), "qa_vrow": qb[2 * P:3 * P],
        "qa_WoT": wo, "qa_W1T": f("L1_attn_b_lin1_w").T, "qa_W2T": f("L1_attn_b_lin2_w").T,
        "qa_mcols": np.concatenate([f("L1_attn_b_ln1_g")[:, None], f("L1_attn_b_ln1_b")[:, None],
                                    f("L1_attn_b_lin1_b").reshape(4, P).T], axis=1),
        "qa_rows": np.stack([f("L1_attn_b_" + n) for n in ("out_b", "ln1_g", "ln1_b", "lin2_b", "ln2_g", "ln2_b")]),
        "spread": spread_matrices(),
        "L0a_ln1": np.stack([f("L0_attn_a_ln1_w"), f("L0_attn_a_ln1_b")], axis=1),
    }


START, UPTO = 0, 99


def kernel(**inputs):
    import concourse.bacc as _bacc
    from concourse.bass_utils import run_bass_kernel_spmd as _run

    nc = _bacc.Bacc("TRN2", target_bir_lowering=False, num_devices=1)
    arrays = {n: np.ascontiguousarray(a) for n, a in layout(inputs).items()}
    dram = {n: nc.dram_tensor("in_" + n, a.shape, mybir.dt.from_np(a.dtype), kind="ExternalInput").ap()
            for n, a in arrays.items()}
    out = nc.dram_tensor("out_0", (B, T, D), F32, kind="ExternalOutput").ap()
    program(nc, dram, out, START, UPTO)
    r = _run(nc, [{"in_" + n: a for n, a in arrays.items()}], core_ids=[0])
    return r.results[0]["out_0"]
```

```python
from contextlib import ExitStack

import numpy as np

import concourse.bass as bass
from concourse import mybir

F32 = mybir.dt.float32
BF16 = mybir.dt.bfloat16
ALU = mybir.AluOpType
ACT = mybir.ActivationFunctionType
AX = mybir.AxisListType.X

P = 128
B, T, D = 2, 1024, 128
NT = B * T // P
TPB = T // P
GT = 4
NG = NT // GT
H = 8
HG = 4
LEVELS = [2, 4, 8, 16, 32, 64]

C_ID, C_UTRI, C_GT, C_ONES, C_BLK, C_M0, C_LV = 0, 128, 256, 384, 512, 640, 768
C_RST = C_LV + 64 * len(LEVELS)
C_SEL = C_RST + 512
C_END = C_SEL + 32


def constants():
    i = np.arange(P)
    row, col = i[:, None], i[None, :]
    c = np.zeros((P, C_END), np.float32)
    c[:, C_ID:C_ID + P] = row == col
    c[:, C_UTRI:C_UTRI + P] = row <= col
    c[:, C_GT:C_GT + P] = row > col
    c[:, C_ONES:C_ONES + P] = 1.0
    c[:, C_BLK:C_BLK + P] = row // 8 == col // 8
    c[:, C_M0:C_M0 + P] = -1.0 * ((row % 2 == 0) & (col == row + 1))
    for n, s in enumerate(LEVELS):
        even = i[(i // s) % 2 == 0]
        c[:, C_LV + 64 * n:C_LV + 64 * n + 64] = row // s == even[None, :] // s + 1
    c[:, C_RST:C_RST + 512] = np.arange(512) % 32 != 0
    c[:, C_SEL:C_SEL + 32] = row % 32 == np.arange(32)[None, :]
    return c


class Core:

    def __init__(self, nc, ctx, dram):
        self.nc, self.ctx, self.dram = nc, ctx, dram
        self.n = 0
        self.held = []

    def sem(self, name):
        self.n += 1
        self.held.append(self.nc.alloc_semaphore(name=f"{name}_{self.n}"))
        return self.held[-1]

    def end_phase(self):
        self.nc.clear_and_free_semaphores(self.held)
        self.nc.all_engine_barrier()
        self.held = []


def layernorm_steps(c, st, name, src, dst, eps=1e-5, rms=False):
    k = dict(
        src=src, dst=dst, eps=eps, rms=rms,
        stats=st.enter_context(c.nc.sbuf_tensor(f"{name}_stats", [P, NT, 6], F32)),
        mv=st.enter_context(c.nc.sbuf_tensor(f"{name}_mv", [P, NT, 2], F32)),
        ve=st.enter_context(c.nc.sbuf_tensor(f"{name}_ve", [P, NT], F32)),
        m2=st.enter_context(c.nc.sbuf_tensor(f"{name}_m2", [P, NT], F32)),
        rstd=st.enter_context(c.nc.sbuf_tensor(f"{name}_rstd", [P, NT], F32)),
        stat=c.sem(name + "_stat"), mean=c.sem(name + "_mean"), sq=c.sem(name + "_sq"),
        var=c.sem(name + "_var"), rs=c.sem(name + "_rs"), out=c.sem(name + "_out"),
    )
    return k


def ln_stats(c, e, k, g, base=0):
    a, b = GT * g, GT * g + GT
    for t in range(a, b):
        e.bn_stats(k["stats"][:, t, :], k["src"][:, t, :]).then_inc(k["stat"], 1)
    e.wait_ge(k["stat"], base * NT + b)
    if not isinstance(base, int):
        e.nop(nofuse=True)
    for t in range(a, b):
        e.bn_aggr(k["mv"][:, t, :], k["stats"][:, t, :]).then_inc(k["mean"], 1)
    e.wait_ge(k["mean"], base * NT + b)
    mean, var, ve = k["mv"][:, a:b, 0], k["mv"][:, a:b, 1], k["ve"][:, a:b]
    if k["rms"]:
        m2 = k["m2"][:, a:b]
        e.tensor_tensor(m2, mean, mean, ALU.mult).then_inc(k["sq"], 1)
        e.wait_ge(k["sq"], base * NG + g + 1)
        e.scalar_tensor_tensor(ve, var, k["eps"], m2, ALU.add, ALU.add).then_inc(k["var"], 1)
    else:
        e.tensor_scalar(ve, var, k["eps"], None, ALU.add).then_inc(k["var"], 1)


def ln_rstd(c, e, k, g, base=0):
    e.wait_ge(k["var"], base * NG + g + 1)
    e.tensor_tensor(k["rstd"][:, GT * g:GT * g + GT], k["ve"][:, GT * g:GT * g + GT],
                    c.neg_half[:, 0:GT], ALU.pow).then_inc(k["rs"], 1)


def ln_apply(c, e, k, g, base=0, waits=()):
    e.wait_ge(k["rs"], base * NG + g + 1)
    for s, v in waits:
        e.wait_ge(s, v)
    for t in range(GT * g, GT * g + GT):
        r = k["rstd"][:, t:t + 1]
        if k["rms"]:
            e.tensor_scalar(k["dst"][:, t, :], k["src"][:, t, :], r, None, ALU.mult).then_inc(k["out"], 1)
        else:
            e.tensor_scalar(k["dst"][:, t, :], k["src"][:, t, :], k["mv"][:, t, 0:1], r,
                            ALU.subtract, ALU.mult).then_inc(k["out"], 1)


def transpose_group(c, e, src, bank, g):
    for t in range(GT):
        ins = e.transpose(c.ps[:, bank, t * P:(t + 1) * P], src[:, GT * g + t, :], c.ident)
    return ins


def load_phase(c):
    loaded = c.sem("loaded")
    with c.nc.Block() as block:
        @block.sync
        def _(e):
            e.dma_start(c.const[:, :], c.dram["consts"]).then_inc(loaded, 16)
            e.dma_start(c.x[:, :, :], c.dram["x"].rearrange("b (t p) d -> p (b t) d", p=P)).then_inc(loaded, 16)
            e.wait_ge(loaded, 32)

        @block.gpsimd
        def _(e):
            e.memset(c.neg_half[:, :], -0.5)
            e.memset(c.neg_one[:, :], -1.0)


def gdn_norm_phase(c, st, x1, nT, w):
    zn = st.enter_context(c.nc.sbuf_tensor("gdn_zn", [P, NT, D], F32))
    ln0 = layernorm_steps(c, st, "ln0", c.x, x1)
    ln1 = layernorm_steps(c, st, "ln1", x1, zn)
    turned, taken, vectors, loaded = (c.sem(n) for n in ("turned", "taken", "vectors", "loaded"))
    with c.nc.Block() as block:
        @block.sync
        def _(e):
            e.dma_start(w["ln1"][:, :], c.dram["L0a_ln1"]).then_inc(vectors, 16)
            for n in "qkv":
                e.dma_start(w[n][:, :], c.dram["L0a_W" + n]).then_inc(loaded, 16)
            e.dma_start(w["ba"][:, :], c.dram["L0a_Wba"]).then_inc(loaded, 16)
            e.dma_start(w["o"][:, :, :], c.dram["L0a_Wo"].rearrange("(h v) d -> v h d", v=P)).then_inc(loaded, 16)
            e.wait_ge(loaded, 80)

        @block.vector
        def _(e):
            for g in range(NG):
                ln_stats(c, e, ln0, g)
            for g in range(NG):
                ln_apply(c, e, ln0, g)
            for g in range(NG):
                e.wait_ge(ln0["out"], GT * g + GT)
                ln_stats(c, e, ln1, g)
            for g in range(NG):
                ln_apply(c, e, ln1, g)

        @block.gpsimd
        def _(e):
            for k in (ln0, ln1):
                for g in range(NG):
                    ln_rstd(c, e, k, g)

        @block.tensor
        def _(e):
            for g in range(NG):
                e.wait_ge(ln1["out"], GT * g + GT)
                transpose_group(c, e, zn, g, g).then_inc(turned, 1)

        @block.scalar
        def _(e):
            e.wait_ge(vectors, 16)
            for g in range(NG):
                e.wait_ge(turned, g + 1)
                e.activation(nT[:, g * 512:(g + 1) * 512], c.ps[:, g, :], ACT.Identity,
                             bias=w["ln1"][:, 1:2], scale=w["ln1"][:, 0:1]).then_inc(taken, 1)


def gdn_phase(c, st, x1, nT, w):
    nc = c.nc

    def sb(name, shape):
        return st.enter_context(nc.sbuf_tensor("gdn_" + name, shape, F32))

    nTs = sb("nTs", [P, 2, P])
    raw = {n: sb("raw" + n, [P, H, P]) for n in "qkv"}
    sq = sb("sq", [P, 2, H, P])
    ss = sb("ss", [P, 2, H]); sse = sb("sse", [P, 2, H]); rn = sb("rn", [P, 2, H])
    Q = sb("Q", [P, 2, H, P]); K = sb("K", [P, 2, H, P]); Kb = sb("Kb", [P, 2, H, P])
    Kd = sb("Kd", [P, 2, H, P]); Bv = sb("Bv", [P, 2, H, P])
    z = sb("z", [P, 16]); zneg = sb("zneg", [P, 16]); ez = sb("ez", [P, 16]); lz = sb("lz", [P, 8])
    zmin = sb("zmin", [P, 8]); eb = sb("eb", [P, 8]); beta = sb("beta", [P, 2, 8]); la = sb("la", [P, 2, 8])
    laU = sb("laU", [P, 2, HG, P])
    G = sb("G", [P, 2, 3, 8])
    bG = sb("bG", [P, 2, 8])
    kT = sb("kT", [P, 2, HG, P]); kbT = sb("kbT", [P, 2, HG, P]); qT = sb("qT", [P, 2, HG, P])
    E = sb("E", [P, 2, HG, P]); Em = sb("Em", [P, 2, HG, P])
    AT = sb("AT", [P, 2, HG, P]); PT = sb("PT", [P, 2, HG, P]); A0 = sb("A0", [P, 2, HG, P])
    X = sb("X", [P, 2, HG, P]); XT = sb("XT", [P, 2, HG, P]); Pm = sb("Pm", [P, 2, HG, 64])
    R = sb("R", [P, 2, HG, P]); U = sb("U", [P, 2, HG, P]); oS = sb("oS", [P, 2, HG, P])
    O = sb("O", [P, 2, HG, P]); oT = sb("oT", [P, 2, HG, P])
    S = sb("S", [P, 2, H, P])

    s = {n: c.sem("gdn_" + n) for n in (
        "nts", "ba", "z", "ez_in", "ez", "lz", "zb", "beta", "la", "laU", "proj_q", "proj_k", "proj_v",
        "raw_q", "raw_k", "raw_v", "sq_q", "sq_k", "ss", "sse", "rn", "K", "Q", "Kb", "Kd", "Bv",
        "lst", "G", "bG", "tk", "tb", "tq", "kT", "kbT", "qT", "d", "E", "Em", "kk", "AT", "kq", "PT",
        "ks", "R", "qs", "oS", "A0", "XT0", "t0", "X0", "m1", "Pm", "m2", "X", "t", "XT",
        "u", "U", "pu", "O", "ku", "S", "to", "oT", "wo", "y")}
    ps = c.ps
    bT, bM, bL = (lambda p: p), (lambda p: 2 + p), (lambda p: 4 + p)
    NL = len(LEVELS)

    def hs(p):
        return slice(HG * p, HG * p + HG)

    def bank(k):
        return ps[:, k, :].rearrange("p (h n) -> p h n", h=HG)

    def even(t, p, l):
        return t[:, p].rearrange("p h (k two s) -> p (h k) two s", two=2, s=LEVELS[l])[:, :, 0, :]

    def even_h(t, p, h, l):
        return t[:, p, h].rearrange("p (k two s) -> p k two s", two=2, s=LEVELS[l])[:, :, 0, :]

    def merges(l):
        b = LEVELS[l]
        return [(slice(k, k + b), slice(k + b, k + 2 * b), k // 2) for k in range(0, P, 2 * b)] if b >= 32 else []

    def lv(n2, l, p):
        return n2 * (2 * NL) + 2 * l + p + 1

    def pe_proj(e, kind, nx, bx, half):
        bk = {"k": 6, "q": 7, "v": 6}[kind] if half == 0 else {"k": 7, "q": 6, "v": 7}[kind]
        e.matmul(ps[:, bk, :], nTs[:, bx, :], w[kind][:, half * 512:(half + 1) * 512],
                 start=True, stop=True).then_inc(s["proj_" + kind], 1)

    def pe_gates(e, nx, bx):
        e.wait_ge(s["nts"], nx + 1)
        e.matmul(ps[:, 6, 0:16], nTs[:, bx, :], w["ba"][:, :], start=True, stop=True).then_inc(s["ba"], 1)

    def pe_lstat(e, nx, bx):
        e.wait_ge(s["la"], nx + 1)
        for j, m in enumerate((c.utri, c.gt, c.ones)):
            ins = e.matmul(ps[:, 7, 8 * j:8 * j + 8], m, la[:, bx, :], start=True, stop=True)
        ins.then_inc(s["lst"], 1)

    def pe_v(e, nx, bx, half):
        e.wait_ge(s["raw_q"], 2 * nx + 2)
        pe_proj(e, "v", nx, bx, half)

    def pe_next(e, step, n2, bx, first=False):
        nx = n2 + 1 if not first else 0
        g = 2 * nx
        if step == 0:
            if not first:
                e.wait_ge(s["y"], n2 + 1)
            pe_gates(e, nx, bx)
        elif step == 1:
            e.wait_ge(s["z"], nx + 1)
            pe_proj(e, "k", nx, bx, 0)
            if not first:
                e.wait_ge(s["G"], nx)
            pe_proj(e, "k", nx, bx, 1)
        elif step == 2:
            e.wait_ge(s["raw_k"], g + 2)
            pe_proj(e, "q", nx, bx, 0)
            pe_proj(e, "q", nx, bx, 1)
        elif step == 3:
            for half in range(2):
                pe_v(e, nx, bx, half)
        elif step == 4:
            e.wait_ge(s["raw_v"], g + 2)
            pe_lstat(e, nx, bx)

    def pe_pair(e, n2, b):
        gs = [(p, 2 * n2 + p) for p in range(2)]
        for p, g in gs:
            e.wait_ge(s["K"], g + 1)
            e.wait_ge(s["S"], g + 3)
            for h in range(HG):
                ins = e.transpose(ps[:, bT(p), h * P:(h + 1) * P], K[:, b, HG * p + h, :], c.ident)
            ins.then_inc(s["tk"], 1)
        for p, g in gs:
            e.wait_ge(s["Kb"], g + 1)
            e.wait_ge(s["oT"], g + 1)
            for h in range(HG):
                ins = e.transpose(ps[:, bM(p), h * P:(h + 1) * P], Kb[:, b, HG * p + h, :], c.ident)
            ins.then_inc(s["tb"], 1)
        for p, g in gs:
            e.wait_ge(s["Q"], g + 1)
            e.wait_ge(s["O"], g + 1)
            for h in range(HG):
                ins = e.transpose(ps[:, bL(p), h * P:(h + 1) * P], Q[:, b, HG * p + h, :], c.ident)
            ins.then_inc(s["tq"], 1)
        for p, g in gs:
            e.wait_ge(s["laU"], g + 1)
            e.wait_ge(s["kT"], g + 1)
            e.matmul(ps[:, bT(p), :], c.gt, laU[:, p].rearrange("p h n -> p (h n)"),
                     start=True, stop=True).then_inc(s["d"], 1)
        for p, g in gs:
            e.wait_ge(s["kbT"], g + 1)
            for h in range(HG):
                ins = e.matmul(ps[:, bM(p), h * P:(h + 1) * P], kT[:, p, h, :], kbT[:, p, h, :],
                               start=True, stop=True)
            ins.then_inc(s["kk"], 1)
        for p, g in gs:
            e.wait_ge(s["qT"], g + 1)
            for h in range(HG):
                ins = e.matmul(ps[:, bL(p), h * P:(h + 1) * P], kT[:, p, h, :], qT[:, p, h, :],
                               start=True, stop=True)
            ins.then_inc(s["kq"], 1)
        pe_next(e, 0, n2, 1 - b)
        for p, g in gs:
            e.wait_ge(s["E"], g + 1)
            for h in range(HG):
                ins = e.matmul(ps[:, bT(p), h * P:(h + 1) * P], kT[:, p, h, :], S[:, b, HG * p + h, :],
                               start=True, stop=True)
            ins.then_inc(s["ks"], 1)
        for p, g in gs:
            e.wait_ge(s["AT"], g + 1)
            for h in range(HG):
                ins = e.matmul(ps[:, bM(p), h * P:(h + 1) * P], qT[:, p, h, :], S[:, b, HG * p + h, :],
                               start=True, stop=True)
            ins.then_inc(s["qs"], 1)
        for p, g in gs:
            e.wait_ge(s["XT0"], g + 1)
            e.wait_ge(s["R"], g + 1)
            for h in range(HG):
                ins = e.transpose(ps[:, bT(p), h * P:(h + 1) * P], XT[:, p, h, :], c.ident)
            ins.then_inc(s["t0"], 1)
        pe_next(e, 1, n2, 1 - b)
        for l in range(NL):
            for p, g in gs:
                if l == 0:
                    e.wait_ge(s["X0"], g + 1)
                    e.wait_ge(s["PT"], g + 1)
                else:
                    e.wait_ge(s["X"], lv(n2, l - 1, p))
                if LEVELS[l] >= 32:
                    e.nop(nofuse=True)
                for h in range(HG):
                    if LEVELS[l] < 32:
                        ins = e.matmul(ps[:, bL(p), h * 64:(h + 1) * 64], AT[:, p, h, :], even_h(X, p, h, l),
                                       start=True, stop=True)
                    for lo, hi, at in merges(l):
                        ins = e.matmul(ps[hi, bL(p), h * 64 + at:h * 64 + at + LEVELS[l]], AT[lo, p, h, hi],
                                       X[lo, p, h, lo], start=True, stop=True)
                ins.then_inc(s["m1"], 1)
            if l >= NL - 2:
                pe_v(e, n2 + 1, 1 - b, l - (NL - 2))
            for p, g in gs:
                e.wait_ge(s["Pm"], lv(n2, l, p))
                if l:
                    e.wait_ge(s["XT"], lv(n2, l - 1, p))
                if LEVELS[l] >= 32:
                    e.nop(nofuse=True)
                for h in range(HG):
                    if LEVELS[l] < 32:
                        ins = e.matmul(ps[:, bL(p), 256 + h * 64:256 + (h + 1) * 64], XT[:, p, h, :],
                                       Pm[:, p, h, :], start=True, stop=True)
                    for lo, hi, at in merges(l):
                        ins = e.matmul(ps[hi, bL(p), 256 + h * 64 + at:256 + h * 64 + at + LEVELS[l]], XT[hi, p, h, hi],
                                       Pm[hi, p, h, at:at + LEVELS[l]], start=True, stop=True)
                ins.then_inc(s["m2"], 1)
            for p, g in gs:
                e.wait_ge(s["X"], lv(n2, l, p))
                if l == NL - 1:
                    e.nop(nofuse=True)
                for h in range(HG):
                    if l < NL - 1:
                        ins = e.transpose(ps[:, bT(p), h * P:(h + 1) * P], X[:, p, h, :], c.ident)
                    else:
                        ins = e.transpose(ps[0:64, bT(p), h * 64:h * 64 + 64], X[64:128, p, h, 0:64],
                                          c.ident[64:128, 64:128])
                ins.then_inc(s["t"], 1)
            if l == 0:
                pe_next(e, 2, n2, 1 - b)
        for p, g in gs:
            e.wait_ge(s["XT"], lv(n2, NL - 1, p))
            e.wait_ge(s["oS"], g + 1)
            for h in range(HG):
                ins = e.matmul(ps[:, bM(p), h * P:(h + 1) * P], XT[:, p, h, :], R[:, p, h, :],
                               start=True, stop=True)
            ins.then_inc(s["u"], 1)
        for p, g in gs:
            e.wait_ge(s["U"], g + 1)
            for h in range(HG):
                ins = e.matmul(ps[:, bL(p), h * P:(h + 1) * P], PT[:, p, h, :], U[:, p, h, :],
                               start=True, stop=True)
            ins.then_inc(s["pu"], 1)
        pe_next(e, 4, n2, 1 - b)
        for p, g in gs:
            for h in range(HG):
                ins = e.matmul(ps[:, bT(p), h * P:(h + 1) * P], Kd[:, b, HG * p + h, :], U[:, p, h, :],
                               start=True, stop=True)
            ins.then_inc(s["ku"], 1)
        for p, g in gs:
            e.wait_ge(s["O"], g + 3)
            for h in range(HG):
                ins = e.transpose(ps[:, bM(p), h * P:(h + 1) * P], O[:, p, h, :], c.ident)
            ins.then_inc(s["to"], 1)
        for p, g in gs:
            e.wait_ge(s["oT"], g + 3)
            for h in range(HG):
                ins = e.matmul(ps[:, 6, 0:P], oT[:, p, h, :], w["o"][:, HG * p + h, :],
                               start=(p == 0 and h == 0), stop=(p == 1 and h == HG - 1))
        ins.then_inc(s["wo"], 1)

    def act_next(e, step, nx, bx):
        g = 2 * nx
        if step == 0:
            e.wait_ge(s["ba"], nx + 1)
            e.wait_ge(s["zb"], nx)
            e.activation(z[:, :], ps[:, 6, 0:16], ACT.Copy).then_inc(s["z"], 1)
        elif step == 1:
            e.wait_ge(s["ez_in"], nx + 1)
            e.activation(ez[:, :], zneg[:, :], ACT.Exp).then_inc(s["ez"], 1)
            e.wait_ge(s["ez"], nx + 1)
            e.wait_ge(s["la"], nx)
            e.activation(lz[:, :], ez[:, 8:16], ACT.Ln, bias=1.0).then_inc(s["lz"], 1)
            silu(e, "k", g)
        elif step == 2:
            silu(e, "q", g)
        elif step == 3:
            silu(e, "v", g)
        elif step == 4:
            e.wait_ge(s["lst"], nx + 1)
            e.activation(G[:, bx].rearrange("p a h -> p (a h)"), ps[:, 7, 0:24], ACT.Exp).then_inc(s["G"], 1)

    def silu(e, kind, g, halves=(0, 1)):
        for half in halves:
            bk = {"k": 6, "q": 7, "v": 6}[kind] if half == 0 else {"k": 7, "q": 6, "v": 7}[kind]
            e.wait_ge(s["proj_" + kind], g + half + 1)
            e.wait_ge(s[{"q": "Q", "k": "Kd", "v": "Bv"}[kind]], g)
            e.activation(raw[kind][:, hs(half), :], bank(bk), ACT.Silu).then_inc(s["raw_" + kind], 1)

    def act_pair(e, n2, b):
        gs = [(p, 2 * n2 + p) for p in range(2)]
        for dst, src, bk, done in ((kT, "tk", bT, "kT"), (kbT, "tb", bM, "kbT"), (qT, "tq", bL, "qT")):
            for p, g in gs:
                e.wait_ge(s[src], g + 1)
                e.activation(dst[:, p], bank(bk(p)), ACT.Copy).then_inc(s[done], 1)
        for p, g in gs:
            e.wait_ge(s["d"], g + 1)
            e.activation(E[:, p], bank(bT(p)), ACT.Exp).then_inc(s["E"], 1)
        act_next(e, 0, n2 + 1, 1 - b)
        for p, g in gs:
            e.wait_ge(s["qs"], g + 1)
            for h in range(HG):
                ins = e.activation(oS[:, p, h, :], ps[:, bM(p), h * P:(h + 1) * P], ACT.Copy,
                                   scale=G[:, b, 0, HG * p + h:HG * p + h + 1])
            ins.then_inc(s["oS"], 1)
        for p, g in gs:
            e.wait_ge(s["t0"], g + 1)
            e.activation(X[:, p], bank(bT(p)), ACT.Copy).then_inc(s["X0"], 1)
        act_next(e, 1, n2 + 1, 1 - b)
        for l in range(NL):
            for p, g in gs:
                e.wait_ge(s["t"], lv(n2, l, p))
                if l < NL - 1:
                    ins = e.activation(XT[:, p], bank(bT(p)), ACT.Copy)
                else:
                    ins = e.activation(XT[0:64, p, :, 64:128],
                                       ps[0:64, bT(p), 0:256].rearrange("p (h n) -> p h n", h=HG), ACT.Copy)
                ins.then_inc(s["XT"], 1)
            if l == 0:
                act_next(e, 2, n2 + 1, 1 - b)
            elif l >= NL - 2:
                silu(e, "v", 2 * n2 + 2, [l - (NL - 2)])
        for p, g in gs:
            e.wait_ge(s["u"], g + 1)
            e.activation(U[:, p], bank(bM(p)), ACT.Copy).then_inc(s["U"], 1)
        for p, g in gs:
            e.wait_ge(s["to"], g + 1)
            e.activation(oT[:, p], bank(bM(p)), ACT.Copy).then_inc(s["oT"], 1)
        act_next(e, 4, n2 + 1, 1 - b)

    def dve_gates(e, nx):
        e.wait_ge(s["z"], nx + 1)
        e.tensor_scalar(zneg[:, 0:8], z[:, 0:8], -1.0, None, ALU.mult)
        e.tensor_scalar(zmin[:, :], z[:, 8:16], 0.0, None, ALU.min)
        e.scalar_tensor_tensor(zneg[:, 8:16], z[:, 8:16], -1.0, z[:, 8:16], ALU.mult, ALU.min)\
            .then_inc(s["ez_in"], 1)

    def dve_next(e, l, slot, nx, bx):
        g, half = 2 * nx, slot // 2
        if l == 0 and slot == 0:
            e.wait_ge(s["ez"], nx + 1)
            e.tensor_scalar(eb[:, :], ez[:, 0:8], 1.0, None, ALU.add).then_inc(s["zb"], 1)
            e.wait_ge(s["zb"], nx + 1)
            e.reciprocal(beta[:, bx, :], eb[:, :]).then_inc(s["beta"], 1)
            e.wait_ge(s["lz"], nx + 1)
            e.tensor_tensor(la[:, bx, :], zmin[:, :], lz[:, :], ALU.subtract).then_inc(s["la"], 1)
        elif l in (1, 2) and slot % 2:
            j, kind = l - 1, "kq"[l - 1]
            e.wait_ge(s["sq_" + kind], g + half + 1)
            e.tensor_reduce(ss[:, j, hs(half)], sq[:, j, hs(half)], AX, ALU.add).then_inc(s["ss"], 1)
            if l == 2 and half:
                e.wait_ge(s["ss"], 4 * nx + 4)
                e.tensor_scalar(sse[:, :, :], ss[:, :, :], 1e-6, None, ALU.add).then_inc(s["sse"], 1)
        elif l == 3 and slot == 3:
            e.wait_ge(s["rn"], nx + 1)
            e.wait_ge(s["beta"], nx + 1)
            dve_k(e, bx, 0)

    def dve_k(e, bx, half):
        for h in range(HG * half, HG * half + HG):
            ins = e.tensor_scalar(K[:, bx, h, :], raw["k"][:, h, :], rn[:, 0, h:h + 1], None, ALU.mult)
        ins.then_inc(s["K"], 1)

    def dve_kb(e, bx):
        for half in range(2):
            for h in range(HG * half, HG * half + HG):
                ins = e.tensor_scalar(Kb[:, bx, h, :], raw["k"][:, h, :], rn[:, 0, h:h + 1],
                                      beta[:, bx, h:h + 1], ALU.mult, ALU.mult)
            ins.then_inc(s["Kb"], 1)

    def dve_q(e, bx):
        for half in range(2):
            for h in range(HG * half, HG * half + HG):
                ins = e.tensor_scalar(Q[:, bx, h, :], raw["q"][:, h, :], rn[:, 1, h:h + 1], None, ALU.mult)
            ins.then_inc(s["Q"], 1)

    def dve_values(e, n2, b):
        e.wait_ge(s["raw_v"], 2 * n2 + 2)
        for half in range(2):
            for h in range(HG * half, HG * half + HG):
                ins = e.tensor_scalar(Bv[:, b, h, :], raw["v"][:, h, :], beta[:, b, h:h + 1], None, ALU.mult)
            ins.then_inc(s["Bv"], 1)
        e.wait_ge(s["G"], n2 + 1)
        e.scalar_tensor_tensor(bG[:, b, :], G[:, b, 0, :], -1.0, beta[:, b, :], ALU.mult, ALU.mult)\
            .then_inc(s["bG"], 1)
        for half in range(2):
            for h in range(HG * half, HG * half + HG):
                ins = e.tensor_scalar(Kd[:, b, h, :], raw["k"][:, h, :], rn[:, 0, h:h + 1],
                                      G[:, b, 1, h:h + 1], ALU.mult, ALU.mult)
            ins.then_inc(s["Kd"], 1)

    def dve_pair(e, n2, b, tile):
        gs = [(p, 2 * n2 + p) for p in range(2)]
        dve_values(e, n2, b)
        for p, g in gs:
            e.wait_ge(s["kk"], g + 1)
            e.wait_ge(s["E"], g + 1)
            e.tensor_tensor(AT[:, p], bank(bM(p)), E[:, p], ALU.mult).then_inc(s["AT"], 1)
        for p, g in gs:
            e.wait_ge(s["AT"], g + 1)
            e.tensor_tensor(A0[:, p], AT[:, p], c.m0.unsqueeze(1).broadcast_to([P, HG, P]), ALU.mult)\
                .then_inc(s["A0"], 1)
        for p, g in gs:
            e.wait_ge(s["A0"], g + 1)
            e.tensor_tensor(XT[:, p], A0[:, p], c.ident.unsqueeze(1).broadcast_to([P, HG, P]), ALU.add)\
                .then_inc(s["XT0"], 1)
        for p, g in gs:
            e.wait_ge(s["ks"], g + 1)
            e.wait_ge(s["bG"], n2 + 1)
            e.wait_ge(s["Bv"], g + 1)
            for h in range(HG):
                hh = HG * p + h
                ins = e.scalar_tensor_tensor(R[:, p, h, :], ps[:, bT(p), h * P:(h + 1) * P], bG[:, b, hh:hh + 1],
                                             Bv[:, b, hh, :], ALU.mult, ALU.add)
            ins.then_inc(s["R"], 1)
        for p, g in gs:
            e.wait_ge(s["kq"], g + 1)
            e.wait_ge(s["Em"], g + 1)
            e.tensor_tensor(PT[:, p], bank(bL(p)), Em[:, p], ALU.mult).then_inc(s["PT"], 1)
        dve_gates(e, n2 + 1)
        for l in range(NL):
            mask = c.lv[:, l, :].unsqueeze(1).broadcast_to([P, HG, 64])
            for p, g in gs:
                e.wait_ge(s["m1"], lv(n2, l, p))
                if LEVELS[l] < 32:
                    ins = e.tensor_tensor(Pm[:, p], ps[:, bL(p), 0:256].rearrange("p (h n) -> p h n", h=HG), mask,
                                          ALU.mult)
                for lo, hi, at in merges(l):
                    ins = e.tensor_copy(Pm[hi, p, :, at:at + LEVELS[l]],
                                        ps[hi, bL(p), 0:256].rearrange("p (h n) -> p h n", h=HG)[:, :, at:at + LEVELS[l]])
                ins.then_inc(s["Pm"], 1)
                dve_next(e, l, p, n2 + 1, 1 - b)
            for p, g in gs:
                e.wait_ge(s["m2"], lv(n2, l, p))
                if LEVELS[l] < 32:
                    xe = even(X, p, l)
                    ins = e.tensor_tensor(xe, xe, ps[:, bL(p), 256:512].rearrange("p (k s) -> p k s", s=LEVELS[l]),
                                          ALU.subtract)
                for lo, hi, at in merges(l):
                    ins = e.tensor_scalar(X[hi, p, :, lo],
                                          ps[hi, bL(p), 256:512].rearrange("p (h n) -> p h n", h=HG)[:, :, at:at + LEVELS[l]],
                                          -1.0, None, ALU.mult)
                ins.then_inc(s["X"], 1)
                dve_next(e, l, 2 + p, n2 + 1, 1 - b)
        dve_k(e, 1 - b, 1)
        dve_kb(e, 1 - b)
        for p, g in gs:
            e.wait_ge(s["pu"], g + 1)
            e.wait_ge(s["oS"], g + 1)
            e.tensor_tensor(O[:, p], oS[:, p], bank(bL(p)), ALU.add).then_inc(s["O"], 1)
        for p, g in gs:
            e.wait_ge(s["ku"], g + 1)
            for h in range(HG):
                hh = HG * p + h
                ins = e.scalar_tensor_tensor(S[:, b, hh, :], S[:, b, hh, :], G[:, b, 2, hh:hh + 1],
                                             ps[:, bT(p), h * P:(h + 1) * P], ALU.mult, ALU.add)
            ins.then_inc(s["S"], 1)
        dve_q(e, 1 - b)
        e.wait_ge(s["wo"], n2 + 1)
        xt = x1[:, tile, :]
        e.tensor_tensor(xt, xt, ps[:, 6, 0:P], ALU.add).then_inc(s["y"], 1)

    def pool_next(e, step, nx, bx, tile=None, first=False):
        g = 2 * nx
        if step == 0:
            if not first:
                e.wait_ge(s["y"], nx)
            e.tensor_copy(nTs[:, bx, :], nT[:, bass.ts(tile, P)]).then_inc(s["nts"], 1)
        elif step == 1:
            e.wait_ge(s["la"], nx + 1)
            for half in range(2):
                if not first:
                    e.wait_ge(s["d"], g - 1 + half)
                e.tensor_tensor(laU[:, half], la[:, bx, hs(half)].unsqueeze(2).broadcast_to([P, HG, P]),
                                c.utri.unsqueeze(1).broadcast_to([P, HG, P]), ALU.mult).then_inc(s["laU"], 1)
            for j, kind in enumerate("kq"):
                for half in range(2):
                    e.wait_ge(s["raw_" + kind], g + half + 1)
                    r = raw[kind][:, hs(half), :]
                    e.tensor_tensor(sq[:, j, hs(half)], r, r, ALU.mult).then_inc(s["sq_" + kind], 1)
            e.wait_ge(s["sse"], nx + 1)
            e.tensor_tensor(rn[:, :, :], sse[:, :, :], c.neg_half[:, :].rearrange("p (a b) -> p a b", a=2), ALU.pow)\
                .then_inc(s["rn"], 1)

    def pool_pair(e, n2, b, next_tile):
        pool_next(e, 0, n2 + 1, 1 - b, next_tile)
        for p in range(2):
            g = 2 * n2 + p
            e.wait_ge(s["E"], g + 1)
            e.tensor_tensor(Em[:, p], E[:, p], c.utri.unsqueeze(1).broadcast_to([P, HG, P]), ALU.mult)\
                .then_inc(s["Em"], 1)
        pool_next(e, 1, n2 + 1, 1 - b)

    with nc.Block() as block:
        @block.tensor
        def _(e):
            for step in range(5):
                pe_next(e, step, 0, 0, first=True)
            with e.Fori(0, TPB) as i:
                for b in range(B):
                    pe_pair(e, i * 2 + b, b)

        @block.scalar
        def _(e):
            e.sem_inc(s["oT"], 2)
            for step in range(5):
                act_next(e, step, 0, 0)
            with e.Fori(0, TPB) as i:
                for b in range(B):
                    act_pair(e, i * 2 + b, b)

        @block.vector
        def _(e):
            e.sem_inc(s["O"], 2)
            e.sem_inc(s["y"], 1)
            dve_gates(e, 0)
            e.memset(S[:, :, :, :], 0.0).then_inc(s["S"], 4)
            for l in range(4):
                for slot in range(4):
                    dve_next(e, l, slot, 0, 0)
            dve_k(e, 0, 1)
            dve_kb(e, 0)
            dve_q(e, 0)
            e.wait_ge(s["S"], 4)
            with e.Fori(0, TPB) as i:
                for b in range(B):
                    dve_pair(e, i * 2 + b, b, i + b * TPB)

        @block.gpsimd
        def _(e):
            pool_next(e, 0, 0, 0, 0, first=True)
            pool_next(e, 1, 0, 0, first=True)
            with e.Fori(0, TPB) as i:
                for b in range(B):
                    pool_pair(e, i * 2 + b, b, i + TPB if b == 0 else i + 1)


def mlp_buffers(c, st, name, w1, b1, w2, src):
    return dict(
        w1=w1, b1=b1, w2=w2, src=src,
        hid=st.enter_context(c.nc.sbuf_tensor(name + "_hid", [P, 2, 4, 512], F32)),
        up=c.sem(name + "_up"), act=c.sem(name + "_act"), down=c.sem(name + "_down"), out=c.sem(name + "_out"))


def mlp_credits(e, k):
    e.sem_inc(k["act"], 4)


def mlp_up(c, e, k, g, n):
    for f in range(4):
        e.wait_ge(k["act"], n * 4 + f + 1)
        e.matmul(c.ps[:, f, :], k["w1"][:, f * P:(f + 1) * P], k["src"][:, g * 512:(g + 1) * 512],
                 start=True, stop=True).then_inc(k["up"], 1)


def mlp_act(c, e, k, g, n):
    for f in range(4):
        e.wait_ge(k["up"], n * 4 + f + 1)
        e.activation(k["hid"][:, g % 2, f, :], c.ps[:, f, :], ACT.Gelu, bias=k["b1"][:, f:f + 1])\
            .then_inc(k["act"], 1)


def mlp_down(c, e, k, g, n):
    e.wait_ge(k["act"], n * 4 + 8)
    e.wait_ge(k["out"], n + 1)
    for t in range(GT):
        for f in range(4):
            ins = e.matmul(c.ps[:, 4 + g % 2, t * P:(t + 1) * P], k["hid"][:, g % 2, f, t * P:(t + 1) * P],
                           k["w2"][:, f, :], start=(f == 0), stop=(f == 3))
    ins.then_inc(k["down"], 1)


def grp(t, g):
    return t[:, GT * g:GT * g + GT, :]


def bank4(c, k):
    return c.ps[:, k, :].rearrange("p (t d) -> p t d", d=D)


def rows4(r):
    return r.unsqueeze(1).broadcast_to([P, GT, D])


def gdn_mlp_phase(c, st, x1):
    nc = c.nc
    weights = Fp4Weights(c, st)
    W1 = st.enter_context(nc.sbuf_tensor("m0_w1", [P, 512], F32))
    W2 = st.enter_context(nc.sbuf_tensor("m0_w2", [P, 4, D], F32))
    cols = st.enter_context(nc.sbuf_tensor("m0_cols", [P, 6], F32))
    b2 = st.enter_context(nc.sbuf_tensor("m0_b2", [P, D], F32))
    zn = st.enter_context(nc.sbuf_tensor("m0_z", [P, NT, D], F32))
    zT = st.enter_context(nc.sbuf_tensor("m0_zT", [P, NT * P], F32))
    base = st.enter_context(nc.sbuf_tensor("m0_base", [P, NT, D], F32))
    ln = layernorm_steps(c, st, "m0", x1, zn)
    mlp = mlp_buffers(c, st, "m0", W1, cols[:, 2:6], W2, zT)
    loaded, turned, taken, based, biased = (c.sem(n) for n in ("loaded", "turned", "taken", "based", "biased"))
    with nc.Block() as block:
        @block.sync
        def _(e):
            e.dma_start(W1[:, :], c.dram["L0a_W1"]).then_inc(loaded, 16)
            e.dma_start(W2[:, :, :], c.dram["L0a_W2"].rearrange("(f p) d -> p f d", p=P)).then_inc(loaded, 16)
            e.dma_start(cols[:, :], c.dram["L0a_cols"]).then_inc(loaded, 16)
            e.dma_start(b2[:, :], c.dram["L0a_b2"].partition_broadcast(P)).then_inc(loaded, 16)
            weights.load(e)

        @block.gpsimd
        def _(e):
            weights.pad(e)
            e.wait_ge(loaded, 64)
            for g in range(NG):
                ln_rstd(c, e, ln, g)
                e.tensor_tensor(grp(base, g), grp(c.x, g), grp(x1, g), ALU.add).then_inc(based, 1)
                e.wait_ge(based, g + 1)
                e.tensor_tensor(grp(base, g), grp(base, g), rows4(b2[:, :]), ALU.add).then_inc(biased, 1)

        @block.vector
        def _(e):
            e.sem_inc(mlp["out"], 2)
            for g in range(NG):
                ln_stats(c, e, ln, g)
                if g:
                    ln_apply(c, e, ln, g - 1)
            ln_apply(c, e, ln, NG - 1)
            weights.quantise(e)
            for g in range(NG):
                e.wait_ge(biased, g + 1)
                e.wait_ge(mlp["down"], g + 1)
                e.tensor_tensor(grp(c.x, g), grp(base, g), bank4(c, 4 + g % 2), ALU.add).then_inc(mlp["out"], 1)

        @block.tensor
        def _(e):
            e.wait_ge(loaded, 64)

            def turn(g):
                e.wait_ge(ln["out"], GT * g + GT)
                if g >= 2:
                    e.wait_ge(taken, g - 1)
                transpose_group(c, e, zn, 6 + g % 2, g).then_inc(turned, 1)

            turn(0)
            for g in range(NG):
                if g + 1 < NG:
                    turn(g + 1)
                e.wait_ge(taken, g + 1)
                mlp_up(c, e, mlp, g, g)
                if g:
                    mlp_down(c, e, mlp, g - 1, g - 1)
            mlp_down(c, e, mlp, NG - 1, NG - 1)
            weights.turn(e)

        @block.scalar
        def _(e):
            mlp_credits(e, mlp)
            e.wait_ge(loaded, 64)

            def take(g):
                e.wait_ge(turned, g + 1)
                e.activation(zT[:, g * 512:(g + 1) * 512], c.ps[:, 6 + g % 2, :], ACT.Identity,
                             bias=cols[:, 1:2], scale=cols[:, 0:1]).then_inc(taken, 1)

            take(0)
            for g in range(NG):
                if g + 1 < NG:
                    take(g + 1)
                mlp_act(c, e, mlp, g, g)
            weights.take(e)


NE, TOPK, FE = 32, 4, 96
NHC = NE * FE // P


def moe_phase(c, st, tag):
    nc = c.nc

    def sb(name, shape, dt=F32):
        return st.enter_context(nc.sbuf_tensor(f"{tag}_{name}", shape, dt))

    zn, zT = sb("z", [P, NT, D]), sb("zT", [P, NT * P])
    gate, ebias = sb("gate", [P, NE]), sb("ebias", [P, NE])
    sc, sbi = sb("scores", [P, NT, NE]), sb("biased", [P, NT, NE])
    m8, ngt = sb("max8", [P, NT, 8]), sb("ngt", [P, NT])
    gt, eq, pre, le = (sb(n, [P, NT, NE]) for n in ("gt", "eq", "pre", "le"))
    tot, rec = sb("tot", [P, NT]), sb("rec", [P, NT])
    comb, rest = sb("comb", [P, NT, NE]), sb("rest", [P, NT, NE])
    c3 = sb("c3", [P, NT, 3 * NE], BF16)
    idb, selb = sb("idb", [P, P], BF16), sb("selb", [P, NE], BF16)
    cT = sb("cT", [3 * NE, NT * P], BF16)
    w13, w2 = sb("w13", [P, 2, 2 * P]), sb("w2", [P, 2, D])
    selw = sb("selw", [3 * NE, NE, FE], BF16)
    sg, au, a = sb("sg", [P, 2, 512]), sb("au", [P, 2, 512]), sb("a", [P, 2, 512])
    yT = sb("yT", [P, NT * P])
    ln = layernorm_steps(c, st, tag, c.x, zn)
    s = {n: c.sem(f"{tag}_{n}") for n in (
        "loaded", "turned", "taken", "logits", "scores", "step", "m8", "c3", "cturn", "cT", "cast", "selw", "zero",
        "w0", "w1", "g", "u", "cb", "silu", "a1", "a", "down", "accT", "yturn", "y")}
    ps = c.ps

    def bc(t):
        return t.unsqueeze(2).broadcast_to([P, NT, NE])

    with nc.Block() as block:
        @block.sync
        def _(e):
            e.dma_start(gate[:, :], c.dram["moe_gateT"]).then_inc(s["loaded"], 16)
            e.dma_start(ebias[:, :], c.dram["moe_ebias"].partition_broadcast(P)).then_inc(s["loaded"], 16)

            def load(k, slot):
                e.dma_start(w13[:, slot, :], c.dram["moe_w13"][k]).then_inc(s[f"w{slot}"], 16)
                e.dma_start(w2[:, slot, :], c.dram["moe_w2"][k]).then_inc(s[f"w{slot}"], 16)

            load(0, 0)
            with e.Fori(0, NHC // 2 - 1) as i:
                e.wait_ge(s["down"], i * 8 + 1)
                load(i * 2 + 1, 1)
                e.wait_ge(s["down"], i * 8 + 5)
                load(i * 2 + 2, 0)
            e.wait_ge(s["down"], 4 * NHC - 7)
            load(NHC - 1, 1)

        @block.gpsimd
        def _(e):
            e.memset(a[:, 1, :], 0.0).then_inc(s["zero"], 1)
            e.memset(w2[:, 1, :], 0.0).then_inc(s["zero"], 1)
            for g in range(NG):
                ln_rstd(c, e, ln, g)

        @block.vector
        def _(e):
            e.tensor_copy(idb[:, :], c.ident).then_inc(s["cast"], 1)
            e.tensor_copy(selb[:, :], c.sel).then_inc(s["cast"], 1)
            for g in range(NG):
                ln_stats(c, e, ln, g)
                if g:
                    ln_apply(c, e, ln, g - 1)
            ln_apply(c, e, ln, NG - 1)
            n = [0]

            def step(ins):
                n[0] += 1
                ins.then_inc(s["step"], 1)
                e.wait_ge(s["step"], n[0])

            e.wait_ge(s["loaded"], 32)
            e.wait_ge(s["scores"], 1)
            step(e.tensor_tensor(sbi[:, :, :], sc[:, :, :], ebias[:, :].unsqueeze(1).broadcast_to([P, NT, NE]), ALU.add))
            for t in range(NT):
                e.max(m8[:, t, :], sbi[:, t, :]).then_inc(s["m8"], 1)
            e.wait_ge(s["m8"], NT)
            thr = bc(m8[:, :, TOPK - 1])
            step(e.tensor_tensor(gt[:, :, :], sbi[:, :, :], thr, ALU.is_gt))
            step(e.tensor_tensor(eq[:, :, :], sbi[:, :, :], thr, ALU.is_equal))
            step(e.tensor_reduce(ngt[:, :], gt[:, :, :], AX, ALU.add))
            step(e.tensor_tensor_scan(pre[:, :, :].rearrange("p t n -> p (t n)"), c.rst[:, :],
                                      eq[:, :, :].rearrange("p t n -> p (t n)"), 0.0, ALU.mult, ALU.add))
            step(e.tensor_tensor(pre[:, :, :], pre[:, :, :], bc(ngt[:, :]), ALU.add))
            step(e.scalar_tensor_tensor(le[:, :, :], pre[:, :, :], float(TOPK), eq[:, :, :], ALU.is_le, ALU.mult))
            step(e.tensor_tensor(gt[:, :, :], gt[:, :, :], le[:, :, :], ALU.add))
            step(e.tensor_tensor(gt[:, :, :], gt[:, :, :], sc[:, :, :], ALU.mult))
            step(e.tensor_reduce(tot[:, :], gt[:, :, :], AX, ALU.add))
            step(e.reciprocal(rec[:, :], tot[:, :]))
            step(e.tensor_tensor(comb[:, :, :], gt[:, :, :], bc(rec[:, :]), ALU.mult))
            step(e.tensor_copy(c3[:, :, 0:NE], comb[:, :, :]))
            step(e.tensor_tensor(rest[:, :, :], comb[:, :, :], c3[:, :, 0:NE], ALU.subtract))
            step(e.tensor_copy(c3[:, :, NE:2 * NE], rest[:, :, :]))
            e.tensor_tensor(c3[:, :, 2 * NE:3 * NE], rest[:, :, :], c3[:, :, NE:2 * NE], ALU.subtract).then_inc(s["c3"], 1)
            e.sem_inc(s["a"], 2)
            e.sem_inc(s["a1"], 1)
            with e.Fori(0, NHC) as k:
                for g in range(NG):
                    m = k * NG + g
                    e.wait_ge(s["silu"], m + 2)
                    e.wait_ge(s["u"], m + 1)
                    e.tensor_tensor(au[:, g % 2, :], sg[:, g % 2, :], ps[:, (3 * g + 1) % 4, :], ALU.mult)\
                        .then_inc(s["a1"], 1)
                    e.wait_ge(s["cb"], m + 1)
                    e.wait_ge(s["a1"], m + 2)
                    e.tensor_tensor(a[:, g % 2, :], au[:, g % 2, :], ps[:, (3 * g + 2) % 4, :], ALU.mult)\
                        .then_inc(s["a"], 1)
            for g in range(NG):
                e.wait_ge(s["yturn"], g + 1)
                e.tensor_tensor(grp(c.x, g), grp(c.x, g), bank4(c, g), ALU.add).then_inc(s["y"], 1)

        @block.tensor
        def _(e):
            def turn(g):
                e.wait_ge(ln["out"], GT * g + GT)
                transpose_group(c, e, zn, g, g).then_inc(s["turned"], 1)

            turn(0)
            for g in range(NG):
                if g + 1 < NG:
                    turn(g + 1)
                if g == 0:
                    e.wait_ge(s["loaded"], 32)
                e.wait_ge(s["taken"], g + 1)
                for t in range(GT * g, GT * g + GT):
                    ins = e.matmul(ps[:, 4, t * NE:(t + 1) * NE], zT[:, t * P:(t + 1) * P], gate[:, :],
                                   start=True, stop=True)
            ins.then_inc(s["logits"], 1)
            e.wait_ge(s["zero"], 2)
            e.wait_ge(s["scores"], 1)
            for g in range(NG):
                e.matmul(ps[:, 4 + g, :], w2[:, 1, :], a[:, 1, :], start=True, stop=False, skip_group_check=True)
            e.wait_ge(s["c3"], 1)
            e.wait_ge(s["cast"], 2)
            for t in range(NT):
                out = ps[0:3 * NE, t // 8, :].bitcast(BF16)[:, (t % 8) * P:(t % 8 + 1) * P]
                ins = e.transpose(out, c3[:, t, :], idb[:, :])
                if t % 8 == 7:
                    ins.then_inc(s["cturn"], 1)
            e.wait_ge(s["cT"], 2)

            def down(g, slot, m):
                e.wait_ge(s["a"], m + 2)
                e.matmul(ps[:, 4 + g, :], w2[:, slot, :], a[:, g % 2, :], start=False, stop=False,
                         skip_group_check=True).then_inc(s["down"], 1)

            e.wait_ge(s["selw"], 1)
            with e.Fori(0, NHC // 2) as i:
                for slot in range(2):
                    k = i * 2 + slot
                    e.wait_ge(s[f"w{slot}"], i * 32 + 32)
                    for g in range(NG):
                        m = k * NG + g
                        z = zT[:, g * 512:(g + 1) * 512]
                        e.wait_ge(s["a"], m + 1)
                        e.matmul(ps[:, 3 * g % 4, :], w13[:, slot, 0:P], z, start=True, stop=True).then_inc(s["g"], 1)
                        e.wait_ge(s["silu"], m + 1)
                        e.matmul(ps[:, (3 * g + 1) % 4, :], w13[:, slot, P:2 * P], z, start=True, stop=True)\
                            .then_inc(s["u"], 1)
                        e.wait_ge(s["a1"], m + 1)
                        e.matmul(ps[:, (3 * g + 2) % 4, :],
                                 selw[:, :, :].rearrange("p e u -> p (e u)")[:, bass.ds(k * P, P)],
                                 cT[:, g * 512:(g + 1) * 512], start=True, stop=True).then_inc(s["cb"], 1)
                        down((g - 1) % NG, slot if g else 1 - slot, m)
            down(NG - 1, 1, 4 * NHC)
            for g in range(NG):
                e.wait_ge(s["accT"], g + 1)
                transpose_cols(c, e, yT, g, g).then_inc(s["yturn"], 1)

        @block.scalar
        def _(e):
            e.wait_ge(s["cast"], 2)
            e.activation(selw[:, :, :], selb[0:3 * NE, :].unsqueeze(2).broadcast_to([3 * NE, NE, FE]), ACT.Copy)\
                .then_inc(s["selw"], 1)
            for g in range(NG):
                e.wait_ge(s["turned"], g + 1)
                e.activation(zT[:, g * 512:(g + 1) * 512], ps[:, g, :], ACT.Copy).then_inc(s["taken"], 1)
            e.wait_ge(s["logits"], 1)
            e.activation(sc[:, :, :].rearrange("p t n -> p (t n)"), ps[:, 4, :], ACT.Sigmoid).then_inc(s["scores"], 1)
            for k in range(2):
                e.wait_ge(s["cturn"], k + 1)
                e.activation(cT[:, k * 1024:(k + 1) * 1024], ps[0:3 * NE, k, :].bitcast(BF16), ACT.Copy)\
                    .then_inc(s["cT"], 1)
            e.sem_inc(s["silu"], 1)
            with e.Fori(0, NHC) as k:
                for g in range(NG):
                    e.wait_ge(s["g"], k * NG + g + 1)
                    e.activation(sg[:, g % 2, :], ps[:, 3 * g % 4, :], ACT.Silu).then_inc(s["silu"], 1)
            e.wait_ge(s["down"], 4 * NHC + 1)
            for g in range(NG):
                e.activation(yT[:, g * 512:(g + 1) * 512], ps[:, 4 + g, :], ACT.Copy).then_inc(s["accT"], 1)


def transpose_cols(c, e, src, bank, g):
    for t in range(GT):
        ins = e.transpose(c.ps[:, bank, t * P:(t + 1) * P], src[:, (GT * g + t) * P:(GT * g + t + 1) * P], c.ident)
    return ins


FS = 344
FSC = [(0, 128), (128, 128), (256, 88)]


def ssm_phase(c, st):
    nc = c.nc

    def sb(name, shape):
        return st.enter_context(nc.sbuf_tensor("ssm_" + name, shape, F32))

    a, un, uT = sb("a", [P, NT, D]), sb("un", [P, NT, D]), sb("uT", [P, NT * P])
    hs, lam = sb("hs", [32, NT * P]), sb("lam", [32, 1])
    Bw, Cw, loglam = sb("Bw", [P, 32]), sb("Cw", [32, D]), sb("loglam", [32, 1])
    cols, diag = sb("cols", [P, 3]), sb("diag", [P, P])
    zT, base = sb("zT", [P, NT * P]), sb("base", [P, NT, D])
    W1, W3, W2 = sb("W1", [P, FS]), sb("W3", [P, FS]), sb("W2", [P, 3, D])
    sg, hid = sb("sg", [P, 2, 512]), sb("hid", [P, 2, 3, 512])
    ln = layernorm_steps(c, st, "ssm0", c.x, a)
    r1 = layernorm_steps(c, st, "ssm1", a, un, eps=1e-6, rms=True)
    r2 = layernorm_steps(c, st, "ssm2", a, un, eps=1e-6, rms=True)
    s = {n: c.sem("ssm_" + n) for n in (
        "loaded", "lam", "diag", "turned", "uT", "bu", "hs", "mix", "x1", "turned2", "zT", "based",
        "gate", "val", "silu", "hid", "down", "out")}
    ps = c.ps
    NF = len(FSC)
    def residual(e, g):
        e.wait_ge(s["down"], g + 1)
        e.wait_ge(s["based"], g + 1)
        e.tensor_tensor(grp(c.x, g), grp(base, g), bank4(c, 4 + g % 2), ALU.add).then_inc(s["out"], 1)

    def down(e, g):
        e.wait_ge(s["hid"], NF * g + NF)
        if g >= 2:
            e.wait_ge(s["out"], g - 1)
        for t in range(GT):
            for f, (f0, fn) in enumerate(FSC):
                ins = e.matmul(ps[:, 4 + g % 2, t * P:(t + 1) * P], hid[0:fn, g % 2, f, t * P:(t + 1) * P],
                               W2[0:fn, f, :], start=(f == 0), stop=(f == NF - 1))
        ins.then_inc(s["down"], 1)

    with nc.Block() as block:
        @block.sync
        def _(e):
            e.dma_start(Bw[:, :], c.dram["ssm_BT"]).then_inc(s["loaded"], 16)
            e.dma_start(Cw[:, :], c.dram["ssm_CT"]).then_inc(s["loaded"], 16)
            e.dma_start(loglam[:, :], c.dram["ssm_loglam"]).then_inc(s["loaded"], 16)
            e.dma_start(cols[:, :], c.dram["ssm_cols"]).then_inc(s["loaded"], 16)
            e.dma_start(W1[:, :], c.dram["ssm_W1T"]).then_inc(s["loaded"], 16)
            e.dma_start(W3[:, :], c.dram["ssm_W3T"]).then_inc(s["loaded"], 16)
            for f, (f0, fn) in enumerate(FSC):
                e.dma_start(W2[0:fn, f, :], c.dram["ssm_W2T"][f0:f0 + fn, :]).then_inc(s["loaded"], 16)

        @block.gpsimd
        def _(e):
            for k in (ln, r1):
                for g in range(NG):
                    ln_rstd(c, e, k, g)
            for g in range(NG):
                ln_rstd(c, e, r2, g)
                e.wait_ge(s["x1"], g + 1)
                e.tensor_tensor(grp(base, g), grp(c.x, g), grp(a, g), ALU.add).then_inc(s["based"], 1)

        @block.vector
        def _(e):
            for g in range(NG):
                ln_stats(c, e, ln, g)
            for g in range(NG):
                ln_apply(c, e, ln, g)
                e.wait_ge(ln["out"], GT * g + GT)
                ln_stats(c, e, r1, g)
                if g:
                    ln_apply(c, e, r1, g - 1)
            ln_apply(c, e, r1, NG - 1)
            e.wait_ge(s["loaded"], 144)
            e.tensor_scalar(diag[:, :], c.ident, cols[:, 1:2], None, ALU.mult).then_inc(s["diag"], 1)
            e.wait_ge(s["lam"], 1)
            for g in range(NG):
                e.wait_ge(s["bu"], g + 1)
                first = g % (NG // B) == 0
                if not first:
                    e.wait_ge(s["hs"], g)
                e.tensor_tensor_scan(hs[:, g * 512:(g + 1) * 512], lam[:, 0:1].broadcast_to([32, 512]), ps[0:32, g % 2, :],
                                     0.0 if first else hs[:, g * 512 - 1:g * 512], ALU.mult, ALU.add)\
                    .then_inc(s["hs"], 1)
            for g in range(NG):
                e.wait_ge(s["mix"], g + 1)
                e.tensor_tensor(grp(a, g), grp(a, g), bank4(c, 2 + g % 2), ALU.add).then_inc(s["x1"], 1)
                e.wait_ge(s["x1"], g + 1)
                ln_stats(c, e, r2, g)
                if g:
                    ln_apply(c, e, r2, g - 1)
            ln_apply(c, e, r2, NG - 1)
            for g in range(NG):
                for f, (f0, fn) in enumerate(FSC):
                    m = NF * g + f
                    e.wait_ge(s["silu"], m + 1)
                    e.wait_ge(s["val"], m + 1)
                    e.tensor_tensor(hid[0:fn, g % 2, f, :], sg[0:fn, m % 2, :], ps[0:fn, 2 + m % 2, :], ALU.mult)\
                        .then_inc(s["hid"], 1)
                if g:
                    residual(e, g - 1)
            residual(e, NG - 1)

        @block.tensor
        def _(e):
            for g in range(NG):
                e.wait_ge(r1["out"], GT * g + GT)
                if g >= 2:
                    e.wait_ge(s["uT"], g - 1)
                transpose_group(c, e, un, 6 + g % 2, g).then_inc(s["turned"], 1)
            e.wait_ge(s["loaded"], 144)
            for g in range(NG):
                e.wait_ge(s["uT"], g + 1)
                if g >= 2:
                    e.wait_ge(s["hs"], g - 1)
                e.matmul(ps[0:32, g % 2, :], Bw[:, :], uT[:, g * 512:(g + 1) * 512], start=True, stop=True)\
                    .then_inc(s["bu"], 1)
            e.wait_ge(s["diag"], 1)
            for g in range(NG):
                e.wait_ge(s["hs"], g + 1)
                if g >= 2:
                    e.wait_ge(s["x1"], g - 1)
                for t in range(GT):
                    tok = slice((GT * g + t) * P, (GT * g + t + 1) * P)
                    e.matmul(ps[:, 2 + g % 2, t * P:(t + 1) * P], hs[:, tok], Cw[:, :], start=True, stop=False)
                    ins = e.matmul(ps[:, 2 + g % 2, t * P:(t + 1) * P], uT[:, tok], diag[:, :], start=False, stop=True)
                ins.then_inc(s["mix"], 1)
            for g in range(NG):
                e.wait_ge(r2["out"], GT * g + GT)
                if g >= 2:
                    e.wait_ge(s["zT"], g - 1)
                transpose_group(c, e, un, 6 + g % 2, g).then_inc(s["turned2"], 1)
            for g in range(NG):
                e.wait_ge(s["zT"], g + 1)
                for f, (f0, fn) in enumerate(FSC):
                    m = NF * g + f
                    if m >= 2:
                        e.wait_ge(s["silu"], m - 1)
                    if m < 2:
                        e.wait_ge(s["hs"], NG)
                    e.matmul(ps[0:fn, m % 2, :], W1[:, f0:f0 + fn], zT[:, g * 512:(g + 1) * 512],
                             start=True, stop=True).then_inc(s["gate"], 1)
                    if m >= 2:
                        e.wait_ge(s["hid"], m - 1)
                    else:
                        e.wait_ge(s["x1"], NG)
                    e.matmul(ps[0:fn, 2 + m % 2, :], W3[:, f0:f0 + fn], zT[:, g * 512:(g + 1) * 512],
                             start=True, stop=True).then_inc(s["val"], 1)
                if g:
                    down(e, g - 1)
            down(e, NG - 1)

        @block.scalar
        def _(e):
            e.wait_ge(s["loaded"], 144)
            e.activation(lam[:, :], loglam[:, :], ACT.Sigmoid).then_inc(s["lam"], 1)
            for g in range(NG):
                e.wait_ge(s["turned"], g + 1)
                e.activation(uT[:, g * 512:(g + 1) * 512], ps[:, 6 + g % 2, :], ACT.Copy, scale=cols[:, 0:1])\
                    .then_inc(s["uT"], 1)
            for g in range(NG):
                e.wait_ge(s["turned2"], g + 1)
                e.activation(zT[:, g * 512:(g + 1) * 512], ps[:, 6 + g % 2, :], ACT.Copy, scale=cols[:, 2:3])\
                    .then_inc(s["zT"], 1)
            for g in range(NG):
                for f, (f0, fn) in enumerate(FSC):
                    m = NF * g + f
                    e.wait_ge(s["gate"], m + 1)
                    if m >= 2:
                        e.wait_ge(s["hid"], m - 1)
                    e.activation(sg[0:fn, m % 2, :], ps[0:fn, m % 2, :], ACT.Silu).then_inc(s["silu"], 1)


FQ = 352
FQC = [(0, 128), (128, 128), (256, 96)]
BLOCK = 16


class Fp4:

    def __init__(self, c, st, name, nb):
        def sb(n, shape):
            return st.enter_context(c.nc.sbuf_tensor(f"{name}_{n}", shape, F32))
        self.amax, self.scale, self.inv = (sb(n, [P, nb]) for n in ("amax", "scale", "inv"))
        self.ax, self.r05, self.r1, self.r2 = (sb(n, [P, nb, BLOCK]) for n in ("ax", "r05", "r1", "r2"))
        self.sem, self.n = c.sem(name + "_fp4"), 0

    def quantise(self, e, q, x, nb, done):
        u = mybir.dt.uint32
        halves = (slice(0, nb // 2), slice(nb // 2, nb))
        last = [0, 0]

        def step(k, ins):
            self.n += 1
            last[k] = self.n
            ins.then_inc(self.sem, 1)

        def ready(k):
            e.wait_ge(self.sem, last[k])

        def wide(t, h):
            return t[:, h].unsqueeze(2).broadcast_to([P, h.stop - h.start, BLOCK])

        amax, scale, inv, ax, r05, r1, r2 = self.amax, self.scale, self.inv, self.ax, self.r05, self.r1, self.r2
        for k, h in enumerate(halves):
            step(k, e.tensor_reduce(amax[:, h], x[:, h], AX, ALU.max, apply_absolute_value=True))
        for k, h in enumerate(halves):
            ready(k)
            step(k, e.tensor_scalar(scale[:, h], amax[:, h], 1.0 / 6.0, 1e-12, ALU.mult, ALU.max))
        for k, h in enumerate(halves):
            ready(k)
            step(k, e.reciprocal(inv[:, h], scale[:, h]))
        for k, h in enumerate(halves):
            ready(k)
            step(k, e.tensor_scalar(inv[:, h], inv[:, h], 1.0 - 2.0 ** -22, None, ALU.mult))
        for k, h in enumerate(halves):
            ready(k)
            step(k, e.tensor_tensor(r1[:, h], x[:, h], wide(inv, h), ALU.mult))
        for k, h in enumerate(halves):
            ready(k)
            step(k, e.tensor_scalar(ax[:, h].bitcast(u), r1[:, h].bitcast(u), 0x7FFFFFFF, None, ALU.bitwise_and))
        for k, h in enumerate(halves):
            ready(k)
            for r, m in ((r05, 1.5 * 2 ** 22), (r2, 1.5 * 2 ** 24), (r1, 1.5 * 2 ** 23)):
                step(k, e.tensor_scalar(r[:, h], ax[:, h], m, m, ALU.add, ALU.subtract))
        for k, h in enumerate(halves):
            ready(k)
            step(k, e.tensor_scalar(r1[:, h], r1[:, h], 2.0, 4.0, ALU.max, ALU.min))
        for k, h in enumerate(halves):
            ready(k)
            step(k, e.scalar_tensor_tensor(r1[:, h], r05[:, h], 2.0, r1[:, h], ALU.min, ALU.add))
        for k, h in enumerate(halves):
            ready(k)
            step(k, e.scalar_tensor_tensor(r1[:, h], r2[:, h], 4.0, r1[:, h], ALU.max, ALU.add))
        for k, h in enumerate(halves):
            ready(k)
            step(k, e.scalar_tensor_tensor(r1[:, h], r1[:, h], -6.0, wide(scale, h), ALU.add, ALU.mult))
        for k, h in enumerate(halves):
            ready(k)
            e.scalar_tensor_tensor(q[:, h].bitcast(u), x[:, h].bitcast(u), 0x80000000, r1[:, h].bitcast(u),
                                   ALU.bitwise_and, ALU.bitwise_or).then_inc(done, 1)


def blocks(t):
    return t.rearrange("p (b k) -> p b k", k=BLOCK)


class Fp4Weights:

    def __init__(self, c, st):
        nc = c.nc
        self.c = c
        self.nr = 2 * len(FQC) * P
        self.rows = st.enter_context(nc.sbuf_tensor("fw_rows", [P, self.nr + FQ], F32))
        self.rq = st.enter_context(nc.sbuf_tensor("fw_rq", [P, self.nr + FQ], F32))
        self.nb = (self.nr + FQ) // BLOCK
        self.fp4 = Fp4(c, st, "fw", self.nb)
        self.padded, self.loaded, self.quant, self.turned, self.taken = (
            c.sem("fw_" + n) for n in ("padded", "loaded", "quant", "turned", "taken"))

    def pad(self, e):
        for k in range(2, self.nr // P, 3):
            e.memset(self.rows[FQC[2][1]:P, k * P:(k + 1) * P], 0.0).then_inc(self.padded, 1)
        e.wait_ge(self.padded, 2)

    def load(self, e):
        for m, name in enumerate(("fp4_gate", "fp4_up")):
            for f, (f0, fn) in enumerate(FQC):
                k = 3 * m + f
                e.dma_start(self.rows[0:fn, k * P:(k + 1) * P], self.c.dram[name][f0:f0 + fn, :]).then_inc(self.loaded, 16)
        e.dma_start(self.rows[:, self.nr:], self.c.dram["fp4_down"]).then_inc(self.loaded, 16)

    def quantise(self, e):
        e.wait_ge(self.loaded, 112)
        e.wait_ge(self.padded, 2)
        self.fp4.quantise(e, blocks(self.rq[:, :]), blocks(self.rows[:, :]), self.nb, self.quant)

    def turn(self, e):
        e.wait_ge(self.quant, 2)
        for m in range(2):
            for f, (f0, fn) in enumerate(FQC):
                k = 3 * m + f
                ins = e.transpose(self.c.ps[:, m, f0:f0 + fn], self.rq[0:fn, k * P:(k + 1) * P], self.c.ident[0:fn, 0:fn])
        for f, (f0, fn) in enumerate(FQC):
            ins = e.transpose(self.c.ps[0:fn, 2, f * P:(f + 1) * P], self.rq[:, self.nr + f0:self.nr + f0 + fn], self.c.ident)
        ins.then_inc(self.turned, 1)

    def take(self, e):
        e.wait_ge(self.turned, 1)
        for m in range(2):
            e.activation(self.c.wgu[:, m * FQ:(m + 1) * FQ], self.c.ps[:, m, 0:FQ], ACT.Copy).then_inc(self.taken, 1)
        for f, (f0, fn) in enumerate(FQC):
            e.activation(self.c.wd[0:fn, f, :], self.c.ps[0:fn, 2, f * P:(f + 1) * P], ACT.Copy).then_inc(self.taken, 1)


def fp4_phase(c, st, tag):
    nc = c.nc

    def sb(name, shape):
        return st.enter_context(nc.sbuf_tensor(f"{tag}_{name}", shape, F32))

    zn, zq, zT = sb("z", [P, NT, D]), sb("zq", [P, NT, D]), sb("zT", [P, NT * P])
    sg, h, hq = sb("sg", [P, 2, 2, FQ]), sb("h", [P, 2, 2, FQ]), sb("hq", [P, 2, 2, FQ])
    hT = sb("hT", [P, 2, 3, P])
    ln = layernorm_steps(c, st, tag, c.x, zn)
    wgu, wd = c.wgu, c.wd
    fx, fh = Fp4(c, st, tag + "x", GT * D // BLOCK), Fp4(c, st, tag + "h", 2 * FQ // BLOCK)
    s = {n: c.sem(f"{tag}_{n}") for n in (
        "zq", "turned", "zT", "up", "silu", "h", "hq", "hturn", "hT", "down", "out")}
    ps = c.ps
    NP = NT // 2

    with nc.Block() as block:
        @block.gpsimd
        def _(e):
            for g in range(NG):
                ln_rstd(c, e, ln, g)

        @block.vector
        def _(e):
            def residual(i):
                e.wait_ge(s["down"], 2 * i + 2)
                xs = c.x[:, 2 * i:2 * i + 2, :]
                e.tensor_tensor(xs, xs, ps[:, 6:8, 0:P], ALU.add).then_inc(s["out"], 1)

            for g in range(NG):
                ln_stats(c, e, ln, g)
                if g:
                    ln_apply(c, e, ln, g - 1)
            ln_apply(c, e, ln, NG - 1)
            for g in range(NG):
                e.wait_ge(ln["out"], GT * g + GT)
                fx.quantise(e, blocks(grp(zq, g).rearrange("p t d -> p (t d)")),
                            blocks(grp(zn, g).rearrange("p t d -> p (t d)")), GT * D // BLOCK, s["zq"])
            for i in range(NP):
                e.wait_ge(s["silu"], i + 1)
                e.wait_ge(s["up"], i + 1)
                e.tensor_tensor(h[:, i % 2], sg[:, i % 2], ps[:, 2:4, 0:FQ], ALU.mult).then_inc(s["h"], 1)
                e.wait_ge(s["h"], i + 1)
                if i >= 2:
                    e.wait_ge(s["hturn"], 2 * i - 2)
                fh.quantise(e, blocks(hq[:, i % 2].rearrange("p t f -> p (t f)")),
                            blocks(h[:, i % 2].rearrange("p t f -> p (t f)")), 2 * FQ // BLOCK, s["hq"])
                if i:
                    residual(i - 1)
            residual(NP - 1)

        @block.tensor
        def _(e):
            def gate_up(i):
                e.wait_ge(s["zT"], 2 * i // GT + 1)
                if i:
                    e.wait_ge(s["silu"], i)
                    e.wait_ge(s["h"], i)
                for k in range(2):
                    tok = zT[:, (2 * i + k) * P:(2 * i + k + 1) * P]
                    e.matmul(ps[:, k, 0:FQ], tok, wgu[:, 0:FQ], start=True, stop=True)
                    ins = e.matmul(ps[:, 2 + k, 0:FQ], tok, wgu[:, FQ:2 * FQ], start=True, stop=True)
                ins.then_inc(s["up"], 1)

            def down(i):
                for k in range(2):
                    t = 2 * i + k
                    e.wait_ge(s["hq"], 2 * i + k + 1)
                    if i == 0:
                        e.wait_ge(s["zT"], k + 1)
                    else:
                        e.wait_ge(s["hT"], 2 * (t - 1))
                    for f, (f0, fn) in enumerate(FQC):
                        ins = e.transpose(ps[0:fn, 4 + k, f * P:(f + 1) * P], hq[:, i % 2, k, f0:f0 + fn], c.ident)
                    ins.then_inc(s["hturn"], 1)
                for k in range(2):
                    t = 2 * i + k
                    e.wait_ge(s["hT"], 2 * t + 2)
                    if i == 0:
                        e.wait_ge(s["zT"], k + 3)
                    else:
                        e.wait_ge(s["out"], i)
                    for f, (f0, fn) in enumerate(FQC):
                        ins = e.matmul(ps[:, 6 + k, 0:P], hT[0:fn, k, f, :], wd[0:fn, f, :],
                                       start=(f == 0), stop=(f == 2))
                    ins.then_inc(s["down"], 1)

            for g in range(NG):
                e.wait_ge(s["zq"], 2 * g + 2)
                transpose_group(c, e, zq, 4 + g, g).then_inc(s["turned"], 1)
                if g == 0:
                    gate_up(0)
            for i in range(1, NP):
                gate_up(i)
                down(i - 1)
            down(NP - 1)

        @block.scalar
        def _(e):
            def take(g):
                e.wait_ge(s["turned"], g + 1)
                e.activation(zT[:, g * 512:(g + 1) * 512], ps[:, 4 + g, :], ACT.Copy).then_inc(s["zT"], 1)

            def silu(i):
                e.wait_ge(s["up"], i + 1)
                if i >= 2:
                    e.wait_ge(s["h"], i - 1)
                e.activation(sg[:, i % 2], ps[:, 0:2, 0:FQ], ACT.Silu).then_inc(s["silu"], 1)

            def turn(i):
                for t in (2 * i, 2 * i + 1):
                    e.wait_ge(s["hturn"], t + 1)
                    if i:
                        e.wait_ge(s["down"], t - 1)
                    whole, (f0, fn) = 2 * P, FQC[2]
                    e.activation(hT[:, t % 2, 0:2, :].rearrange("p f n -> p (f n)"), ps[:, 4 + t % 2, 0:whole],
                                 ACT.Copy).then_inc(s["hT"], 1)
                    e.activation(hT[0:fn, t % 2, 2, :], ps[0:fn, 4 + t % 2, whole:whole + P], ACT.Copy).then_inc(s["hT"], 1)

            take(0)
            silu(0)
            for g in range(1, NG):
                take(g)
            for i in range(1, NP):
                silu(i)
                turn(i - 1)
            turn(NP - 1)


NL1 = 8
HL1, DL1 = 16, 8


def linear_attention_phase(c, st):
    nc = c.nc

    def sb(name, shape):
        return st.enter_context(nc.sbuf_tensor("la_" + name, shape, F32))

    Wq, Wkv, Wo = sb("Wq", [P, P]), sb("Wkv", [P, 2 * P]), sb("Wo", [P, P])
    W1, W2 = sb("W1", [P, 512]), sb("W2", [P, 4, D])
    colA, colB = sb("colA", [P, 3]), sb("colB", [P, 6])
    rowA, rowB = sb("rowA", [P, 5, P]), sb("rowB", [P, 3, P])
    rowF = sb("rowF", [P, 4, P])
    bq1, bk1 = sb("bq1", [P, 1]), sb("bk1", [P, 2, P])
    sumA, sumB = sb("sumA", [P, P]), sb("sumB", [P, P])
    z, base = sb("z", [P, NT, D]), sb("base", [P, NT, D])
    hT, qf = sb("hT", [P, NT * P]), sb("qf", [P, NT * P])
    kv = sb("kv", [P, NT, 2 * P + 1])
    q1, qe, ke = sb("q1", [P, 2, 512]), sb("qe", [P, 2, 512]), sb("ke", [P, 2, GT, P])
    KV = sb("KV", [P, B, P + HL1])
    den, rec = sb("den", [P, 2, GT, HL1]), sb("rec", [P, 2, GT, HL1])
    at = sb("at", [P, 2, GT, P])
    attT, h1T = sb("attT", [P, NT * P]), sb("h1T", [P, NT * P])
    ln0 = layernorm_steps(c, st, "la0", c.x, z)
    lna = layernorm_steps(c, st, "laa", base, z)
    lnb = layernorm_steps(c, st, "lab", base, z)
    lnf = layernorm_steps(c, st, "laf", base, z)
    mlp = mlp_buffers(c, st, "la", W1, colB[:, 2:6], W2, h1T)
    s = {n: c.sem("la_" + n) for n in (
        "wA", "wB", "wF", "ones", "prepA", "prepB", "tr", "hT", "g0", "base1", "q", "q1", "qe", "qf",
        "kvp", "kv1", "ke", "kf", "s", "KV", "num", "den", "rec", "at", "tra", "att", "wo", "y1",
        "tr2", "h1T", "g1", "base2", "f0", "f1", "f2", "f3", "f4")}
    ps = c.ps
    NA, NB = 8, 5

    def token(t):
        return slice(t * P, (t + 1) * P)

    def pair(g, k):
        return ps[:, 2 * k + g % 2, 0:2 * (P + HL1)].rearrange("p (t n) -> p t n", t=2)

    def kslice(g):
        return kv[:, GT * g:GT * g + GT, 0:P]

    def add1(e, l, g):
        e.wait_ge(s["wo"], l * NG + g + 1)
        e.wait_ge(s["base1"], l * NG + g + 1)
        e.tensor_tensor(grp(base, g), grp(base, g), bank4(c, 4 + g % 2), ALU.add).then_inc(s["y1"], 1)
        e.wait_ge(s["y1"], l * NG + g + 1)

    with nc.Block() as block:
        @block.sync
        def _(e):
            def load_a(l):
                d = c.dram
                e.dma_start(Wq[:, :], d["la_Wq"][l]).then_inc(s["wA"], 16)
                e.dma_start(Wkv[:, :], d["la_Wkv"][l]).then_inc(s["wA"], 16)
                e.dma_start(Wo[:, :], d["la_Wo"][l]).then_inc(s["wA"], 16)
                e.dma_start(colA[:, :], d["la_colA"][l]).then_inc(s["wA"], 16)
                e.dma_start(rowA[:, :, :], d["la_rowA"][l].partition_broadcast(P)).then_inc(s["wA"], 16)

            def load_b(l):
                d = c.dram
                e.dma_start(W1[:, :], d["la_W1"][l]).then_inc(s["wB"], 16)
                e.dma_start(W2[:, :, :], d["la_W2"][l].rearrange("(f p) d -> p f d", p=P)).then_inc(s["wB"], 16)
                e.dma_start(colB[:, :], d["la_colB"][l]).then_inc(s["wB"], 16)
                e.dma_start(rowB[:, :, :], d["la_rowB"][l].partition_broadcast(P)).then_inc(s["wB"], 16)

            load_a(0)
            load_b(0)
            e.dma_start(rowF[:, :, :], c.dram["la_rowF"].partition_broadcast(P)).then_inc(s["wF"], 16)
            with e.Fori(0, NL1 - 1) as l:
                e.wait_ge(s["y1"], l * NG + NG)
                load_a(l + 1)
                e.wait_ge(mlp["out"], l * NG + NG + 2)
                load_b(l + 1)

        @block.gpsimd
        def _(e):
            e.memset(kv[:, :, 2 * P:2 * P + 1], 1.0).then_inc(s["ones"], 1)
            for g in range(NG):
                ln_rstd(c, e, ln0, g)
            with e.Fori(0, NL1) as l:
                e.wait_ge(s["wA"], l * 80 + 80)
                e.tensor_tensor(sumA[:, :], rowA[:, 1, :], rowA[:, 2, :], ALU.add).then_inc(s["prepA"], 1)
                for g in range(NG):
                    e.wait_ge(s["hT"], l * NG + g + 1)
                    e.tensor_tensor(grp(base, g), grp(z, g), rows4(rowA[:, 0, :]), ALU.mult).then_inc(s["g0"], 1)
                    e.wait_ge(s["g0"], l * NG + g + 1)
                    e.wait_ge(s["prepA"], l * 3 + 1)
                    e.tensor_tensor(grp(base, g), grp(base, g), rows4(sumA[:, :]), ALU.add).then_inc(s["base1"], 1)
                e.wait_ge(s["wB"], l * 64 + 64)
                e.tensor_tensor(sumB[:, :], rowB[:, 1, :], rowB[:, 2, :], ALU.add).then_inc(s["prepB"], 1)
                for g in range(NG):
                    ln_rstd(c, e, lna, g, l)
                for g in range(NG):
                    e.wait_ge(s["h1T"], l * NG + g + 5)
                    e.tensor_tensor(grp(base, g), grp(z, g), rows4(rowB[:, 0, :]), ALU.mult).then_inc(s["g1"], 1)
                    e.wait_ge(s["g1"], l * NG + g + 1)
                    e.wait_ge(s["prepB"], l + 1)
                    e.tensor_tensor(grp(base, g), grp(base, g), rows4(sumB[:, :]), ALU.add).then_inc(s["base2"], 1)
                for g in range(NG):
                    ln_rstd(c, e, lnb, g, l)
            for g in range(NG):
                ln_rstd(c, e, lnf, g)

        @block.vector
        def _(e):
            e.sem_inc(mlp["out"], 2)
            for g in range(NG):
                ln_stats(c, e, ln0, g)
                if g:
                    ln_apply(c, e, ln0, g - 1)
            ln_apply(c, e, ln0, NG - 1)
            e.wait_ge(ln0["out"], NT)
            e.sem_inc(lnb["out"], NT)

            def phi_q(l, g):
                e.wait_ge(s["qe"], l * NG + g + 1)
                e.scalar_tensor_tensor(qf[:, g * 512:(g + 1) * 512], qe[:, g % 2, :], 1.0, q1[:, g % 2, :],
                                       ALU.min, ALU.max).then_inc(s["qf"], 1)

            def phi_k(l, g):
                e.wait_ge(s["ke"], l * NG + g + 1)
                e.scalar_tensor_tensor(kslice(g), ke[:, g % 2], 1.0, kslice(g), ALU.min, ALU.max).then_inc(s["kf"], 1)

            with e.Fori(0, NL1) as l:
                e.wait_ge(s["wA"], l * 80 + 80)
                e.tensor_scalar(bq1[:, :], colA[:, 2:3], 1.0, None, ALU.add).then_inc(s["prepA"], 1)
                e.tensor_scalar(rowA[:, 3, :], rowA[:, 3, :], 1.0, None, ALU.add).then_inc(s["prepA"], 1)
                e.wait_ge(s["prepA"], l * 3 + 3)
                bkv = rowA[:, 3:5, :].rearrange("p a n -> p (a n)").unsqueeze(1).broadcast_to([P, 2, 2 * P])

                def biases(g):
                    e.wait_ge(s["q"], l * NG + g + 1)
                    if g >= 2:
                        e.wait_ge(s["qf"], l * NG + g - 1)
                    e.tensor_scalar(q1[:, g % 2, :], ps[:, g % 2, :], bq1[:, 0:1], None, ALU.add).then_inc(s["q1"], 1)
                    for k in range(2):
                        e.wait_ge(s["kvp"], l * 8 + 2 * g + k + 1)
                        e.tensor_tensor(kv[:, GT * g + 2 * k:GT * g + 2 * k + 2, 0:2 * P],
                                        ps[:, 2 + k, :].rearrange("p (t n) -> p t n", t=2), bkv, ALU.add)\
                            .then_inc(s["kv1"], 1)

                def states(b):
                    e.wait_ge(s["s"], l * B + b + 1)
                    e.tensor_tensor(KV[:, b, 0:P], ps[:, 4 + b, 0:P], c.blk, ALU.mult)
                    e.tensor_scalar(KV[:, b, P:P + HL1], c.blk[:, ::DL1], ps[:, 4 + b, P:P + 1], None, ALU.mult)\
                        .then_inc(s["KV"], 1)

                def divide(g):
                    e.wait_ge(s["num"], l * NG + g + 1)
                    if g >= 2:
                        e.wait_ge(s["tra"], l * NG + g - 1)
                    for k in range(2):
                        e.tensor_scalar(den[:, g % 2, 2 * k:2 * k + 2, :], pair(g, k)[:, :, P:P + HL1], 1e-6, None,
                                        ALU.add).then_inc(s["den"], 1)
                    e.wait_ge(s["den"], l * 2 * NG + 2 * g + 2)
                    e.reciprocal(rec[:, g % 2].rearrange("p t h -> p (t h)"),
                                 den[:, g % 2].rearrange("p t h -> p (t h)")).then_inc(s["rec"], 1)
                    e.wait_ge(s["rec"], l * NG + g + 1)
                    for k in range(2):
                        e.tensor_tensor(at[:, g % 2, 2 * k:2 * k + 2, :].rearrange("p t (h d) -> p t h d", d=DL1),
                                        pair(g, k)[:, :, 0:P].rearrange("p t (h d) -> p t h d", d=DL1),
                                        rec[:, g % 2, 2 * k:2 * k + 2, :].unsqueeze(3).broadcast_to([P, 2, HL1, DL1]),
                                        ALU.mult).then_inc(s["at"], 1)

                biases(0)
                biases(1)
                phi_q(l, 0)
                phi_k(l, 0)
                phi_q(l, 1)
                phi_k(l, 1)
                biases(2)
                phi_q(l, 2)
                phi_k(l, 2)
                biases(3)
                states(0)
                phi_q(l, 3)
                phi_k(l, 3)
                divide(0)
                states(1)
                divide(1)
                divide(2)
                add1(e, l, 0)
                ln_stats(c, e, lna, 0, l)
                divide(3)
                for g in range(1, NG):
                    ln_apply(c, e, lna, g - 1, l)
                    add1(e, l, g)
                    ln_stats(c, e, lna, g, l)
                ln_apply(c, e, lna, NG - 1, l)
                for g in range(NG):
                    e.wait_ge(mlp["down"], l * NG + g + 1)
                    e.wait_ge(s["base2"], l * NG + g + 1)
                    e.tensor_tensor(grp(base, g), grp(base, g), bank4(c, 4 + g % 2), ALU.add).then_inc(mlp["out"], 1)
                    e.wait_ge(mlp["out"], l * NG + g + 3)
                    ln_stats(c, e, lnb, g, l)
                    if g:
                        ln_apply(c, e, lnb, g - 1, l)
                ln_apply(c, e, lnb, NG - 1, l)
            e.wait_ge(s["wF"], 16)
            e.wait_ge(lnb["out"], NT * NL1 + NT)
            for g in range(NG):
                e.tensor_tensor(grp(base, g), grp(z, g), rows4(rowF[:, 0, :]), ALU.mult).then_inc(s["f0"], 1)
                e.wait_ge(s["f0"], g + 1)
                e.tensor_tensor(grp(base, g), grp(base, g), rows4(rowF[:, 1, :]), ALU.add).then_inc(s["f1"], 1)
                e.wait_ge(s["f1"], g + 1)
                ln_stats(c, e, lnf, g)
                if g:
                    ln_apply(c, e, lnf, g - 1)
            ln_apply(c, e, lnf, NG - 1)
            for g in range(NG):
                e.wait_ge(lnf["out"], GT * g + GT)
                e.tensor_tensor(grp(z, g), grp(z, g), rows4(rowF[:, 2, :]), ALU.mult).then_inc(s["f2"], 1)
                e.wait_ge(s["f2"], g + 1)
                e.tensor_tensor(grp(z, g), grp(z, g), rows4(rowF[:, 3, :]), ALU.add).then_inc(s["f3"], 1)
                e.wait_ge(s["f3"], g + 1)
                e.tensor_tensor(grp(c.x, g), grp(c.x, g), grp(z, g), ALU.add).then_inc(s["f4"], 1)

        @block.tensor
        def _(e):
            e.wait_ge(s["ones"], 1)
            with e.Fori(0, NL1) as l:
                n = l * NG

                def turn(g):
                    e.wait_ge(lnb["out"], l * NT + GT * g + GT)
                    if g == 0:
                        e.wait_ge(s["h1T"], n + 4)
                    if g >= 2:
                        e.wait_ge(s["hT"], n + g - 1)
                    transpose_group(c, e, z, 6 + g % 2, g).then_inc(s["tr"], 1)

                def qkv(g):
                    e.wait_ge(s["hT"], n + g + 1)
                    if g >= 2:
                        e.wait_ge(s["q1"], n + g - 1)
                    e.matmul(ps[:, g % 2, :], Wq[:, :], hT[:, g * 512:(g + 1) * 512], start=True, stop=True)\
                        .then_inc(s["q"], 1)
                    for k in range(2):
                        if g:
                            e.wait_ge(s["kv1"], l * 8 + 2 * g + k - 1)
                        for t in range(2):
                            ins = e.matmul(ps[:, 2 + k, t * 256:(t + 1) * 256], hT[:, token(GT * g + 2 * k + t)],
                                           Wkv[:, :], start=True, stop=True)
                        ins.then_inc(s["kvp"], 1)

                def state(b):
                    e.wait_ge(s["kf"], n + 2 * b + 2)
                    for t in range(TPB):
                        ins = e.matmul(ps[:, 4 + b, 0:P + 1], kv[:, b * TPB + t, 0:P], kv[:, b * TPB + t, P:2 * P + 1],
                                       start=(t == 0), stop=(t == TPB - 1))
                    ins.then_inc(s["s"], 1)

                def attend(g):
                    b = g // (NG // B)
                    e.wait_ge(s["KV"], l * B + b + 1)
                    e.wait_ge(s["qf"], n + g + 1)
                    if g < 2:
                        e.wait_ge(s["q1"], n + 4)
                        e.wait_ge(s["kv1"], l * 8 + 8)
                    else:
                        e.wait_ge(s["at"], 2 * (n + g) - 2)
                    for t in range(GT):
                        ins = e.matmul(pair(g, t // 2)[:, t % 2, :], qf[:, token(GT * g + t)], KV[:, b, :],
                                       start=True, stop=True)
                    ins.then_inc(s["num"], 1)

                def turn_att(g):
                    e.wait_ge(s["at"], 2 * (n + g) + 2)
                    if g < 2:
                        e.wait_ge(s["hT"], n + g + 3)
                    else:
                        e.wait_ge(s["att"], n + g - 1)
                    for t in range(GT):
                        ins = e.transpose(ps[:, 6 + g % 2, t * P:(t + 1) * P], at[:, g % 2, t, :], c.ident)
                    ins.then_inc(s["tra"], 1)

                def project(g):
                    e.wait_ge(s["att"], n + g + 1)
                    if g >= 2:
                        e.wait_ge(s["y1"], n + g - 1)
                    else:
                        e.wait_ge(s["KV"], l * B + g + 1)
                    for t in range(GT):
                        ins = e.matmul(ps[:, 4 + g % 2, t * P:(t + 1) * P], attT[:, token(GT * g + t)], Wo[:, :],
                                       start=True, stop=True)
                    ins.then_inc(s["wo"], 1)

                def turn2(g):
                    e.wait_ge(lna["out"], l * NT + GT * g + GT)
                    if g >= 2:
                        e.wait_ge(s["h1T"], n + g + 3)
                    else:
                        e.wait_ge(s["att"], n + g + 3)
                    transpose_group(c, e, z, 6 + g % 2, g).then_inc(s["tr2"], 1)

                def up(g):
                    e.wait_ge(s["h1T"], n + g + 5)
                    mlp_up(c, e, mlp, g, n + g)

                def down(g):
                    if g < 2:
                        e.wait_ge(s["y1"], n + g + 3)
                    mlp_down(c, e, mlp, g, n + g)

                e.wait_ge(s["wA"], l * 80 + 80)
                turn(0)
                turn(1)
                qkv(0)
                turn(2)
                qkv(1)
                turn(3)
                qkv(2)
                qkv(3)
                state(0)
                attend(0)
                attend(1)
                state(1)
                turn_att(0)
                attend(2)
                project(0)
                turn_att(1)
                attend(3)
                project(1)
                turn_att(2)
                project(2)
                turn_att(3)
                turn2(0)
                e.wait_ge(s["wB"], l * 64 + 64)
                up(0)
                turn2(1)
                project(3)
                up(1)
                turn2(2)
                down(0)
                turn2(3)
                up(2)
                down(1)
                up(3)
                down(2)
                down(3)

        @block.scalar
        def _(e):
            mlp_credits(e, mlp)
            e.sem_inc(s["h1T"], 4)
            with e.Fori(0, NL1) as l:
                n = l * NG

                def take(g):
                    e.wait_ge(s["tr"], n + g + 1)
                    e.activation(hT[:, g * 512:(g + 1) * 512], ps[:, 6 + g % 2, :], ACT.Identity,
                                 bias=colA[:, 1:2], scale=colA[:, 0:1]).then_inc(s["hT"], 1)

                def exps(g):
                    e.wait_ge(s["q1"], n + g + 1)
                    e.activation(qe[:, g % 2, :], q1[:, g % 2, :], ACT.Exp, bias=c.neg_one[:, 0:1]).then_inc(s["qe"], 1)
                    e.wait_ge(s["kv1"], l * 8 + 2 * g + 2)
                    e.activation(ke[:, g % 2], kslice(g), ACT.Exp, bias=c.neg_one[:, 0:1]).then_inc(s["ke"], 1)

                e.wait_ge(s["wA"], l * 80 + 80)
                take(0)
                take(1)
                exps(0)
                exps(1)
                take(2)
                take(3)
                exps(2)
                exps(3)
                for g in range(NG):
                    e.wait_ge(s["tra"], n + g + 1)
                    e.activation(attT[:, g * 512:(g + 1) * 512], ps[:, 6 + g % 2, :], ACT.Copy).then_inc(s["att"], 1)
                e.wait_ge(s["wB"], l * 64 + 64)
                for g in range(NG):
                    e.wait_ge(s["tr2"], n + g + 1)
                    e.activation(h1T[:, g * 512:(g + 1) * 512], ps[:, 6 + g % 2, :], ACT.Identity,
                                 bias=colB[:, 1:2], scale=colB[:, 0:1]).then_inc(s["h1T"], 1)
                    if g:
                        mlp_act(c, e, mlp, g - 1, n + g - 1)
                mlp_act(c, e, mlp, NG - 1, n + NG - 1)


HB, DH = 16, 8
HQ = 4
PQ = [0, 0, 1, 1, 0, 2, 1, 2]
PK = [0, 1, 0, 1, 2, 0, 2, 1]


def spread_matrices():
    m = np.zeros((P, 2, 3, HB // 2, P), np.uint16)
    for j in range(HB // 2):
        for hp in range(2):
            for k in range(8):
                for d in range(DH):
                    f, r = (2 * j + hp) * DH + d, hp * 64 + k * DH + d
                    m[f, 0, PQ[k], j, r] = 0x3F80
                    m[f, 1, PK[k], j, r] = 0x3F80
    return m.reshape(P, -1)


def query_attention_project(c, st, a, parts, v, spread):
    nc = c.nc

    def sb(name, shape, dt=F32):
        return st.enter_context(nc.sbuf_tensor("qp_" + name, shape, dt))

    aT, W, cols, vrow = sb("aT", [P, NT * P]), sb("W", [P, 3, P]), sb("cols", [P, 2]), sb("vrow", [P, P])
    xf, r1 = sb("xf", [P, 2, 512]), sb("r1", [P, 2, 512])
    ln = layernorm_steps(c, st, "qp", c.x, a)
    s = {n: c.sem("qp_" + n) for n in ("loaded", "spread", "turned", "aT", "qk", "xf", "p0", "r1", "p1", "p2", "vp", "v")}
    ps = c.ps
    with nc.Block() as block:
        @block.sync
        def _(e):
            e.dma_start(W[:, :, :], c.dram["qa_WT"].rearrange("p (a n) -> p a n", a=3)).then_inc(s["loaded"], 16)
            e.dma_start(cols[:, :], c.dram["qa_cols"]).then_inc(s["loaded"], 16)
            e.dma_start(vrow[:, :], c.dram["qa_vrow"].partition_broadcast(P)).then_inc(s["loaded"], 16)
            e.dma_start(spread[:, :], c.dram["spread"]).then_inc(s["spread"], 16)
            e.wait_ge(s["spread"], 16)

        @block.gpsimd
        def _(e):
            for g in range(NG):
                ln_rstd(c, e, ln, g)

        @block.vector
        def _(e):
            for g in range(NG):
                ln_stats(c, e, ln, g)
                if g:
                    ln_apply(c, e, ln, g - 1)
            ln_apply(c, e, ln, NG - 1)
            e.wait_ge(s["loaded"], 48)
            for g in range(NG):
                for k in range(2):
                    m = 2 * g + k
                    e.wait_ge(s["qk"], m + 1)
                    if m >= 2:
                        e.wait_ge(s["p0"], m - 1)
                    e.tensor_scalar(xf[:, k, :], ps[:, k, :], cols[:, k:k + 1], DH ** -0.5 if k == 0 else 1.0,
                                    ALU.add, ALU.mult).then_inc(s["xf"], 1)
                for k in range(2):
                    m = 2 * g + k
                    e.wait_ge(s["p0"], m + 1)
                    e.tensor_tensor(r1[:, k, :], xf[:, k, :], parts[:, k, 0, g * 512:(g + 1) * 512], ALU.subtract)\
                        .then_inc(s["r1"], 1)
                for k in range(2):
                    m = 2 * g + k
                    e.wait_ge(s["p1"], m + 1)
                    e.tensor_tensor(parts[:, k, 2, g * 512:(g + 1) * 512], r1[:, k, :],
                                    parts[:, k, 1, g * 512:(g + 1) * 512], ALU.subtract).then_inc(s["p2"], 1)
                e.wait_ge(s["vp"], g + 1)
                e.tensor_tensor(grp(v, g), bank4(c, 2 + g % 2), rows4(vrow[:, :]), ALU.add).then_inc(s["v"], 1)

        @block.tensor
        def _(e):
            for g in range(NG):
                e.wait_ge(ln["out"], GT * g + GT)
                if g >= 2:
                    e.wait_ge(s["aT"], g - 1)
                transpose_group(c, e, a, 6 + g % 2, g).then_inc(s["turned"], 1)
            e.wait_ge(s["loaded"], 48)
            for g in range(NG):
                e.wait_ge(s["aT"], g + 1)
                for k in range(2):
                    if g:
                        e.wait_ge(s["xf"], 2 * g + k - 1)
                    e.matmul(ps[:, k, :], W[:, k, :], aT[:, g * 512:(g + 1) * 512], start=True, stop=True)\
                        .then_inc(s["qk"], 1)
                if g >= 2:
                    e.wait_ge(s["v"], g - 1)
                for t in range(GT):
                    ins = e.matmul(ps[:, 2 + g % 2, t * P:(t + 1) * P], aT[:, (GT * g + t) * P:(GT * g + t + 1) * P],
                                   W[:, 2, :], start=True, stop=True)
                ins.then_inc(s["vp"], 1)

        @block.scalar
        def _(e):
            for g in range(NG):
                e.wait_ge(s["turned"], g + 1)
                e.activation(aT[:, g * 512:(g + 1) * 512], ps[:, 6 + g % 2, :], ACT.Copy).then_inc(s["aT"], 1)
            for g in range(NG):
                for k in range(2):
                    e.wait_ge(s["xf"], 2 * g + k + 1)
                    e.activation(parts[:, k, 0, g * 512:(g + 1) * 512], xf[:, k, :], ACT.Copy).then_inc(s["p0"], 1)
                for k in range(2):
                    e.wait_ge(s["r1"], 2 * g + k + 1)
                    e.activation(parts[:, k, 1, g * 512:(g + 1) * 512], r1[:, k, :], ACT.Copy).then_inc(s["p1"], 1)


def query_attention_core(c, st, parts, v, post, spread):
    nc = c.nc

    def sb(name, shape, dt=F32):
        return st.enter_context(nc.sbuf_tensor("qc_" + name, shape, dt))

    qs, ks = sb("qs", [P, B, 2, T], BF16), sb("ks", [P, B, 2, T], BF16)
    E = sb("E", [P, 3, HQ, T])
    vz = sb("vz", [P, 3, HQ, 32])
    mx, zs, rz = sb("mx", [P, 8]), sb("zs", [P, 8]), sb("rz", [P, 8])
    s = {n: c.sem("qc_" + n) for n in (
        "vz0", "first", "firstd", "filled", "mx", "drained", "rz", "vz", "pv", "post")}
    ps = c.ps
    NHQ = HB // HQ
    NTL, NU = B * TPB, B * TPB * HQ
    order = []
    for u in range(NU):
        order.append(("unit", u))
        w = u % (TPB * HQ)
        if w % 8 == 1:
            order.append(("stack", u // (TPB * HQ), w // 8))
    NFILL = len(order)
    assert NFILL % 3 == 0
    pos = {o[1]: f for f, o in enumerate(order) if o[0] == "unit"}

    def slot(f):
        return ps[:, 2 * (f % 3):2 * (f % 3) + 2, :].rearrange("p a n -> p (a n)")

    with nc.Block() as block:
        @block.gpsimd
        def _(e):
            e.memset(vz[:, :, :, :], 0.0).then_inc(s["vz0"], 1)

        @block.scalar
        def _(e):
            e.sem_inc(s["post"], 1)
            e.sem_inc(s["drained"], 3)
            for k in range(4):
                e.wait_ge(s["first"], k + 1)
                e.activation((qs, ks)[k // 2][:, 0, k % 2, :], slot(k), ACT.Copy).then_inc(s["firstd"], 1)
            with e.Fori(0, NHQ) as hq:
                def save(b):
                    e.wait_ge(s["pv"], hq * NTL + (b + 1) * TPB)
                    e.activation(post[:, bass.ds(hq * 2 + b, 1), :].rearrange("p a t -> p (a t)"),
                                 ps[:, 6:8, :].rearrange("p a n -> p (a n)"), ACT.Copy).then_inc(s["post"], 1)

                for f, o in enumerate(order):
                    if o[0] == "stack":
                        b, k = o[1:]
                        e.wait_ge(s["filled"], hq * NFILL + f + 1)
                        e.activation((qs, ks)[k // 2][:, (b + 1) % B, k % 2, :], slot(f), ACT.Copy)\
                            .then_inc(s["drained"], 1)
                        continue
                    u = o[1]
                    t, h = u // HQ, u % HQ
                    e.wait_ge(s["mx"], hq * NU + u + 1)
                    if t >= 3 and h == 0:
                        e.wait_ge(s["pv"], hq * NTL + t - 2)
                    e.activation(E[:, t % 3, h, :], slot(f), ACT.Exp, bias=mx[:, u % 8:u % 8 + 1],
                                 accum_out=zs[:, u % 8:u % 8 + 1]).then_inc(s["drained"], 1)
                    if u % (TPB * HQ) == 4 and t >= TPB:
                        save(t // TPB - 1)
                save(B - 1)

        @block.vector
        def _(e):
            e.wait_ge(s["vz0"], 1)
            with e.Fori(0, NHQ) as hq:
                def weight(t):
                    r = slice(HQ * (t % 2), HQ * (t % 2) + HQ)
                    e.wait_ge(s["drained"], hq * NFILL + pos[HQ * t + HQ - 1] + 4)
                    e.reciprocal(rz[:, r], zs[:, r]).then_inc(s["rz"], 1)
                    e.wait_ge(s["rz"], hq * NTL + t + 1)
                    if t >= 3:
                        e.wait_ge(s["pv"], hq * NTL + t - 2)
                    e.tensor_tensor(vz[:, t % 3, :, 0:DH],
                                    v[:, t, bass.ds(hq * (HQ * DH), HQ * DH)].rearrange("p (h d) -> p h d", d=DH),
                                    rz[:, r].unsqueeze(2).broadcast_to([P, HQ, DH]), ALU.mult).then_inc(s["vz"], 1)

                for u in range(NU):
                    e.wait_ge(s["filled"], hq * NFILL + pos[u] + 1)
                    e.tensor_reduce(mx[:, u % 8:u % 8 + 1], slot(pos[u]), AX, ALU.max, negate=True).then_inc(s["mx"], 1)
                    if u % HQ == 1 and u >= HQ:
                        weight(u // HQ - 1)
                weight(NTL - 1)

        @block.tensor
        def _(e):
            def stack(f, dst, pair, hq, b, done):
                for half in range(2):
                    for p in range(3):
                        row = (dst * 3 + p) * (HB // 2) * P + pair * P
                        ins = e.matmul(ps[:, 2 * (f % 3) + half, :], spread[:, bass.ds(hq * (2 * P) + row, P)],
                                       parts[:, dst, p, b * T + half * 512:b * T + half * 512 + 512],
                                       start=(p == 0), stop=(p == 2))
                ins.then_inc(done, 1)

            for k in range(4):
                if k == 3:
                    e.wait_ge(s["firstd"], 1)
                stack(k, k // 2, k % 2, 0, 0, s["first"])
            e.wait_ge(s["firstd"], 4)
            with e.Fori(0, NHQ) as hq:
                def scores(f, u):
                    t, h = u // HQ, u % HQ
                    r = slice(64 * (h % 2), 64 * (h % 2) + 64)
                    for half in range(2):
                        ins = e.matmul(ps[:, 2 * (f % 3) + half, :],
                                       ks[r, t // TPB, h // 2, (t % TPB) * P:(t % TPB) * P + P],
                                       qs[r, t // TPB, h // 2, half * 512:(half + 1) * 512], start=True, stop=True)
                    ins.then_inc(s["filled"], 1)

                def weigh(t, half):
                    e.wait_ge(s["vz"], hq * NTL + t + 1)
                    if t % TPB == 0:
                        e.wait_ge(s["post"], hq * B + t // TPB + 1)
                    for h in range(HQ):
                        ins = e.matmul(ps[32 * h:32 * h + 32, 6 + half, :], vz[:, t % 3, h, :],
                                       E[:, t % 3, h, half * 512:(half + 1) * 512],
                                       start=(t % TPB == 0), stop=(t % TPB == TPB - 1))
                    if half:
                        ins.then_inc(s["pv"], 1)

                for f, o in enumerate(order):
                    e.wait_ge(s["drained"], hq * NFILL + f + 1)
                    if o[0] == "stack":
                        b, k = o[1:]
                        stack(f, k // 2, k % 2, hq if b + 1 < B else (hq + 1) % NHQ, (b + 1) % B, s["filled"])
                        continue
                    u = o[1]
                    scores(f, u)
                    if u >= HQ + 3 and u % HQ == 3:
                        weigh(u // HQ - 1, 0)
                    if u >= 2 * HQ and u % HQ == 0:
                        weigh(u // HQ - 2, 1)
                weigh(NTL - 2, 1)
                weigh(NTL - 1, 0)
                weigh(NTL - 1, 1)


def query_attention_finish(c, st, a, post):
    nc = c.nc

    def sb(name, shape):
        return st.enter_context(nc.sbuf_tensor("qf_" + name, shape, F32))

    Wo, W1, W2 = sb("Wo", [P, HB // HQ, D]), sb("W1", [P, 512]), sb("W2", [P, 4, D])
    cols, rows, sumr = sb("cols", [P, 6]), sb("rows", [P, 6, P]), sb("sum", [P, P])
    z, h1T = sb("z", [P, NT, D]), sb("h1T", [P, NT * P])
    lna = layernorm_steps(c, st, "qfa", a, z)
    lnb = layernorm_steps(c, st, "qfb", a, z)
    mlp = mlp_buffers(c, st, "qf", W1, cols[:, 2:6], W2, h1T)
    s = {n: c.sem("qf_" + n) for n in (
        "loaded", "wo", "sum", "gelu", "o", "based", "y1", "tr", "h1T", "g1", "base2", "o1", "o2", "o3")}
    ps = c.ps
    NH = HB // HQ

    def add1(e, g):
        e.wait_ge(s["o"], g + 1)
        e.wait_ge(s["based"], g + 1)
        e.tensor_tensor(grp(a, g), grp(a, g), bank4(c, 4 + g % 2), ALU.add).then_inc(s["y1"], 1)
        e.wait_ge(s["y1"], g + 1)

    with nc.Block() as block:
        @block.sync
        def _(e):
            d = c.dram
            e.dma_start(Wo[:, :, :], d["qa_WoT"]).then_inc(s["loaded"], 16)
            e.dma_start(W1[:, :], d["qa_W1T"]).then_inc(s["loaded"], 16)
            e.dma_start(W2[:, :, :], d["qa_W2T"].rearrange("(f p) d -> p f d", p=P)).then_inc(s["loaded"], 16)
            e.dma_start(cols[:, :], d["qa_mcols"]).then_inc(s["loaded"], 16)
            e.dma_start(rows[:, :, :], d["qa_rows"].partition_broadcast(P)).then_inc(s["loaded"], 16)

        @block.gpsimd
        def _(e):
            e.wait_ge(s["loaded"], 80)
            e.tensor_tensor(sumr[:, :], rows[:, 2, :], rows[:, 3, :], ALU.add).then_inc(s["sum"], 1)
            for g in range(NG):
                e.tensor_tensor(grp(a, g), grp(a, g), rows4(rows[:, 0, :]), ALU.add).then_inc(s["based"], 1)
            for g in range(NG):
                ln_rstd(c, e, lna, g)
            e.wait_ge(s["sum"], 1)
            for g in range(NG):
                e.wait_ge(lna["out"], GT * g + GT)
                e.tensor_tensor(grp(a, g), grp(z, g), rows4(rows[:, 1, :]), ALU.mult).then_inc(s["g1"], 1)
                e.wait_ge(s["g1"], g + 1)
                e.tensor_tensor(grp(a, g), grp(a, g), rows4(sumr[:, :]), ALU.add).then_inc(s["base2"], 1)
            for g in range(NG):
                ln_rstd(c, e, lnb, g)

        @block.vector
        def _(e):
            def finish(g):
                ln_apply(c, e, lnb, g)
                e.wait_ge(lnb["out"], GT * g + GT)
                e.tensor_tensor(grp(z, g), grp(z, g), rows4(rows[:, 4, :]), ALU.mult).then_inc(s["o1"], 1)
                e.wait_ge(s["o1"], g + 1)
                e.tensor_tensor(grp(z, g), grp(z, g), rows4(rows[:, 5, :]), ALU.add).then_inc(s["o2"], 1)
                e.wait_ge(s["o2"], g + 1)
                e.tensor_tensor(grp(c.x, g), grp(c.x, g), grp(z, g), ALU.add).then_inc(s["o3"], 1)

            e.sem_inc(mlp["out"], 2)
            e.wait_ge(s["loaded"], 80)
            e.tensor_scalar(Wo[:, :, :], Wo[:, :, :], T ** -0.5, None, ALU.mult).then_inc(s["wo"], 1)
            for g in range(NG):
                add1(e, g)
                ln_stats(c, e, lna, g)
                if g:
                    ln_apply(c, e, lna, g - 1)
            ln_apply(c, e, lna, NG - 1)
            for g in range(NG):
                e.wait_ge(mlp["down"], g + 1)
                e.wait_ge(s["base2"], g + 1)
                e.tensor_tensor(grp(a, g), grp(a, g), bank4(c, 4 + g % 2), ALU.add).then_inc(mlp["out"], 1)
                e.wait_ge(mlp["out"], g + 3)
                ln_stats(c, e, lnb, g)
                if g:
                    finish(g - 1)
            finish(NG - 1)

        @block.tensor
        def _(e):
            e.wait_ge(s["wo"], 1)
            for g in range(NG):
                if g >= 2:
                    e.wait_ge(s["y1"], g - 1)
                b = g // (NG // B)
                e.wait_ge(s["gelu"], NH * (g + 1))
                for t in range(GT):
                    tok = ((g % (NG // B)) * GT + t) * P
                    for h in range(NH):
                        ins = e.matmul(ps[:, 4 + g % 2, t * P:(t + 1) * P], post[:, 2 * h + b, tok:tok + P], Wo[:, h, :],
                                       start=(h == 0), stop=(h == NH - 1))
                ins.then_inc(s["o"], 1)
            e.wait_ge(s["y1"], NG)

            def turn(g):
                e.wait_ge(lna["out"], GT * g + GT)
                if g >= 2:
                    e.wait_ge(s["h1T"], g - 1)
                transpose_group(c, e, z, 6 + g % 2, g).then_inc(s["tr"], 1)

            turn(0)
            for g in range(NG):
                if g + 1 < NG:
                    turn(g + 1)
                e.wait_ge(s["h1T"], g + 1)
                mlp_up(c, e, mlp, g, g)
                if g:
                    mlp_down(c, e, mlp, g - 1, g - 1)
            mlp_down(c, e, mlp, NG - 1, NG - 1)

        @block.scalar
        def _(e):
            mlp_credits(e, mlp)
            for g in range(NG):
                b, half = g // (NG // B), g % (NG // B)
                for h in range(NH):
                    part = post[:, 2 * h + b, half * 512:(half + 1) * 512]
                    e.activation(part, part, ACT.Gelu).then_inc(s["gelu"], 1)
            e.wait_ge(s["loaded"], 80)

            def take(g):
                e.wait_ge(s["tr"], g + 1)
                e.activation(h1T[:, g * 512:(g + 1) * 512], ps[:, 6 + g % 2, :], ACT.Identity,
                             bias=cols[:, 1:2], scale=cols[:, 0:1]).then_inc(s["h1T"], 1)

            take(0)
            for g in range(NG):
                if g + 1 < NG:
                    take(g + 1)
                mlp_act(c, e, mlp, g, g)


def program(nc, dram, out):
    with ExitStack() as ctx:
        c = Core(nc, ctx, dram)
        c.x = ctx.enter_context(nc.sbuf_tensor("x_res", [P, NT, D], F32))
        c.const = ctx.enter_context(nc.sbuf_tensor("const", [P, C_END], F32))
        c.wgu = ctx.enter_context(nc.sbuf_tensor("wgu", [P, 2 * FQ], F32))
        c.wd = ctx.enter_context(nc.sbuf_tensor("wd", [P, 3, D], F32))
        c.neg_half = ctx.enter_context(nc.sbuf_tensor("neg_half", [P, 16], F32))
        c.neg_one = ctx.enter_context(nc.sbuf_tensor("neg_one", [P, 1], F32))
        c.ps = ctx.enter_context(nc.psum_tensor("ps", [P, 8, 512], F32))
        c.ident = c.const[:, C_ID:C_ID + P]
        c.utri = c.const[:, C_UTRI:C_UTRI + P]
        c.gt = c.const[:, C_GT:C_GT + P]
        c.ones = c.const[:, C_ONES:C_ONES + P]
        c.blk = c.const[:, C_BLK:C_BLK + P]
        c.m0 = c.const[:, C_M0:C_M0 + P]
        c.lv = c.const[:, C_LV:C_LV + 64 * len(LEVELS)].rearrange("p (l n) -> p l n", n=64)
        c.rst = c.const[:, C_RST:C_RST + 512]
        c.sel = c.const[:, C_SEL:C_SEL + 32]
        load_phase(c)
        c.end_phase()
        with ExitStack() as st:
            x1 = st.enter_context(nc.sbuf_tensor("x1", [P, NT, D], F32))
            with ExitStack() as s1:
                nT = s1.enter_context(nc.sbuf_tensor("nT", [P, NT * P], F32))
                w = gdn_weights(c, s1)
                with ExitStack() as s2:
                    gdn_norm_phase(c, s2, x1, nT, w)
                    c.end_phase()
                with ExitStack() as s2:
                    gdn_phase(c, s2, x1, nT, w)
                    c.end_phase()
            with ExitStack() as s1:
                gdn_mlp_phase(c, s1, x1)
                c.end_phase()
        with ExitStack() as st:
            moe_phase(c, st, "moe0")
            c.end_phase()
        with ExitStack() as st:
            ssm_phase(c, st)
            c.end_phase()
        with ExitStack() as st:
            moe_phase(c, st, "moe1")
            c.end_phase()
        with ExitStack() as st:
            linear_attention_phase(c, st)
            c.end_phase()
        with ExitStack() as st:
            fp4_phase(c, st, "fp0")
            c.end_phase()
        with ExitStack() as st:
            a = st.enter_context(nc.sbuf_tensor("qa_a", [P, NT, D], F32))
            post = st.enter_context(nc.sbuf_tensor("qa_post", [P, 2 * HB // HQ, T], F32))
            with ExitStack() as s1:
                parts = s1.enter_context(nc.sbuf_tensor("qa_parts", [P, 2, 3, NT * P], BF16))
                v = s1.enter_context(nc.sbuf_tensor("qa_v", [P, NT, D], F32))
                spread = s1.enter_context(nc.sbuf_tensor("qa_spread", [P, 2 * 3 * (HB // 2) * P], mybir.dt.uint16))
                with ExitStack() as s2:
                    query_attention_project(c, s2, a, parts, v, spread)
                    c.end_phase()
                with ExitStack() as s2:
                    query_attention_core(c, s2, parts, v, post, spread[:, :].bitcast(BF16))
                    c.end_phase()
            with ExitStack() as s1:
                query_attention_finish(c, s1, a, post)
                c.end_phase()
        with ExitStack() as st:
            fp4_phase(c, st, "fp1")
            c.end_phase()
        store_phase(c, out)


def gdn_weights(c, st):
    nc = c.nc
    w = {n: st.enter_context(nc.sbuf_tensor("gdn_w" + n, [P, H * P], F32)) for n in "qkv"}
    w["ba"] = st.enter_context(nc.sbuf_tensor("gdn_wba", [P, 16], F32))
    w["o"] = st.enter_context(nc.sbuf_tensor("gdn_wo", [P, H, P], F32))
    w["ln1"] = st.enter_context(nc.sbuf_tensor("gdn_vec", [P, 2], F32))
    return w


def store_phase(c, out):
    stored = c.sem("stored")
    with c.nc.Block() as block:
        @block.sync
        def _(e):
            e.dma_start(out.rearrange("b (t p) d -> p (b t) d", p=P), c.x[:, :, :]).then_inc(stored, 16)
            e.wait_ge(stored, 16)


def layout(inputs):
    i = {k: np.asarray(v) for k, v in inputs.items()}
    f = lambda n: i[n]
    units = lambda w: w.transpose(1, 0, 2).reshape(D, NHC, P).transpose(1, 0, 2)
    gin = np.concatenate([np.ones((1, D), np.float32), f("L1_attn_a_g2")[:-1]])
    bein = np.concatenate([np.zeros((1, D), np.float32), f("L1_attn_a_be2")[:-1]])
    qw, qb = f("L1_attn_b_in_proj_w"), f("L1_attn_b_in_proj_b")
    wo = np.zeros((HQ, 32, HB // HQ, D), np.float32)
    wo[:, 0:DH] = f("L1_attn_b_out_w").T.reshape(HB // HQ, HQ, DH, D).transpose(1, 2, 0, 3)
    wo = wo.reshape(P, HB // HQ, D)
    return {
        "consts": constants(),
        "x": f("L0_attn_a_x"),
        "L0a_Wq": f("L0_attn_a_Wq"), "L0a_Wk": f("L0_attn_a_Wk"), "L0a_Wv": f("L0_attn_a_Wv"),
        "L0a_Wba": np.concatenate([f("L0_attn_a_Wb"), f("L0_attn_a_Wa")], axis=1),
        "L0a_Wo": f("L0_attn_a_Wo"),
        "L0a_W1": f("L0_attn_a_W1"), "L0a_W2": f("L0_attn_a_W2"), "L0a_b2": f("L0_attn_a_b2"),
        "L0a_cols": np.concatenate([f("L0_attn_a_ln2_w")[:, None], f("L0_attn_a_ln2_b")[:, None],
                                    f("L0_attn_a_b1").reshape(4, P).T], axis=1),
        "moe_gateT": f("L0_ffn_gate_w").T, "moe_ebias": f("L0_ffn_e_bias"),
        "moe_w13": np.concatenate([units(f("L0_ffn_w1")), units(f("L0_ffn_w3"))], axis=2),
        "moe_w2": f("L0_ffn_w2").reshape(NHC, P, D),
        "ssm_BT": f("L0_attn_b_B_w").T, "ssm_CT": f("L0_attn_b_C_w").T,
        "ssm_loglam": f("L0_attn_b_log_lambda")[:, None],
        "ssm_cols": np.stack([f("L0_attn_b_ssm_norm_w"), f("L0_attn_b_D_skip"), f("L0_attn_b_ffn_norm_w")], axis=1),
        "ssm_W1T": f("L0_attn_b_w1").T, "ssm_W3T": f("L0_attn_b_w3").T, "ssm_W2T": f("L0_attn_b_w2").T,
        "fp4_gate": f("L1_ffn_w_gate"), "fp4_up": f("L1_ffn_w_up"), "fp4_down": f("L1_ffn_w_down"),
        "la_Wq": f("L1_attn_a_Wq"), "la_Wkv": np.concatenate([f("L1_attn_a_Wk"), f("L1_attn_a_Wv")], axis=2),
        "la_Wo": f("L1_attn_a_Wo"), "la_W1": f("L1_attn_a_W1"), "la_W2": f("L1_attn_a_W2"),
        "la_colA": np.stack([gin, bein, f("L1_attn_a_bq")], axis=2),
        "la_rowA": np.stack([gin, bein, f("L1_attn_a_bo"), f("L1_attn_a_bk"), f("L1_attn_a_bv")], axis=1),
        "la_colB": np.concatenate([f("L1_attn_a_g1")[:, :, None], f("L1_attn_a_be1")[:, :, None],
                                   f("L1_attn_a_c1").reshape(NL1, 4, P).transpose(0, 2, 1)], axis=2),
        "la_rowB": np.stack([f("L1_attn_a_g1"), f("L1_attn_a_be1"), f("L1_attn_a_c2")], axis=1),
        "la_rowF": np.stack([f("L1_attn_a_g2")[-1], f("L1_attn_a_be2")[-1], f("L1_attn_a_gf"), f("L1_attn_a_bef")]),
        "qa_WT": np.concatenate([qw[k * P:(k + 1) * P].T for k in range(3)], axis=1),
        "qa_cols": np.stack([qb[0:P], qb[P:2 * P]], axis=1), "qa_vrow": qb[2 * P:3 * P],
        "qa_WoT": wo, "qa_W1T": f("L1_attn_b_lin1_w").T, "qa_W2T": f("L1_attn_b_lin2_w").T,
        "qa_mcols": np.concatenate([f("L1_attn_b_ln1_g")[:, None], f("L1_attn_b_ln1_b")[:, None],
                                    f("L1_attn_b_lin1_b").reshape(4, P).T], axis=1),
        "qa_rows": np.stack([f("L1_attn_b_" + n) for n in ("out_b", "ln1_g", "ln1_b", "lin2_b", "ln2_g", "ln2_b")]),
        "spread": spread_matrices(),
        "L0a_ln1": np.stack([f("L0_attn_a_ln1_w"), f("L0_attn_a_ln1_b")], axis=1),
    }


def kernel(**inputs):
    import concourse.bacc as _bacc
    from concourse.bass_utils import run_bass_kernel_spmd as _run

    nc = _bacc.Bacc("TRN2", target_bir_lowering=False, num_devices=1)
    arrays = {n: np.ascontiguousarray(a) for n, a in layout(inputs).items()}
    dram = {n: nc.dram_tensor("in_" + n, a.shape, mybir.dt.from_np(a.dtype), kind="ExternalInput").ap()
            for n, a in arrays.items()}
    out = nc.dram_tensor("out_0", (B, T, D), F32, kind="ExternalOutput").ap()
    program(nc, dram, out)
    r = _run(nc, [{"in_" + n: a for n, a in arrays.items()}], core_ids=[0])
    return r.results[0]["out_0"]
```
